# Optimizing a Trainium2 kernel written in Bass

```python
import numpy as np
import jax
import jax.numpy as jnp

def _softmax(x, axis=-1):
    return jax.nn.softmax(x, axis=axis)

def _gelu(x):
    return jax.nn.gelu(x, approximate=True)

def _silu(x):
    return jax.nn.silu(x)

def _sigmoid(x):
    return jax.nn.sigmoid(x)

def _layernorm(x, axis=-1, eps=1e-05):
    m = jnp.mean(x, axis=axis, keepdims=True)
    v = jnp.var(x, axis=axis, keepdims=True)
    return (x - m) / jnp.sqrt(v + eps)

def _scatter_add(tgt, idx, src, axis=0):
    return tgt.at[idx].add(src)

def _segment_sum(src, seg, n):
    return jax.ops.segment_sum(src, seg, n)
kernel_name = 'mk_vit_tower_cls_d2_tok_img768_r4_f15d80'

def setup_inputs(seed: int=0):
    np.random.seed(seed)
    _w = jnp.asarray

    def _rec_inputs():
        import jax
        import jax.numpy as jnp
        _rk = jax.random.key(seed)
        x = -0.000356955 + 1 * jax.random.normal(jax.random.fold_in(_rk, 1), (16, 3, 96, 96), jnp.float32)
        cls_tok = 0.02 * jax.random.normal(jax.random.fold_in(_rk, 5), (1, 1, 192), jnp.float32)
        return (x, cls_tok)
    x, cls_tok = _rec_inputs()

    def _L0_tok_setup():
        import jax, jax.numpy as jnp
        import numpy as np
        PATCH = 16
        EMBED = 192
        IN_DIM = PATCH * PATCH * 3

        def extract_patches(x, p):
            B, C, H, Wd = x.shape
            h, w = (H // p, Wd // p)
            xr = x.reshape(B, C, h, p, w, p)
            xr = xr.transpose(0, 2, 4, 3, 5, 1)
            return xr.reshape(B, h * w, p * p * C)
        key = jax.random.key(seed)
        kx, kw, kb = jax.random.split(key, 3)
        x = jax.random.normal(kx, (128, 3, 224, 224), dtype=jnp.float32)
        bound = 1.0 / np.sqrt(IN_DIM)
        W = jax.random.uniform(kw, (EMBED, IN_DIM), jnp.float32, -bound, bound)
        b = jax.random.uniform(kb, (EMBED,), jnp.float32, -bound, bound)
        return {'x': x, 'W': W, 'b': b}
    _L0_tok_all = _L0_tok_setup()
    _L0_tok_in = {k: v for k, v in _L0_tok_all.items() if k in ('W', 'b')}
    del _L0_tok_all

    def _L0_attn_setup():
        import jax, jax.numpy as jnp
        import numpy as np
        NUM_HEADS = 12
        DIM = 192
        HEAD_DIM = DIM // NUM_HEADS
        B, N = (32, 64)
        key = jax.random.key(seed)
        ks = jax.random.split(key, 8)
        s = 0.02
        return {'x': jax.random.normal(ks[0], (B, N, DIM), dtype=jnp.float32), 'qkv_w': jax.random.normal(ks[1], (3 * DIM, DIM), dtype=jnp.float32) * s, 'qkv_b': jnp.zeros((3 * DIM,), dtype=jnp.float32), 'grassman_scale': jnp.asarray(HEAD_DIM ** (-0.5), dtype=jnp.float32), 'conv_w': jax.random.normal(ks[2], (NUM_HEADS, 2 * NUM_HEADS), dtype=jnp.float32) * s, 'conv_b': jnp.zeros((NUM_HEADS,), dtype=jnp.float32), 'proj_w': jax.random.normal(ks[3], (DIM, DIM), dtype=jnp.float32) * s, 'proj_b': jnp.zeros((DIM,), dtype=jnp.float32)}
    _L0_attn_all = _L0_attn_setup()
    _L0_attn_in = {k: v for k, v in _L0_attn_all.items() if k in ('qkv_w', 'qkv_b', 'grassman_scale', 'conv_w', 'conv_b', 'proj_w', 'proj_b')}
    del _L0_attn_all

    def _L0_ffn_setup():
        import jax, jax.numpy as jnp
        import numpy as np
        N_HEAD = 8 * 0 + 12
        TOP_K = 2
        GELU_C = 0.7978845608028654

        def _gelu(x):
            return 0.5 * x * (1.0 + jnp.tanh(GELU_C * (x + 0.044715 * x * x * x)))

        def _layernorm_global(x, w, b, eps=1e-12):
            m = jnp.mean(x)
            v = jnp.var(x, ddof=1)
            return (x - m) / jnp.sqrt(v + eps) * w + b

        def _attn(x, W1_w, W1_b, W2_w, W2_b):
            B, N, D = x.shape
            h = N_HEAD
            dh = D // h
            qkv = x @ W1_w + W1_b
            Q, K, V = jnp.split(qkv, 3, axis=-1)
            q = Q.reshape(B, N, h, dh).transpose(0, 2, 3, 1)
            k = K.reshape(B, N, h, dh).transpose(0, 2, 1, 3)
            v = V.reshape(B, N, h, dh).transpose(0, 2, 3, 1)
            w = jax.nn.softmax(q @ k / jnp.sqrt(jnp.asarray(N, x.dtype)), axis=-1)
            out = (w @ v).reshape(B, N, h * dh)
            return out @ W2_w + W2_b

        def _moe(x, r_w, r_b, fc_w, fc_b, proj_w, proj_b):
            B, N, D = x.shape
            scores = x @ r_w + r_b
            gate = jax.nn.softmax(jnp.mean(scores, axis=1), axis=-1)
            vals, idx = jax.lax.top_k(gate, TOP_K)
            hmid = _gelu(jnp.einsum('bnd,edf->benf', x, fc_w) + fc_b[None, :, None, :])
            outs = jnp.einsum('benf,efd->bend', hmid, proj_w) + proj_b[None, :, None, :]
            k_outs = jnp.take_along_axis(outs, idx[:, :, None, None], axis=1)
            return jnp.sum(vals[:, :, None, None] * k_outs, axis=1)
        key = jax.random.key(seed)
        ks = jax.random.split(key, 16)
        B, N, D, E = (2, 512, 192, 8)
        H = 4 * D
        s = 0.02
        return {'x': jax.random.normal(ks[0], (B, N, D), jnp.float32), 'W1_w': jax.random.normal(ks[1], (D, 3 * D), jnp.float32) * s, 'W1_b': jnp.zeros((3 * D,), jnp.float32), 'W2_w': jax.random.normal(ks[2], (D, D), jnp.float32) * s, 'W2_b': jnp.zeros((D,), jnp.float32), 'r_w': jax.random.normal(ks[3], (D, E), jnp.float32) * s, 'r_b': jnp.zeros((E,), jnp.float32), 'fc_w': jax.random.normal(ks[4], (E, D, H), jnp.float32) * s, 'fc_b': jnp.zeros((E, H), jnp.float32), 'proj_w': jax.random.normal(ks[5], (E, H, D), jnp.float32) * s, 'proj_b': jnp.zeros((E, D), jnp.float32), 'ln1_w': jnp.ones((D,), jnp.float32), 'ln1_b': jnp.zeros((D,), jnp.float32), 'ln2_w': jnp.ones((D,), jnp.float32), 'ln2_b': jnp.zeros((D,), jnp.float32)}
    _L0_ffn_all = _L0_ffn_setup()
    _L0_ffn_in = {k: v for k, v in _L0_ffn_all.items() if k in ('W1_w', 'W1_b', 'W2_w', 'W2_b', 'r_w', 'r_b', 'fc_w', 'fc_b', 'proj_w', 'proj_b', 'ln1_w', 'ln1_b', 'ln2_w', 'ln2_b')}
    del _L0_ffn_all

    def _L1_attn_setup():
        import jax, jax.numpy as jnp
        import numpy as np
        DIM = 192
        HEADS = 12
        HEAD_DIM = DIM // HEADS
        EPS = 1e-12

        def _l1_normalize(t):
            denom = jnp.maximum(jnp.sum(jnp.abs(t), axis=-2, keepdims=True), EPS)
            return t / denom
        key = jax.random.key(seed)
        k1, k2, k3 = jax.random.split(key, 3)
        x = jax.random.normal(k1, (8, 1024, DIM), dtype=jnp.float32)
        s = 1.0 / np.sqrt(DIM)
        w_qkv = jax.random.uniform(k2, (3 * DIM, DIM), dtype=jnp.float32, minval=-s, maxval=s)
        w_proj = jax.random.uniform(k3, (DIM, DIM), dtype=jnp.float32, minval=-s, maxval=s)
        b_proj = jnp.zeros((DIM,), dtype=jnp.float32)
        return {'x': x, 'w_qkv': w_qkv, 'w_proj': w_proj, 'b_proj': b_proj}
    _L1_attn_all = _L1_attn_setup()
    _L1_attn_in = {k: v for k, v in _L1_attn_all.items() if k in ('w_qkv', 'w_proj', 'b_proj')}
    del _L1_attn_all

    def _L1_ffn_setup():
        import jax, jax.numpy as jnp
        import numpy as np
        NUM_EXPERTS = 8
        TOP_K = 2
        CAPACITY_FACTOR = 1.25
        MAX_GROUP_SIZE = 1024
        MIN_EXPERT_CAPACITY = 4

        def _moe_forward(x, w_router, wi, wo):
            B, T, D = x.shape
            E = NUM_EXPERTS
            num_tokens = B * T
            G = max(num_tokens // MAX_GROUP_SIZE, E)
            while num_tokens % G != 0 or G % E != 0:
                G += 1
            S = num_tokens // G
            C = max(int(TOP_K * CAPACITY_FACTOR * S / E), MIN_EXPERT_CAPACITY)
            xg = x.reshape(G, S, D)
            logits = jnp.einsum('gsd,de->gse', xg.astype(jnp.float32), w_router.astype(jnp.float32))
            probs = jax.nn.softmax(logits, axis=-1)
            gate, idx = jax.lax.top_k(probs, TOP_K)
            idx_kf = jnp.swapaxes(idx, 1, 2).reshape(G, TOP_K * S)
            mask = jax.nn.one_hot(idx_kf, E, dtype=jnp.int32)
            prio = jnp.cumsum(mask, axis=1) * mask - 1
            prio = jnp.swapaxes(prio.reshape(G, TOP_K, S, E), 1, 2)
            prio_se = prio.max(axis=2)
            gate_se = jnp.einsum('gsk,gske->gse', gate, jax.nn.one_hot(idx, E, dtype=gate.dtype))
            dispatch = jax.nn.one_hot(prio_se, C, dtype=x.dtype)
            combine = dispatch * gate_se[..., None].astype(x.dtype)
            expert_in = jnp.einsum('gsec,gsd->egcd', dispatch, xg)
            h = jax.nn.relu(jnp.einsum('egcd,edf->egcf', expert_in, wi))
            expert_out = jnp.einsum('egcf,efd->egcd', h, wo)
            out = jnp.einsum('gsec,egcd->gsd', combine, expert_out)
            return out.reshape(B, T, D)
        key = jax.random.key(seed)
        k1, k2, k3, k4 = jax.random.split(key, 4)
        B, T, D, F = (8, 256, 192, 768)
        x = jax.random.normal(k1, (B, T, D), jnp.float32)
        w_router = jax.random.normal(k2, (D, NUM_EXPERTS), jnp.float32) * D ** (-0.5)
        wi = jax.random.normal(k3, (NUM_EXPERTS, D, F), jnp.float32) * D ** (-0.5)
        wo = jax.random.normal(k4, (NUM_EXPERTS, F, D), jnp.float32) * F ** (-0.5)
        return {'x': x, 'w_router': w_router, 'wi': wi, 'wo': wo}
    _L1_ffn_all = _L1_ffn_setup()
    _L1_ffn_in = {k: v for k, v in _L1_ffn_all.items() if k in ('w_router', 'wi', 'wo')}
    del _L1_ffn_all
    return {'x': x, 'cls_tok': cls_tok, 'L0_tok_W': _L0_tok_in['W'], 'L0_tok_b': _L0_tok_in['b'], 'L0_attn_qkv_w': _L0_attn_in['qkv_w'], 'L0_attn_qkv_b': _L0_attn_in['qkv_b'], 'L0_attn_grassman_scale': _L0_attn_in['grassman_scale'], 'L0_attn_conv_w': _L0_attn_in['conv_w'], 'L0_attn_conv_b': _L0_attn_in['conv_b'], 'L0_attn_proj_w': _L0_attn_in['proj_w'], 'L0_attn_proj_b': _L0_attn_in['proj_b'], 'L0_ffn_W1_w': _L0_ffn_in['W1_w'], 'L0_ffn_W1_b': _L0_ffn_in['W1_b'], 'L0_ffn_W2_w': _L0_ffn_in['W2_w'], 'L0_ffn_W2_b': _L0_ffn_in['W2_b'], 'L0_ffn_r_w': _L0_ffn_in['r_w'], 'L0_ffn_r_b': _L0_ffn_in['r_b'], 'L0_ffn_fc_w': _L0_ffn_in['fc_w'], 'L0_ffn_fc_b': _L0_ffn_in['fc_b'], 'L0_ffn_proj_w': _L0_ffn_in['proj_w'], 'L0_ffn_proj_b': _L0_ffn_in['proj_b'], 'L0_ffn_ln1_w': _L0_ffn_in['ln1_w'], 'L0_ffn_ln1_b': _L0_ffn_in['ln1_b'], 'L0_ffn_ln2_w': _L0_ffn_in['ln2_w'], 'L0_ffn_ln2_b': _L0_ffn_in['ln2_b'], 'L1_attn_w_qkv': _L1_attn_in['w_qkv'], 'L1_attn_w_proj': _L1_attn_in['w_proj'], 'L1_attn_b_proj': _L1_attn_in['b_proj'], 'L1_ffn_w_router': _L1_ffn_in['w_router'], 'L1_ffn_wi': _L1_ffn_in['wi'], 'L1_ffn_wo': _L1_ffn_in['wo']}

def reference(x, cls_tok, L0_tok_W, L0_tok_b, L0_attn_qkv_w, L0_attn_qkv_b, L0_attn_grassman_scale, L0_attn_conv_w, L0_attn_conv_b, L0_attn_proj_w, L0_attn_proj_b, L0_ffn_W1_w, L0_ffn_W1_b, L0_ffn_W2_w, L0_ffn_W2_b, L0_ffn_r_w, L0_ffn_r_b, L0_ffn_fc_w, L0_ffn_fc_b, L0_ffn_proj_w, L0_ffn_proj_b, L0_ffn_ln1_w, L0_ffn_ln1_b, L0_ffn_ln2_w, L0_ffn_ln2_b, L1_attn_w_qkv, L1_attn_w_proj, L1_attn_b_proj, L1_ffn_w_router, L1_ffn_wi, L1_ffn_wo):
    import jax
    import jax.numpy as jnp

    def _L0_tok_ref(x, W, b):
        import jax, jax.numpy as jnp
        import numpy as np
        PATCH = 16
        EMBED = 192
        IN_DIM = PATCH * PATCH * 3

        def extract_patches(x, p):
            B, C, H, Wd = x.shape
            h, w = (H // p, Wd // p)
            xr = x.reshape(B, C, h, p, w, p)
            xr = xr.transpose(0, 2, 4, 3, 5, 1)
            return xr.reshape(B, h * w, p * p * C)
        patches = extract_patches(x, PATCH)
        return jnp.einsum('bnd,ed->bne', patches, W) + b

    def _L0_attn_ref(x, qkv_w, qkv_b, grassman_scale, conv_w, conv_b, proj_w, proj_b):
        import jax, jax.numpy as jnp
        import numpy as np
        NUM_HEADS = 12
        DIM = 192
        HEAD_DIM = DIM // NUM_HEADS
        B, N = (32, 64)
        Bs, Ns, C = x.shape
        H, d = (NUM_HEADS, C // NUM_HEADS)
        qkv = (x @ qkv_w.T + qkv_b).reshape(Bs, Ns, 3, H, d).transpose(2, 0, 3, 1, 4)
        q, k, v = (qkv[0], qkv[1], qkv[2])
        qgr = jnp.linalg.qr(q, mode='reduced')[0]
        kgr = jnp.linalg.qr(k, mode='reduced')[0]
        dots = jnp.einsum('bhnd,bhmd->bhnm', qgr, kgr)
        attn_g = dots * dots * grassman_scale
        cat = jnp.concatenate([attn_g, attn_g], axis=1)
        mixed = jnp.einsum('oc,bcnm->bonm', conv_w, cat) + conv_b[None, :, None, None]
        attn = jax.nn.softmax(mixed, axis=-1)
        out = jnp.einsum('bhnm,bhmd->bhnd', attn, v)
        out = out.transpose(0, 2, 1, 3).reshape(Bs, Ns, C)
        return out @ proj_w.T + proj_b

    def _L0_ffn_ref(x, W1_w, W1_b, W2_w, W2_b, r_w, r_b, fc_w, fc_b, proj_w, proj_b, ln1_w, ln1_b, ln2_w, ln2_b):
        import jax, jax.numpy as jnp
        import numpy as np
        N_HEAD = 8 * 0 + 12
        TOP_K = 2
        GELU_C = 0.7978845608028654

        def _gelu(x):
            return 0.5 * x * (1.0 + jnp.tanh(GELU_C * (x + 0.044715 * x * x * x)))

        def _layernorm_global(x, w, b, eps=1e-12):
            m = jnp.mean(x)
            v = jnp.var(x, ddof=1)
            return (x - m) / jnp.sqrt(v + eps) * w + b

        def _attn(x, W1_w, W1_b, W2_w, W2_b):
            B, N, D = x.shape
            h = N_HEAD
            dh = D // h
            qkv = x @ W1_w + W1_b
            Q, K, V = jnp.split(qkv, 3, axis=-1)
            q = Q.reshape(B, N, h, dh).transpose(0, 2, 3, 1)
            k = K.reshape(B, N, h, dh).transpose(0, 2, 1, 3)
            v = V.reshape(B, N, h, dh).transpose(0, 2, 3, 1)
            w = jax.nn.softmax(q @ k / jnp.sqrt(jnp.asarray(N, x.dtype)), axis=-1)
            out = (w @ v).reshape(B, N, h * dh)
            return out @ W2_w + W2_b

        def _moe(x, r_w, r_b, fc_w, fc_b, proj_w, proj_b):
            B, N, D = x.shape
            scores = x @ r_w + r_b
            gate = jax.nn.softmax(jnp.mean(scores, axis=1), axis=-1)
            vals, idx = jax.lax.top_k(gate, TOP_K)
            hmid = _gelu(jnp.einsum('bnd,edf->benf', x, fc_w) + fc_b[None, :, None, :])
            outs = jnp.einsum('benf,efd->bend', hmid, proj_w) + proj_b[None, :, None, :]
            k_outs = jnp.take_along_axis(outs, idx[:, :, None, None], axis=1)
            return jnp.sum(vals[:, :, None, None] * k_outs, axis=1)
        a = _attn(x, W1_w, W1_b, W2_w, W2_b)
        x = _layernorm_global(a + x, ln1_w, ln1_b)
        m = _moe(x, r_w, r_b, fc_w, fc_b, proj_w, proj_b)
        x = _layernorm_global(m + x, ln2_w, ln2_b)
        return x

    def _L1_attn_ref(x, w_qkv, w_proj, b_proj):
        import jax, jax.numpy as jnp
        import numpy as np
        DIM = 192
        HEADS = 12
        HEAD_DIM = DIM // HEADS
        EPS = 1e-12

        def _l1_normalize(t):
            denom = jnp.maximum(jnp.sum(jnp.abs(t), axis=-2, keepdims=True), EPS)
            return t / denom
        B, N, C = x.shape
        hd = C // HEADS
        qkv = x @ w_qkv.T
        qkv = qkv.reshape(B, N, 3, HEADS, hd).transpose(2, 0, 3, 1, 4)
        q, k, v = (qkv[0], qkv[1], qkv[2])
        q = _l1_normalize(q)
        k = _l1_normalize(k)
        if N < hd:
            out = jnp.einsum('bhnd,bhmd,bhme->bhne', q, k, v)
        else:
            kv = jnp.einsum('bhnd,bhne->bhde', k, v)
            out = jnp.einsum('bhnd,bhde->bhne', q, kv)
        out = out.transpose(0, 2, 1, 3).reshape(B, N, C)
        return out @ w_proj.T + b_proj

    def _L1_ffn_ref(x, w_router, wi, wo):
        import jax, jax.numpy as jnp
        import numpy as np
        NUM_EXPERTS = 8
        TOP_K = 2
        CAPACITY_FACTOR = 1.25
        MAX_GROUP_SIZE = 1024
        MIN_EXPERT_CAPACITY = 4

        def _moe_forward(x, w_router, wi, wo):
            B, T, D = x.shape
            E = NUM_EXPERTS
            num_tokens = B * T
            G = max(num_tokens // MAX_GROUP_SIZE, E)
            while num_tokens % G != 0 or G % E != 0:
                G += 1
            S = num_tokens // G
            C = max(int(TOP_K * CAPACITY_FACTOR * S / E), MIN_EXPERT_CAPACITY)
            xg = x.reshape(G, S, D)
            logits = jnp.einsum('gsd,de->gse', xg.astype(jnp.float32), w_router.astype(jnp.float32))
            probs = jax.nn.softmax(logits, axis=-1)
            gate, idx = jax.lax.top_k(probs, TOP_K)
            idx_kf = jnp.swapaxes(idx, 1, 2).reshape(G, TOP_K * S)
            mask = jax.nn.one_hot(idx_kf, E, dtype=jnp.int32)
            prio = jnp.cumsum(mask, axis=1) * mask - 1
            prio = jnp.swapaxes(prio.reshape(G, TOP_K, S, E), 1, 2)
            prio_se = prio.max(axis=2)
            gate_se = jnp.einsum('gsk,gske->gse', gate, jax.nn.one_hot(idx, E, dtype=gate.dtype))
            dispatch = jax.nn.one_hot(prio_se, C, dtype=x.dtype)
            combine = dispatch * gate_se[..., None].astype(x.dtype)
            expert_in = jnp.einsum('gsec,gsd->egcd', dispatch, xg)
            h = jax.nn.relu(jnp.einsum('egcd,edf->egcf', expert_in, wi))
            expert_out = jnp.einsum('egcf,efd->egcd', h, wo)
            out = jnp.einsum('gsec,egcd->gsd', combine, expert_out)
            return out.reshape(B, T, D)
        return _moe_forward(x, w_router, wi, wo)
    h = _L0_tok_ref(x, L0_tok_W, L0_tok_b)
    h = jnp.concatenate([jnp.broadcast_to(cls_tok, (h.shape[0], 1, h.shape[2])), h], axis=1)
    h = h + _L0_attn_ref(_layernorm(h, axis=-1), L0_attn_qkv_w, L0_attn_qkv_b, L0_attn_grassman_scale, L0_attn_conv_w, L0_attn_conv_b, L0_attn_proj_w, L0_attn_proj_b)
    h = h + _L0_ffn_ref(_layernorm(h, axis=-1), L0_ffn_W1_w, L0_ffn_W1_b, L0_ffn_W2_w, L0_ffn_W2_b, L0_ffn_r_w, L0_ffn_r_b, L0_ffn_fc_w, L0_ffn_fc_b, L0_ffn_proj_w, L0_ffn_proj_b, L0_ffn_ln1_w, L0_ffn_ln1_b, L0_ffn_ln2_w, L0_ffn_ln2_b)
    h = h + _L1_attn_ref(_layernorm(h, axis=-1), L1_attn_w_qkv, L1_attn_w_proj, L1_attn_b_proj)
    h = h + _L1_ffn_ref(_layernorm(h, axis=-1), L1_ffn_w_router, L1_ffn_wi, L1_ffn_wo)
    return h

_drawn_inputs = setup_inputs


def setup_inputs(seed=0):
    import zlib

    import numpy as np

    out = dict(_drawn_inputs(seed))
    spreads = {'L0_attn_qkv_b': (0.0, 0.1),
     'L0_attn_conv_b': (0.0, 0.8),
     'L0_attn_proj_b': (0.0, 0.1),
     'L0_ffn_W1_b': (0.0, 0.758),
     'L0_ffn_W2_b': (0.0, 0.1),
     'L0_ffn_r_b': (0.0, 0.334),
     'L0_ffn_fc_b': (0.0, 0.77),
     'L0_ffn_proj_b': (0.0, 0.336),
     'L0_ffn_ln1_w': (1.0, 0.2),
     'L0_ffn_ln1_b': (0.0, 0.1),
     'L0_ffn_ln2_w': (1.0, 0.2),
     'L0_ffn_ln2_b': (0.0, 0.1),
     'L1_attn_b_proj': (0.0, 0.1)}
    factors = {'L0_attn_conv_w': 8.0,
     'L0_ffn_W1_w': 2.769,
     'L0_ffn_W2_w': 2.854,
     'L0_ffn_r_w': 2.902,
     'L0_ffn_fc_w': 3.257,
     'L1_attn_w_qkv': 5.561,
     'L1_attn_w_proj': 4.077}
    for name, (base, spread) in spreads.items():
        noise = np.random.default_rng([zlib.crc32(name.encode()), seed]).standard_normal(out[name].shape)
        drawn = base * np.exp(spread * noise) if base else spread * noise
        out[name] = jnp.asarray(drawn.astype(out[name].dtype))
    for name, factor in factors.items():
        out[name] = (out[name] * factor).astype(out[name].dtype)
    return out
```

```python
from contextlib import ExitStack

import numpy as np

import concourse.bass as bass
from concourse import mybir

F32 = mybir.dt.float32
U32 = mybir.dt.uint32
ALU = mybir.AluOpType
ACT = mybir.ActivationFunctionType
AX = mybir.AxisListType.X

IMAGES, TOKENS, DIM, HEADS, HD = 16, 37, 192, 12, 16
PATCHES = 36
T = IMAGES // 2
HALF = 64
KC = 2
C = DIM // KC
HC = HEADS // KC
PAIRS = HC // 2
COLS = T * TOKENS
ALLC = 2 * COLS
PK = 6
FF = 768
FC = FF // 128
EXPERTS = 8
NCH = 10
CH = 4
NP = NCH * CH
CAP = 23
SLOTS = T * CAP
MATS = 2 * 2 * KC * T

R_QKVB = 0
R_PROJB = R_QKVB + 3 * DIM
R_W1B = R_PROJB + DIM
R_W2B = R_W1B + 2 * DIM
R_RB = R_W2B + DIM
R_BP = R_RB + EXPERTS
R_ALL = R_BP + DIM
Q_QKB = 0
Q_VB = Q_QKB + 4
Q_LN1W = Q_VB + 2
Q_LN1B = Q_LN1W + 2
Q_LN2W = Q_LN1B + 2
Q_LN2B = Q_LN2W + 2
Q_PB = Q_LN2B + 2
Q_FCB = Q_PB + 2 * EXPERTS
Q_GS = Q_FCB + FC * EXPERTS
Q_CB = Q_GS + 1
Q_CW = Q_CB + 1
Q_ALL = Q_CW + 2 * HEADS
K_ID = 0
K_TRI = K_ID + 128
K_VALID = K_TRI + 128
K_ONE = K_VALID + 128
K_II = K_ONE + 128
K_PAIR = K_II + 64
K_NEG = K_PAIR + 32
K_HEAD = K_NEG + 32
K_E1 = K_HEAD + HC
K_DN = K_E1 + 128
K_I8 = K_DN + NCH
K_I23 = K_I8 + EXPERTS
K_IND = K_I23 + CAP
K_EYE = K_IND + 128
K_ALL = K_EYE + 256


def vit_tower(nc, patches, tok_w, cls_b, rows, cols, consts, qkv_w, proj_w, w1, w2, r_w, fc_w, pr_w,
              qkv2_w, proj2_w, router_w, wi, wo, scratch, out):
    ctx = ExitStack()
    with ctx:
        def sb(name, shape, dt=F32):
            return ctx.enter_context(nc.sbuf_tensor(name, shape, dt))

        def sem(name):
            return ctx.enter_context(nc.semaphore(name))

        def bc(ap, axis, n):
            v = ap.unsqueeze(axis)
            shape = list(v.shape)
            shape[axis] = n
            return v.broadcast_to(shape)

        PS = ctx.enter_context(nc.psum_tensor("PS", [128, 8, 512], F32))

        P = sb("P", [128, 2 * FC * ALLC])
        Q = sb("Q", [128, 8192])
        M = sb("M", [128, T * CH * 128])
        h = sb("h", [128, T, DIM])
        xn = sb("xn", [128, T, DIM])
        XT = sb("XT", [128, KC, T * 128])
        x1T = sb("x1T", [128, KC, ALLC])
        acc = sb("acc", [128, KC, ALLC])
        ytmp = sb("ytmp", [128, 2, COLS])
        row = sb("row", [128, R_ALL])
        col = sb("col", [128, Q_ALL])
        con = sb("con", [128, K_ALL])
        cb2 = sb("cb2", [2, DIM])
        qkT = sb("qkT", [128, MATS, NP])
        qt = sb("qt", [128, MATS, NP])
        vpad = sb("vpad", [128, T, HEADS * 32])
        tokw = sb("tokw", [128, PK, DIM])
        qkvw = sb("qkvw", [128, KC, 3 * DIM])
        projw = sb("projw", [128, KC, DIM])
        w1w = sb("w1w", [128, KC, 3 * DIM])
        w2w = sb("w2w", [128, KC, DIM])
        rw = sb("rw", [128, KC, EXPERTS])
        qkv2w = sb("qkv2w", [128, KC, 3 * DIM])
        proj2w = sb("proj2w", [128, KC, DIM])
        routw = sb("routw", [128, KC, EXPERTS])
        wi_sb = sb("wi_sb", [128, 2, KC * FF])
        wo_sb = sb("wo_sb", [128, 2, FC * DIM])
        mixT = sb("mixT", [128, KC, 64])
        small = sb("small", [128, 1024])

        at = [0]

        def sm(*shape):
            n = int(np.prod(shape))
            v = small[:, at[0]:at[0] + n]
            at[0] += n
            if len(shape) == 1:
                return v
            names = "abcd"[:len(shape)]
            return v.rearrange(f"p ({' '.join(names)}) -> p {' '.join(names)}",
                               **{x: s for x, s in zip(names, shape)})

        eps = sm(1)
        eps12 = sm(1)
        stats = sm(T, 6)
        mv = sm(T, 2)
        sd = sm(T)
        rstd = sm(T)
        tsg = sm(3, 16)
        nsg = sm(3, 16)
        inv = sm(3)
        lcol = sm(3, 16)
        sq = sm(48)
        rs = sm(48)
        wpT = sm(HEADS)
        convb = sm(1)
        mx = sm(T, 8)
        sme = sm(T, 8)
        rsm = sm(T, 8)
        wmax = sm(32)
        wsum = sm(32)
        wrec = sm(32)
        gst = sm(2)
        gmv = sm(2)
        gg = sm(8)
        gsc = sm(KC)
        gbi = sm(KC)
        xbar = sm(KC, IMAGES)
        sc16 = sm(EXPERTS)
        ga = sm(EXPERTS)
        g8 = sm(8)
        gi_f = sm(8)
        gone = sm(8)
        gm = sm(EXPERTS)
        sq2 = sm(32)
        sk2 = sm(32)
        lmax = sm(T)
        fcb = sm(2, FC)
        gi = sb("gi", [128, 8], U32)
        Gd = sb("Gd", [16, EXPERTS, IMAGES])
        Gb = sb("Gb", [128, EXPERTS, IMAGES])
        pr = sb("pr", [128, T, EXPERTS])
        v8 = sb("v8", [128, T, 8])
        i8 = sb("i8", [128, T, 8], U32)
        i8f = sb("i8f", [128, T, 8])
        m12 = sb("m12", [128, 2, T, EXPERTS])
        rank = sb("rank", [128, 2, T, EXPERTS])
        gse = sb("gse", [128, T, EXPERTS])

        patT = P[:, 0:PK * T * 128].rearrange("p (k n) -> p k n", k=PK)
        BD = P[:, 0:MATS * C].rearrange("p (m c) -> p m c", m=MATS)
        S2 = P[:, 0:T * 8 * TOKENS].rearrange("p (t n) -> p t n", t=T)
        attnT = P[:, 2368:2368 + T * 512].rearrange("p (t n) -> p t n", t=T)
        BD2 = P[:, 0:32 * C].rearrange("p (m c) -> p m c", m=32)
        oS = P[:, 3072:3072 + 32 * TOKENS].rearrange("p (m n) -> p m n", m=32)
        O = P[:, 4256:4256 + T * DIM].rearrange("p (t d) -> p t d", t=T)
        hT = [P[:, b * FC * ALLC:(b + 1) * FC * ALLC].rearrange("p (f n) -> p f n", f=FC) for b in range(2)]
        A = Q[:, 0:T * 2 * DIM].rearrange("p (t n) -> p t n", t=T)
        Gs = Q[:, 3072:5120].rearrange("p (m n) -> p m n", m=MATS)
        E = Q[:, 5120:6656].rearrange("p (a r c) -> p a r c", a=3, r=16)
        Ef = Q[:, 5120:6656].rearrange("p (a n) -> p a n", a=3)
        Tm = Q[:, 6656:7424].rearrange("p (a r c) -> p a r c", a=3, r=16)
        Pb = Q[:, 7424:8192]
        Qblk = Q[:, :].rearrange("p (a m c x) -> p a m c x", a=2, m=16, c=CH)
        vT = Q[:, 3072:4256].rearrange("p (m n) -> p m n", m=32)
        Wm = Q[:, 4256:5280].rearrange("p (m n) -> p m n", m=32)
        qT2 = vT
        Aabs = Q[:, 4256:4256 + T * DIM].rearrange("p (t n) -> p t n", t=T)
        kvs = Q[:, 5792:6816].rearrange("p (m n) -> p m n", m=32)
        GE = EXPERTS * CAP
        disp = Q[:, 0:T * GE].rearrange("p (g e c) -> p g e c", g=T, e=EXPERTS)
        comb = Q[:, T * GE:2 * T * GE].rearrange("p (g e c) -> p g e c", g=T, e=EXPERTS)
        xinT = Q[:, 2 * T * GE:4 * T * GE].rearrange("p (k e s) -> p k e s", k=KC, e=EXPERTS)
        combT = Q[:, 4 * T * GE:4 * T * GE + 2048].rearrange("p (g a n) -> p g a n", g=T, a=2)
        BLK = M[:, 0:16 * C].rearrange("p (j c) -> p j c", j=16)
        Mx = M[:, :].rearrange("p (t c a n) -> p t c a n", t=T, c=CH, a=2)
        yT = M[:, 0:2 * T * GE].rearrange("p (k g e c) -> p k g e c", k=KC, g=T, e=EXPERTS)
        hT1 = [P[:, b * FC * SLOTS:(b + 1) * FC * SLOTS].rearrange("p (f n) -> p f n", f=FC) for b in range(2)]
        yG = P[:, 2300:2300 + T * 2 * DIM].rearrange("p (g a n) -> p g a n", g=T, a=2)
        fcball = col[:, Q_FCB:Q_FCB + FC * EXPERTS].rearrange("p (e f) -> p e f", f=FC)
        ident = con[:, K_ID:K_ID + 128]
        id96 = con[0:C, K_ID:K_ID + C]
        idpar = con[0:C, K_ID:K_ID + C].rearrange("p (a x) -> p a x", a=PAIRS)
        head = [con[0:C, K_HEAD + i:K_HEAD + i + 1] for i in range(HC)]
        eye = con[:, K_EYE:K_EYE + 256].rearrange("p (r c) -> p r c", r=16)
        XTi = XT[0:C, :, :].rearrange("p k (t a n) -> p k t a n", a=2, n=HALF)

        def cq(i, p=C, n=1):
            return col[0:p, i:i + n]

        def qb_out(a, hd):
            return Qblk[0:C, a, :, :, :].rearrange("p m c x -> p (m c) x")[:, :, hd * NCH:(hd + 1) * NCH]

        def qb_in(a):
            return qt[0:C, a * 32:a * 32 + 16, :].rearrange("p m (c n) -> p (m c) n", c=CH)

        s_const, s_pat, s_tokw, s_bias, s_attw, s_ffnw, s_l1w = [
            sem(n) for n in ("s_const", "s_pat", "s_tokw", "s_bias", "s_attw", "s_ffnw", "s_l1w")]
        s_w = [sem("s_w0"), sem("s_w1")]
        s_patk = [sem(f"s_patk{k}") for k in range(PK)]
        dchain, achain, pchain = sem("dchain"), sem("achain"), sem("pchain")
        s_zero = sem("s_zero")
        s_emb = sem("s_emb")
        s_hcopy = sem("s_hcopy")
        s_var, s_sd, s_xn = sem("s_var"), sem("s_sd"), sem("s_xn")
        s_xtp, s_xt = sem("s_xtp"), sem("s_xt")
        s_hb = sem("s_hb")
        s_tok, s_tokv = sem("s_tok"), sem("s_tokv")
        s_chan, s_chanv = sem("s_chan"), sem("s_chanv")
        s_gram, s_gramv = sem("s_gram"), sem("s_gramv")
        s_et, s_etv = sem("s_et"), sem("s_etv")
        s_piv, s_sq, s_blk = sem("s_piv"), sem("s_sq"), sem("s_blk")
        s_back, s_bda, s_bdv = sem("s_back"), sem("s_bda"), sem("s_bdv")
        s_qt, s_qte = sem("s_qt"), sem("s_qte")
        s_qba, s_qbv, s_qbp = sem("s_qba"), sem("s_qbv"), sem("s_qbp")
        s_mixw, s_mixr, s_mix1 = sem("s_mixw"), sem("s_mixr"), sem("s_mix1")
        s_dots, s_s2, s_mixp, s_mixe = sem("s_dots"), sem("s_s2"), sem("s_mixp"), sem("s_mixe")
        s_sub, s_exp, s_att = sem("s_sub"), sem("s_exp"), sem("s_att")
        s_atp, s_atT = sem("s_atp"), sem("s_atT")
        s_av, s_oT, s_oTv = sem("s_av"), sem("s_oT"), sem("s_oTv")
        s_prj, s_h = sem("s_prj"), sem("s_h")
        s_w_ps, s_wsub, s_wexp, s_wT = sem("s_w_ps"), sem("s_wsub"), sem("s_wexp"), sem("s_wT")
        s_wv, s_os, s_scr, s_scr2 = sem("s_wv"), sem("s_os"), sem("s_scr"), sem("s_scr2")
        s_otp, s_ot = sem("s_otp"), sem("s_ot")
        s_zb = sem("s_zb")
        s_w2p, s_s = sem("s_w2p"), sem("s_s")
        s_gst, s_gps, s_gva, s_gsd, s_gsc = sem("s_gst"), sem("s_gps"), sem("s_gva"), sem("s_gsd"), sem("s_gsc")
        s_x1p, s_x1 = sem("s_x1p"), sem("s_x1")
        s_xbar, s_rps, s_nm, s_ge, s_gd, s_gbp, s_gb = [
            sem(n) for n in ("s_xbar", "s_rps", "s_nm", "s_ge", "s_gd", "s_gbp", "s_gb")]
        s_fcb, s_hp, s_gelu, s_ytmp, s_acc, s_edone = [
            sem(n) for n in ("s_fcb", "s_hp", "s_gelu", "s_ytmp", "s_acc", "s_edone")]
        s_x2, s_x2p = sem("s_x2"), sem("s_x2p")
        s_q2, s_q2e, s_kv2, s_kv2e = sem("s_q2"), sem("s_q2e"), sem("s_kv2"), sem("s_kv2e")
        s_kvp, s_bd3, s_o2, s_o2e = sem("s_kvp"), sem("s_bd3"), sem("s_o2"), sem("s_o2e")
        s_lg, s_lsub, s_lexp, s_m12, s_rk = [sem(n) for n in ("s_lg", "s_lsub", "s_lexp", "s_m12", "s_rk")]
        s_disp, s_comb, s_xip, s_xin, s_ctp, s_ct = [
            sem(n) for n in ("s_disp", "s_comb", "s_xip", "s_xin", "s_ctp", "s_ct")]
        s_h1p, s_relu, s_y1p, s_y1 = sem("s_h1p"), sem("s_relu"), sem("s_y1p"), sem("s_y1")
        s_ygp, s_yg, s_fin, s_res, s_out = [sem(n) for n in ("s_ygp", "s_yg", "s_fin", "s_res", "s_out")]

        block = ctx.enter_context(nc.Block())

        @block.sync
        def _(sp):
            sp.dma_start(tokw[:, :, :], tok_w[:, :, :]).then_inc(s_tokw, 16)
            for k in range(PK):
                sp.dma_start(patT[:, k, :], patches[:, k, :]).then_inc(s_patk[k], 16)
            sp.dma_start(con[:, :], consts[:, :]).then_inc(s_const, 16)
            sp.dma_start(cb2[:, :], cls_b[:, :]).then_inc(s_const, 16)
            sp.dma_start(col[:, :], cols[:, :]).then_inc(s_bias, 16)
            sp.dma_start(row[:, :], rows.partition_broadcast(128)).then_inc(s_bias, 16)
            sp.dma_start(qkvw[0:C, :, :], qkv_w[:, :, :]).then_inc(s_attw, 16)
            sp.dma_start(projw[0:C, :, :], proj_w[:, :, :]).then_inc(s_attw, 16)
            sp.dma_start(w1w[0:C, :, :], w1[:, :, :]).then_inc(s_ffnw, 16)
            sp.dma_start(w2w[0:C, :, :], w2[:, :, :]).then_inc(s_ffnw, 16)
            sp.dma_start(rw[0:C, :, :], r_w[:, :, :]).then_inc(s_ffnw, 16)
            for b in range(2):
                sp.dma_start(wi_sb[0:C, b, :], fc_w[b, :, :]).then_inc(s_w[b], 16)
                sp.dma_start(wo_sb[:, b, :], pr_w[b, :, :]).then_inc(s_w[b], 16)
            sp.dma_start(qkv2w[0:C, :, :], qkv2_w[:, :, :]).then_inc(s_l1w, 16)
            sp.dma_start(proj2w[0:C, :, :], proj2_w[:, :, :]).then_inc(s_l1w, 16)
            sp.dma_start(routw[0:C, :, :], router_w[:, :, :]).then_inc(s_l1w, 16)

            for i in range(4):
                a, kc = divmod(i, 2)
                sp.wait_ge(s_os, i + 1)
                sp.dma_start(scratch[:, a, kc].rearrange("t p n -> p t n"),
                             oS[0:C, i * 8:(i + 1) * 8, :]).then_inc(s_scr, 16)
            sp.wait_ge(s_scr, 64)
            sp.wait_ge(s_zero, 5)
            back = scratch.rearrange("t a k p n -> t a (k p n)").rearrange("t a (m d) -> a m t d", d=DIM)
            for a in range(2):
                sp.dma_start(O[a * HALF:a * HALF + 36, :, :], back[a, 0:36]).then_inc(s_scr2, 16)
                sp.dma_start(O[a * HALF + 36:a * HALF + 37, :, :], back[a, 36:37]).then_inc(s_scr2, 16)

            with sp.Fori(1, EXPERTS // 2) as it:
                for b in range(2):
                    sp.wait_ge(s_edone, it * 2 + (b - 1))
                    sp.dma_start(wi_sb[0:C, b, :], fc_w[it * 2 + b, :, :]).then_inc(s_w[b], 16)
                    sp.dma_start(wo_sb[:, b, :], pr_w[it * 2 + b, :, :]).then_inc(s_w[b], 16)
            with sp.Fori(0, EXPERTS // 2) as it:
                for b in range(2):
                    sp.wait_ge(s_edone, it * 2 + (EXPERTS + b - 1))
                    sp.dma_start(wi_sb[0:C, b, :], wi[it * 2 + b, :, :]).then_inc(s_w[b], 16)
                    sp.dma_start(wo_sb[:, b, :], wo[it * 2 + b, :, :]).then_inc(s_w[b], 16)

            for t in range(T):
                sp.wait_ge(s_res, t + 1)
                for a in range(2):
                    sp.dma_start(out[2 * t + a, :, :], h[a * HALF:a * HALF + TOKENS, t, :]).then_inc(s_out, 16)
            sp.wait_ge(s_out, 16 * IMAGES)

        @block.gpsimd
        def _(po):
            n = [0]

            def link(ins):
                n[0] += 1
                ins.then_inc(pchain, 1)
                po.wait_ge(pchain, n[0])

            po.memset(vpad[:, :, :], 0.0).then_inc(s_zero, 1)
            po.memset(qkT[:, :, :], 0.0).then_inc(s_zero, 1)
            po.memset(eps, 1e-5)
            po.memset(eps12, 1e-12)
            po.memset(mixT[:, :, :], 0.0).then_inc(s_zero, 1)
            po.memset(BLK, 0.0).then_inc(s_zero, 1)
            po.wait_ge(s_const, 32)
            for a in range(3):
                last = po.tensor_copy(E[:, a, :, 16:32], eye)
            last.then_inc(s_etv, 1)
            po.wait_ge(s_bias, 32)
            po.wait_ge(s_xn, T)
            po.tensor_tensor(h[:, :, :], h[:, :, :], bc(row[:, R_PROJB:R_PROJB + DIM], 1, T), ALU.add).then_inc(s_hb, 1)
            po.wait_ge(s_qte, 8)
            for hd in (4, 5):
                for a in range(2):
                    last = po.tensor_scalar(qb_out(a, hd), qb_in(a), head[hd], None, ALU.mult)
            last.then_inc(s_qbp, 1)
            po.memset(Qblk[0:C, :, :, :, 60:64].rearrange("p a m c x -> p (a m c) x"), 0.0).then_inc(s_qbp, 1)
            po.memset(M[:, :].rearrange("p (x n) -> p x n", n=64)[:, :, 37:64], 0.0).then_inc(s_qbp, 1)
            po.wait_ge(s_av, 1)
            po.memset(BD2[0:C], 0.0)
            po.memset(O, 0.0).then_inc(s_zero, 1)
            po.wait_ge(s_xt, 8)
            po.tensor_tensor(xn[:, :, :], xn[:, :, :], bc(row[:, R_W2B:R_W2B + DIM], 1, T), ALU.add).then_inc(s_zb, 1)
            po.wait_ge(s_edone, EXPERTS)
            po.memset(BD2[0:C], 0.0).then_inc(s_zero, 1)
            po.wait_ge(s_xn, 3 * T)
            po.tensor_tensor(h[:, :, :], h[:, :, :], bc(row[:, R_BP:R_BP + DIM], 1, T), ALU.add).then_inc(s_hb, 1)

        @block.tensor
        def _(pe):
            def transposes(r):
                for t in range(T):
                    pe.wait_ge(s_xn, r * T + t + 1)
                    for kc in range(KC):
                        last = pe.transpose(PS[0:C, t // 2, kc * 256 + (t % 2) * 128:kc * 256 + (t % 2) * 128 + 128],
                                            xn[:, t, kc * C:(kc + 1) * C], ident)
                    if t % 2:
                        last.then_inc(s_xtp, 1)

            pe.wait_ge(s_tokw, 16)
            for k in range(PK):
                pe.wait_ge(s_patk[k], 16)
                for t in range(T):
                    pe.matmul(PS[:, t, 0:DIM], patT[:, k, t * 128:(t + 1) * 128], tokw[:, k, :],
                              start=(k == 0), stop=False)
            pe.wait_ge(s_const, 32)
            for t in range(T):
                pe.matmul(PS[:, t, 0:DIM], con[0:2, K_IND:K_IND + 128], cb2[:, :], start=False,
                          stop=True).then_inc(s_emb, 1)
            pe.wait_ge(s_hcopy, T)
            pe.wait_ge(s_var, 1)
            transposes(0)
            pe.wait_ge(s_mixw, 1)
            pe.matmul(PS[:, 7, 0:HEADS], con[0:HEADS, K_E1:K_E1 + 128], wpT[0:HEADS, :], start=True, stop=True)
            pe.matmul(PS[:, 7, HEADS:HEADS + 1], con[0:HEADS, K_E1:K_E1 + 128], col[0:HEADS, Q_CB:Q_CB + 1],
                      start=True, stop=True).then_inc(s_mixr, 1)
            pe.wait_ge(s_attw, 32)
            pe.wait_ge(s_xt, 4)
            pe.wait_ge(s_mix1, 1)

            for t in range(T):
                if t >= 4:
                    pe.wait_ge(s_tokv, t - 3)
                b = 2 * (t % 4)
                for kc in range(KC):
                    pe.matmul(PS[:, b, 0:2 * DIM], XT[0:C, kc, t * 128:(t + 1) * 128], qkvw[0:C, kc, 0:2 * DIM],
                              start=(kc == 0), stop=(kc == 1))
                for kc in range(KC):
                    last = pe.matmul(PS[:, b + 1, 0:DIM], XT[0:C, kc, t * 128:(t + 1) * 128],
                                     qkvw[0:C, kc, 2 * DIM:3 * DIM], start=(kc == 0), stop=(kc == 1))
                last.then_inc(s_tok, 1)
            for i in range(8):
                a, qk, kc = i // 4, (i // 2) % 2, i % 2
                pe.wait_ge(s_tokv, 5 + i // 2)
                for k in range(KC):
                    last = pe.matmul(PS[0:C, i, 0:COLS], qkvw[0:C, k, (qk * 2 + kc) * C:(qk * 2 + kc + 1) * C],
                                     XTi[:, k, :, a, 0:TOKENS], start=(k == 0), stop=(k == 1))
                last.then_inc(s_chan, 1)
            for a in range(2):
                for qk in range(2):
                    s = a * 2 + qk
                    pe.wait_ge(s_chanv, s + 1)
                    for kc in range(KC):
                        for t in range(T):
                            for j in range(PAIRS):
                                v = A[a * HALF:a * HALF + TOKENS, t, (qk * 2 + kc) * C + 32 * j:(qk * 2 + kc) * C + 32 * j + 32]
                                last = pe.matmul(PS[32 * j:32 * j + 32, s, (kc * 8 + t) * 32:(kc * 8 + t) * 32 + 32],
                                                 v, v, start=True, stop=True)
                    last.then_inc(s_gram, 1)
            pe.wait_ge(s_chanv, 8)
            for par in range(2):
                for r in range(16):
                    last = pe.matmul(PS[par * 64:par * 64 + 64, 4 + r // 8, (r % 8) * 48:(r % 8) * 48 + 48],
                                     qkT[0:C, :, r], idpar[:, :, par * 16:par * 16 + 16], start=True, stop=True)
            last.then_inc(s_et, 1)
            pe.wait_ge(s_gramv, 4)
            for par in range(2):
                for r in range(16):
                    last = pe.matmul(PS[par * 64:par * 64 + 64, 6 + r // 8, (r % 8) * 48:(r % 8) * 48 + 48],
                                     Gs[0:C, :, par * 16 + r], idpar[:, :, par * 16:par * 16 + 16],
                                     start=True, stop=True)
            last.then_inc(s_et, 1)
            pe.wait_ge(s_blk, 1)
            for j in range(16):
                last = pe.matmul(PS[0:C, j // 8, (j % 8) * 64:(j % 8) * 64 + 64], BLK[:, j, :],
                                 con[:, K_II:K_II + 64], start=True, stop=True)
            last.then_inc(s_back, 1)
            pe.wait_ge(s_bda, 1)
            pe.wait_ge(s_bdv, 1)
            for b in range(8):
                for i in range(8):
                    m = b * 8 + i
                    last = pe.matmul(PS[0:C, b, i * NP:(i + 1) * NP], BD[0:C, m, :], qkT[0:C, m, :],
                                     start=True, stop=True)
                last.then_inc(s_qt, 1)
            pe.wait_ge(s_qte, 8)
            pe.wait_ge(s_qba, 1)
            pe.wait_ge(s_qbv, 1)
            pe.wait_ge(s_qbp, 3)
            for t in range(T):
                for kc in range(KC):
                    for c in range(CH):
                        for a in range(2):
                            last = pe.matmul(PS[kc * 64:kc * 64 + 64, t, (c * 2 + a) * TOKENS:(c * 2 + a + 1) * TOKENS],
                                             Qblk[0:C, a, kc * 8 + t, c, :],
                                             qt[0:C, a * 32 + 16 + kc * 8 + t, 0:TOKENS], start=True, stop=True)
                last.then_inc(s_dots, 1)
            for t in range(T):
                pe.wait_ge(s_s2, t + 1)
                pe.matmul(PS[:, t, 0:8 * TOKENS], mixT[:, :, :].rearrange("p k x -> p (k x)"), S2[:, t, :],
                          start=True, stop=True).then_inc(s_mixp, 1)
            for t in range(T):
                pe.wait_ge(s_att, t // 2 + 1)
                if t >= 4:
                    pe.wait_ge(s_atT, t - 3)
                else:
                    pe.wait_ge(s_mixe, t + 5)
                for c in range(CH):
                    last = pe.transpose(PS[:, 4 + t % 4, c * 128:(c + 1) * 128],
                                        Mx[:, t, c].rearrange("p a n -> p (a n)"), ident)
                last.then_inc(s_atp, 1)
            for t in range(T):
                pe.wait_ge(s_atT, t + 1)
                for kc in range(KC):
                    for j in range(PAIRS):
                        for a in range(2):
                            for par in range(2):
                                c0 = (kc * PAIRS + j) * 64 + par * 16
                                r0 = kc * 64 + (2 * j + par) * NCH
                                rhs = attnT[a * HALF:a * HALF + TOKENS, t, :].rearrange("p (c x) -> p c x", c=CH)
                                last = pe.matmul(PS[32 * j:32 * j + 32, a * 2 + kc, t * NP:(t + 1) * NP],
                                                 vpad[a * HALF:a * HALF + TOKENS, t, c0:c0 + 32],
                                                 rhs[:, :, r0:r0 + NCH], start=(par == 0), stop=(par == 1))
            last.then_inc(s_av, 1)
            pe.wait_ge(s_oT, 2)
            pe.wait_ge(s_oTv, 2)
            for t in range(T):
                for kc in range(KC):
                    last = pe.matmul(PS[:, t, 0:DIM], XT[0:C, kc, t * 128:(t + 1) * 128], projw[0:C, kc, :],
                                     start=(kc == 0), stop=(kc == 1))
                last.then_inc(s_prj, 1)

            pe.wait_ge(s_h, T)
            transposes(1)
            pe.wait_ge(s_ffnw, 48)
            pe.wait_ge(s_xt, 8)
            for t in range(T):
                if t >= 4:
                    pe.wait_ge(s_tokv, T + t - 3)
                for kc in range(KC):
                    last = pe.matmul(PS[:, t % 4, 0:2 * DIM], XT[0:C, kc, t * 128:(t + 1) * 128],
                                     w1w[0:C, kc, 0:2 * DIM], start=(kc == 0), stop=(kc == 1))
                last.then_inc(s_tok, 1)
            for i in range(4):
                a, kc = divmod(i, 2)
                for k in range(KC):
                    last = pe.matmul(PS[0:C, 4 + i, 0:COLS], w1w[0:C, k, 2 * DIM + kc * C:2 * DIM + (kc + 1) * C],
                                     XTi[:, k, :, a, 0:TOKENS], start=(k == 0), stop=(k == 1))
                last.then_inc(s_chan, 1)
            pe.wait_ge(s_tokv, 2 * T)
            for a in range(2):
                for kc in range(KC):
                    for t in range(T):
                        for j in range(PAIRS):
                            q0 = kc * C + 32 * j
                            last = pe.matmul(PS[32 * j:32 * j + 32, a, (kc * 8 + t) * 32:(kc * 8 + t) * 32 + 32],
                                             A[a * HALF:a * HALF + TOKENS, t, q0:q0 + 32],
                                             A[a * HALF:a * HALF + TOKENS, t, DIM + q0:DIM + q0 + 32],
                                             start=True, stop=True)
                last.then_inc(s_w_ps, 1)
            pe.wait_ge(s_wT, 1)
            pe.wait_ge(s_chanv, 12)
            for b in range(4):
                for i in range(8):
                    m = b * 8 + i
                    last = pe.matmul(PS[0:C, 2 + b, i * TOKENS:(i + 1) * TOKENS], BD2[0:C, m, :], vT[0:C, m, :],
                                     start=True, stop=True)
                last.then_inc(s_wv, 1)
            pe.wait_ge(s_scr2, 64)
            for t in range(T):
                if t >= 4:
                    pe.wait_ge(s_os, 4)
                for kc in range(KC):
                    last = pe.transpose(PS[0:C, t // 2, kc * 256 + (t % 2) * 128:kc * 256 + (t % 2) * 128 + 128],
                                        O[:, t, kc * C:(kc + 1) * C], ident)
                if t % 2:
                    last.then_inc(s_xtp, 1)
            pe.wait_ge(s_xt, 12)
            for t in range(T):
                for kc in range(KC):
                    last = pe.matmul(PS[:, t, 0:DIM], XT[0:C, kc, t * 128:(t + 1) * 128], w2w[0:C, kc, :],
                                     start=(kc == 0), stop=(kc == 1))
                last.then_inc(s_w2p, 1)
            pe.wait_ge(s_s, T)
            for t in range(T):
                for kc in range(KC):
                    last = pe.transpose(PS[0:C, t // 2, kc * 256 + (t % 2) * 128:kc * 256 + (t % 2) * 128 + 128],
                                        xn[:, t, kc * C:(kc + 1) * C], ident)
            last.then_inc(s_x1p, 1)
            pe.wait_ge(s_gst, 1)
            pe.matmul(PS[:, 4, 0:2], con[:, K_VALID:K_VALID + 128], gst, start=True, stop=True).then_inc(s_gps, 1)
            pe.wait_ge(s_xbar, 1)
            for kc in range(KC):
                last = pe.matmul(PS[0:IMAGES, 5, 0:EXPERTS], xbar[0:C, kc, :], rw[0:C, kc, :],
                                 start=(kc == 0), stop=(kc == 1))
            last.then_inc(s_rps, 1)
            pe.wait_ge(s_gd, 1)
            pe.matmul(PS[0:C, 6, 0:128], con[0:IMAGES, K_ONE:K_ONE + C], Gd[:, :, :].rearrange("p e b -> p (e b)"),
                      start=True, stop=True).then_inc(s_gbp, 1)
            pe.wait_ge(s_gb, 1)

            with pe.Fori(0, EXPERTS // 2) as it:
                for b in range(2):
                    pe.wait_ge(s_w[b], it * 32 + 32)
                    for i in range(2 * FC):
                        f, nh = divmod(i, 2)
                        if i >= 4:
                            pe.wait_ge(s_gelu, it * 24 + (b * 12 + i - 3))
                        for kc in range(KC):
                            last = pe.matmul(PS[:, i % 4, 0:COLS],
                                             wi_sb[0:C, b, kc * FF + f * 128:kc * FF + (f + 1) * 128],
                                             x1T[0:C, kc, nh * COLS:(nh + 1) * COLS], start=(kc == 0), stop=(kc == 1))
                        last.then_inc(s_hp, 1)
                    pe.wait_ge(s_acc, it * 8 + (4 * b + 1))
                    for f in range(FC):
                        pe.wait_ge(s_gelu, it * 24 + (b * 12 + 2 * f + 2))
                        for kc in range(KC):
                            for nh in range(2):
                                last = pe.matmul(PS[0:C, 4 + kc * 2 + nh, 0:COLS],
                                                 wo_sb[:, b, f * DIM + kc * C:f * DIM + (kc + 1) * C],
                                                 hT[b][:, f, nh * COLS:(nh + 1) * COLS],
                                                 start=(f == 0), stop=(f == FC - 1))
                    last.then_inc(s_edone, 1)

            pe.wait_ge(s_gst, 2)
            pe.matmul(PS[:, 0, 0:2], con[0:C, K_ONE:K_ONE + 128], gst[0:C], start=True, stop=True).then_inc(s_gps, 1)
            pe.wait_ge(s_x2, 2)
            for t in range(T):
                for kc in range(KC):
                    last = pe.matmul(PS[:, t, kc * C:(kc + 1) * C], XT[0:C, kc, t * 128:(t + 1) * 128], id96,
                                     start=True, stop=True, is_transpose=True)
                last.then_inc(s_x2p, 1)

            pe.wait_ge(s_h, 2 * T)
            transposes(2)
            pe.wait_ge(s_l1w, 48)
            pe.wait_ge(s_xt, 16)
            for i in range(4):
                a, kc = divmod(i, 2)
                for k in range(KC):
                    last = pe.matmul(PS[0:C, 4 + i, 0:COLS], qkv2w[0:C, k, kc * C:(kc + 1) * C],
                                     XTi[:, k, :, a, 0:TOKENS], start=(k == 0), stop=(k == 1))
                last.then_inc(s_q2, 1)
            for t in range(T):
                if t >= 4:
                    pe.wait_ge(s_kv2e, t - 3)
                    pe.wait_ge(s_kv2, t)
                for kc in range(KC):
                    last = pe.matmul(PS[:, t % 4, 0:2 * DIM], XT[0:C, kc, t * 128:(t + 1) * 128],
                                     qkv2w[0:C, kc, DIM:3 * DIM], start=(kc == 0), stop=(kc == 1))
                last.then_inc(s_kv2, 1)
            pe.wait_ge(s_kv2e, T)
            for a in range(2):
                for kc in range(KC):
                    for t in range(T):
                        for j in range(PAIRS):
                            k0 = kc * C + 32 * j
                            pe.matmul(PS[32 * j:32 * j + 32, a, (kc * 8 + t) * 32:(kc * 8 + t) * 32 + 32],
                                      A[a * HALF:a * HALF + TOKENS, t, k0:k0 + 32],
                                      A[a * HALF:a * HALF + TOKENS, t, DIM + k0:DIM + k0 + 32],
                                      start=True, stop=True)
                for kc in range(KC):
                    for t in range(T):
                        m = a * 16 + kc * 8 + t
                        last = pe.matmul(PS[0:C, 2 + a, m:m + 1],
                                         Aabs[a * HALF:a * HALF + TOKENS, t, kc * C:(kc + 1) * C],
                                         con[a * HALF:a * HALF + TOKENS, K_ONE:K_ONE + 1], start=True, stop=True)
            last.then_inc(s_kvp, 1)
            pe.wait_ge(s_bd3, 3)
            pe.wait_ge(s_q2e, 4)
            for b in range(4):
                for i in range(8):
                    m = b * 8 + i
                    last = pe.matmul(PS[0:C, 4 + b, i * TOKENS:(i + 1) * TOKENS], BD2[0:C, m, :], qT2[0:C, m, :],
                                     start=True, stop=True)
                last.then_inc(s_o2, 1)
            pe.wait_ge(s_o2e, 4)
            for t in range(T):
                for kc in range(KC):
                    last = pe.matmul(PS[:, t, 0:DIM], XT[0:C, kc, t * 128:(t + 1) * 128], proj2w[0:C, kc, :],
                                     start=(kc == 0), stop=(kc == 1))
                last.then_inc(s_prj, 1)

            pe.wait_ge(s_h, 3 * T)
            transposes(3)
            pe.wait_ge(s_xt, 20)
            for t in range(T):
                for kc in range(KC):
                    last = pe.matmul(PS[:, 4, t * 8:t * 8 + 8], XT[0:C, kc, t * 128:(t + 1) * 128], routw[0:C, kc, :],
                                     start=(kc == 0), stop=(kc == 1))
            last.then_inc(s_lg, 1)
            pe.wait_ge(s_m12, 1)
            f1 = m12[:, 0].rearrange("p g e -> p (g e)")
            f2 = m12[:, 1].rearrange("p g e -> p (g e)")
            pe.matmul(PS[:, 5, 0:64], con[:, K_TRI:K_TRI + 128], f1, start=True, stop=True)
            pe.matmul(PS[:, 5, 64:128], con[:, K_ONE:K_ONE + 128], f1, start=True, stop=False)
            pe.matmul(PS[:, 5, 64:128], con[:, K_TRI:K_TRI + 128], f2, start=False, stop=True).then_inc(s_rk, 1)
            pe.wait_ge(s_disp, 1)
            for g in range(T):
                for kc in range(KC):
                    last = pe.matmul(PS[0:C, g, kc * GE:(kc + 1) * GE], xn[:, g, kc * C:(kc + 1) * C],
                                     disp[:, g].rearrange("p e c -> p (e c)"), start=True, stop=True)
                last.then_inc(s_xip, 1)
            pe.wait_ge(s_comb, 1)
            for b in range(4):
                pe.wait_ge(s_xin, b + 1)
                for i in range(4):
                    g, hf = 2 * b + i // 2, i % 2
                    src = comb[:, g].rearrange("p e c -> p (e c)")[:, hf * 92:(hf + 1) * 92]
                    last = pe.transpose(PS[0:92, b, i * 128:(i + 1) * 128], src, ident)
                last.then_inc(s_ctp, 1)
            pe.wait_ge(s_ct, 4)
            pe.wait_ge(s_xin, 8)
            with pe.Fori(0, EXPERTS // 2) as it:
                for b in range(2):
                    pe.wait_ge(s_w[b], it * 32 + 160)
                    for i in range(3):
                        for u in range(2):
                            f = 2 * i + u
                            for kc in range(KC):
                                last = pe.matmul(PS[:, 3 * b + i, u * SLOTS:(u + 1) * SLOTS],
                                                 wi_sb[0:C, b, kc * FF + f * 128:kc * FF + (f + 1) * 128],
                                                 xinT[0:C, kc, it * 2 + b, :], start=(kc == 0), stop=(kc == 1))
                        last.then_inc(s_h1p, 1)
                    pe.wait_ge(s_y1, it * 2 + (b + 1))
                    pe.wait_ge(s_relu, it * 6 + (3 * b + 3))
                    for kc in range(KC):
                        for f in range(FC):
                            last = pe.matmul(PS[0:C, 6 + b, kc * SLOTS:(kc + 1) * SLOTS],
                                             wo_sb[:, b, f * DIM + kc * C:f * DIM + (kc + 1) * C],
                                             hT1[b][:, f, :], start=(f == 0), stop=(f == FC - 1))
                    last.then_inc(s_edone, 1)
            pe.wait_ge(s_y1, EXPERTS + 2)
            for g in range(T):
                for hf in range(2):
                    for kc in range(KC):
                        src = yT[0:C, kc, g].rearrange("p e c -> p (e c)")[:, hf * 92:(hf + 1) * 92]
                        last = pe.matmul(PS[0:92, g, hf * DIM + kc * C:hf * DIM + (kc + 1) * C], src, id96,
                                         start=True, stop=True, is_transpose=True)
                last.then_inc(s_ygp, 1)
            for g in range(T):
                pe.wait_ge(s_yg, g + 1)
                for hf in range(2):
                    last = pe.matmul(PS[:, g, 0:DIM], combT[0:92, g, hf, :], yG[0:92, g, hf, :],
                                     start=(hf == 0), stop=(hf == 1))
                last.then_inc(s_fin, 1)

        @block.scalar
        def _(ac):
            n = [0]

            def link(ins):
                n[0] += 1
                ins.then_inc(achain, 1)
                ac.wait_ge(achain, n[0])

            def evac_xt(r, banks):
                for b in banks:
                    ac.wait_ge(s_xtp, r * 4 + b + 1)
                    ac.activation(XT[0:C, :, b * 256:(b + 1) * 256],
                                  PS[0:C, b, :].rearrange("p (k x) -> p k x", k=KC), ACT.Copy).then_inc(s_xt, 1)

            def sqrt_ln(r):
                ac.wait_ge(s_var, r + 1)
                ac.activation(sd, mv[:, :, 1], ACT.Sqrt, bias=eps).then_inc(s_sd, 1)

            for t in range(T):
                ac.wait_ge(s_emb, t + 1)
                ac.activation(h[:, t, :], PS[:, t, 0:DIM], ACT.Copy).then_inc(s_hcopy, 1)
            ac.wait_ge(s_zero, 3)
            sqrt_ln(0)
            evac_xt(0, range(4))
            ac.wait_ge(s_bias, 32)
            for i in range(8):
                qk, kc = (i // 2) % 2, i % 2
                ac.wait_ge(s_chan, i + 1)
                ac.activation(qkT[0:C, i * 8:(i + 1) * 8, 0:TOKENS],
                              PS[0:C, i, 0:COLS].rearrange("p (t n) -> p t n", t=T), ACT.Identity,
                              bias=cq(Q_QKB + qk * 2 + kc)).then_inc(s_chanv, 1)
            for s in range(4):
                ac.wait_ge(s_gram, s + 1)
                ac.activation(Gs[0:C, s * 16:(s + 1) * 16, :], PS[0:C, s, :].rearrange("p (m x) -> p m x", m=16),
                              ACT.Copy).then_inc(s_gramv, 1)
            ac.wait_ge(s_et, 1)
            for b in range(2):
                ac.activation(Tm[:, :, b * 8:(b + 1) * 8, :],
                              PS[:, 4 + b, 0:384].rearrange("p (r a c) -> p a r c", r=8, a=3), ACT.Copy)\
                  .then_inc(s_etv, 1)
            ac.wait_ge(s_et, 2)
            for b in range(2):
                ac.activation(E[:, :, b * 8:(b + 1) * 8, 0:16],
                              PS[:, 6 + b, 0:384].rearrange("p (r a c) -> p a r c", r=8, a=3), ACT.Copy)\
                  .then_inc(s_etv, 1)
            ac.wait_ge(s_piv, 1)
            ac.activation(sq.rearrange("p (a j) -> p a j", a=3), Ef[:, :, 0:496:33], ACT.Sqrt).then_inc(s_sq, 1)
            ac.wait_ge(s_back, 1)
            src = PS[0:C, 0, :].rearrange("p (j m) -> p m j", j=8)
            for hd in range(HC):
                last = ac.activation(BD[0:C, :, hd * 16:hd * 16 + 8], src, ACT.Copy, scale=head[hd])
            last.then_inc(s_bda, 1)
            for b in range(0, 8, 2):
                ac.wait_ge(s_qt, b + 1)
                ac.activation(qt[0:C, b * 8:(b + 1) * 8, :], PS[0:C, b, 0:320].rearrange("p (m n) -> p m n", m=8),
                              ACT.Copy).then_inc(s_qte, 1)
            ac.wait_ge(s_qte, 8)
            for hd in (2, 3):
                for a in range(2):
                    last = ac.activation(qb_out(a, hd), qb_in(a), ACT.Copy, scale=head[hd])
            last.then_inc(s_qba, 1)
            for t in range(T):
                ac.wait_ge(s_dots, t + 1)
                ac.activation(S2[:, t, :], PS[:, t, 0:8 * TOKENS], ACT.Square).then_inc(s_s2, 1)

            def mix_evac(t):
                ac.wait_ge(s_mixp, t + 1)
                ac.activation(Mx[:, t, :, :, 0:TOKENS].rearrange("p c a n -> p (c a) n"),
                              PS[:, t, 0:8 * TOKENS].rearrange("p (x n) -> p x n", n=TOKENS), ACT.Identity,
                              bias=convb).then_inc(s_mixe, 1)

            def exp_pair(u):
                ac.wait_ge(s_sub, u + 1)
                v = Mx[:, 2 * u:2 * u + 2, :, :, 0:TOKENS].rearrange("p t c a n -> p (t c a) n")
                ac.activation(v, v, ACT.Exp).then_inc(s_exp, 1)

            ac.wait_ge(s_mix1, 2)
            for t in range(T):
                mix_evac(t)
            for u in range(4):
                exp_pair(u)
            for t in range(T):
                ac.wait_ge(s_atp, t + 1)
                ac.activation(attnT[:, t, :], PS[:, 4 + t % 4, :], ACT.Copy).then_inc(s_atT, 1)
            ac.wait_ge(s_av, 1)
            for kc in range(KC):
                ac.activation(XTi[:, kc, :, 0, 0:TOKENS],
                              PS[0:C, kc, 0:320].rearrange("p (t n) -> p t n", t=T)[:, :, 0:TOKENS], ACT.Copy)\
                  .then_inc(s_oT, 1)

            sqrt_ln(1)
            evac_xt(1, range(4))
            for i in range(4):
                ac.wait_ge(s_chan, 8 + i + 1)
                ac.activation(vT[0:C, i * 8:(i + 1) * 8, :], PS[0:C, 4 + i, 0:COLS].rearrange("p (t n) -> p t n", t=T),
                              ACT.Identity, bias=cq(Q_VB + i % 2)).then_inc(s_chanv, 1)
            for a in range(2):
                ac.wait_ge(s_wsub, a + 1)
                ac.activation(Wm[0:C, a * 16:(a + 1) * 16, :], Wm[0:C, a * 16:(a + 1) * 16, :], ACT.Exp)\
                  .then_inc(s_wexp, 1)
            ac.wait_ge(s_zero, 5)
            for b in range(4):
                ac.wait_ge(s_wv, b + 1)
                ac.activation(oS[0:C, b * 8:(b + 1) * 8, :], PS[0:C, 2 + b, 0:COLS].rearrange("p (t n) -> p t n", t=T),
                              ACT.Copy).then_inc(s_os, 1)
            evac_xt(2, range(4))
            ac.wait_ge(s_gva, 1)
            ac.activation(gg[:, 3:4], gg[:, 2:3], ACT.Sqrt, bias=eps12).then_inc(s_gsd, 1)
            ac.wait_ge(s_x1p, 1)
            ac.wait_ge(s_gsc, 1)
            for b in range(4):
                for kc in range(KC):
                    last = ac.activation(
                        x1T[0:C, kc, b * 148:(b + 1) * 148].rearrange("p (x n) -> p x n", n=TOKENS),
                        PS[0:C, b, kc * 256:(kc + 1) * 256].rearrange("p (x n) -> p x n", n=HALF)[:, :, 0:TOKENS],
                        ACT.Identity, bias=gbi[0:C, kc:kc + 1], scale=gsc[0:C, kc:kc + 1])
            last.then_inc(s_x1, 1)
            ac.wait_ge(s_nm, 1)
            ac.activation(ga[0:IMAGES, :], sc16[0:IMAGES, :], ACT.Exp).then_inc(s_ge, 1)
            ac.wait_ge(s_gbp, 1)
            ac.activation(Gb[0:C, :, :].rearrange("p e b -> p (e b)"), PS[0:C, 6, 0:128], ACT.Copy).then_inc(s_gb, 1)
            with ac.Fori(0, EXPERTS // 2) as it:
                for b in range(2):
                    ac.activation(fcb[:, b, :], fcball[:, it * 2 + b, :], ACT.Copy).then_inc(s_fcb, 1)
                    ac.wait_ge(s_fcb, it * 2 + (b + 1))
                    for i in range(2 * FC):
                        f, nh = divmod(i, 2)
                        ac.wait_ge(s_hp, it * 24 + (b * 12 + i + 1))
                        ac.activation(hT[b][:, f, nh * COLS:(nh + 1) * COLS], PS[:, i % 4, 0:COLS],
                                      ACT.Gelu_apprx_tanh,
                                      bias=fcb[:, b, f:f + 1]).then_inc(s_gelu, 1)
            ac.wait_ge(s_gva, 2)
            ac.activation(gg[:, 3:4], gg[:, 2:3], ACT.Sqrt, bias=eps12).then_inc(s_gsd, 1)
            ac.wait_ge(s_gsc, 2)
            for kc in range(KC):
                ac.activation(XT[0:C, kc, :].rearrange("p (x n) -> p x n", n=HALF)[:, :, 0:TOKENS],
                              acc[0:C, kc, :].rearrange("p (x n) -> p x n", n=TOKENS), ACT.Identity,
                              bias=gbi[0:C, kc:kc + 1], scale=gsc[0:C, kc:kc + 1]).then_inc(s_x2, 1)

            sqrt_ln(2)
            evac_xt(3, range(4))
            for i in range(4):
                ac.wait_ge(s_q2, i + 1)
                ac.activation(qT2[0:C, i * 8:(i + 1) * 8, :], PS[0:C, 4 + i, 0:COLS].rearrange("p (t n) -> p t n", t=T),
                              ACT.Copy).then_inc(s_q2e, 1)
            for t in range(T):
                ac.wait_ge(s_kv2, t + 1)
                ac.activation(A[:, t, :], PS[:, t % 4, 0:2 * DIM], ACT.Copy)
                ac.activation(Aabs[:, t, :], PS[:, t % 4, 0:DIM], ACT.Abs).then_inc(s_kv2e, 1)
            for i in range(4):
                a, kc = divmod(i, 2)
                ac.wait_ge(s_o2, i + 1)
                ac.activation(XTi[:, kc, :, a, 0:TOKENS], PS[0:C, 4 + i, 0:COLS].rearrange("p (t n) -> p t n", t=T),
                              ACT.Copy).then_inc(s_o2e, 1)

            sqrt_ln(3)
            evac_xt(4, range(4))
            ac.wait_ge(s_lsub, 1)
            ac.activation(pr[:, :, :], pr[:, :, :], ACT.Exp).then_inc(s_lexp, 1)
            for g in range(T):
                ac.wait_ge(s_xip, g + 1)
                ac.activation(xinT[0:C, :, :, g * CAP:(g + 1) * CAP],
                              PS[0:C, g, 0:KC * GE].rearrange("p (k e c) -> p k e c", k=KC, e=EXPERTS),
                              ACT.Copy).then_inc(s_xin, 1)
            for b in range(4):
                ac.wait_ge(s_ctp, b + 1)
                ac.activation(combT[0:92, 2 * b:2 * b + 2, :, :].rearrange("p g a n -> p (g a n)"), PS[0:92, b, :],
                              ACT.Copy).then_inc(s_ct, 1)
            with ac.Fori(0, EXPERTS // 2) as it:
                for b in range(2):
                    ac.wait_ge(s_edone, it * 2 + EXPERTS)
                    for i in range(3):
                        ac.wait_ge(s_h1p, it * 6 + (3 * b + i + 1))
                        ac.activation(hT1[b][:, 2 * i:2 * i + 2, :].rearrange("p f n -> p (f n)"),
                                      PS[:, 3 * b + i, 0:2 * SLOTS], ACT.Relu).then_inc(s_relu, 1)
            for g in range(T):
                ac.wait_ge(s_ygp, g + 1)
                ac.activation(yG[0:92, g, :, :].rearrange("p a n -> p (a n)"), PS[0:92, g, 0:2 * DIM],
                              ACT.Copy).then_inc(s_yg, 1)

        @block.vector
        def _(ve):
            n = [0]

            def link(ins):
                n[0] += 1
                ins.then_inc(dchain, 1)
                ve.wait_ge(dchain, n[0])

            def layer_norm(r):
                for t in range(T):
                    if r == 0:
                        ve.wait_ge(s_hcopy, t + 1)
                    last = ve.bn_stats(stats[:, t, :], h[:, t, :])
                link(last)
                for t in range(T):
                    last = ve.bn_aggr(mv[:, t, :], stats[:, t, :])
                last.then_inc(s_var, 1)
                ve.wait_ge(s_sd, r + 1)
                link(ve.reciprocal(rstd, sd))
                for t in range(T):
                    ve.tensor_scalar(xn[:, t, :], h[:, t, :], mv[:, t, 0:1], rstd[:, t:t + 1], ALU.subtract,
                                     ALU.mult).then_inc(s_xn, 1)

            layer_norm(0)
            ve.wait_ge(s_bias, 32)
            link(ve.tensor_tensor(wpT[0:HEADS, :], cq(Q_CW, HEADS, HEADS), cq(Q_CW + HEADS, HEADS, HEADS), ALU.add))
            ve.tensor_scalar(wpT[0:HEADS, :], wpT[0:HEADS, :], cq(Q_GS, HEADS), None, ALU.mult).then_inc(s_mixw, 1)
            ve.wait_ge(s_mixr, 1)
            ve.wait_ge(s_zero, 3)
            ve.tensor_copy(convb, PS[:, 7, HEADS:HEADS + 1])
            ve.tensor_tensor(mixT[:, :, 0:60].rearrange("p k (o n) -> p k o n", o=HC),
                             bc(PS[:, 7, 0:HEADS].rearrange("p (k o) -> p k o", k=KC), 3, NCH),
                             bc(bc(con[:, K_DN:K_DN + NCH], 1, HC), 1, KC), ALU.mult).then_inc(s_mix1, 2)

            for t in range(T):
                ve.wait_ge(s_tok, t + 1)
                b = 2 * (t % 4)
                ve.tensor_tensor(A[:, t, :], PS[:, b, 0:2 * DIM], row[:, R_QKVB:R_QKVB + 2 * DIM], ALU.add)
                ve.tensor_tensor(vpad[:, t, :].rearrange("p (x c) -> p x c", c=32)[:, :, 0:HD],
                                 PS[:, b + 1, 0:DIM].rearrange("p (x c) -> p x c", c=HD),
                                 row[:, R_QKVB + 2 * DIM:R_QKVB + 3 * DIM].rearrange("p (x c) -> p x c", c=HD),
                                 ALU.add).then_inc(s_tokv, 1)

            ve.wait_ge(s_etv, 5)
            inv3 = inv.unsqueeze(2)
            for s in range(15):
                r = 15 - s
                link(ve.reciprocal(inv3, E[:, :, s, s:s + 1]))
                link(ve.tensor_tensor(lcol[:, :, 0:r], E[:, :, s + 1:16, s], inv3.broadcast_to([128, 3, r]), ALU.mult))
                prod = Pb[:, 0:3 * r * 16].rearrange("p (a r c) -> p a r c", a=3, r=r)
                link(ve.tensor_tensor(prod, bc(lcol[:, :, 0:r], 3, 16), bc(E[:, :, s, s + 1:s + 17], 2, r), ALU.mult))
                link(ve.tensor_tensor(E[:, :, s + 1:16, s + 1:s + 17], E[:, :, s + 1:16, s + 1:s + 17], prod,
                                      ALU.subtract))
            ve.sem_inc(s_piv, 1)
            ve.wait_ge(s_sq, 1)
            link(ve.reciprocal(rs, sq))
            Er = Q[:, 5120:6656].rearrange("p (x c) -> p x c", c=32)
            link(ve.tensor_tensor(Er, Er, bc(rs, 2, 32), ALU.mult))
            for s in range(16):
                w = 16 - s
                link(ve.tensor_scalar(tsg[:, :, s:s + 1], Tm[:, :, s, s:s + 1], 0.0, 2.0, ALU.is_ge, ALU.mult))
                sr = Pb[:, 0:3 * w].rearrange("p (a c) -> p a c", a=3)
                link(ve.scalar_tensor_tensor(sr, tsg[:, :, s:s + 1].broadcast_to([128, 3, w]), -1.0,
                                             E[:, :, s, s:16], ALU.add, ALU.mult))
                link(ve.tensor_tensor(Tm[:, :, s, s:16], Tm[:, :, s, s:16], sr, ALU.add))
                if s == 15:
                    break
                r = 15 - s
                link(ve.reciprocal(inv3, Tm[:, :, s, s:s + 1]))
                link(ve.tensor_tensor(lcol[:, :, 0:r], Tm[:, :, s + 1:16, s], inv3.broadcast_to([128, 3, r]), ALU.mult))
                prod = Pb[:, 0:3 * r * r].rearrange("p (a r c) -> p a r c", a=3, r=r)
                link(ve.tensor_tensor(prod, bc(lcol[:, :, 0:r], 3, r), bc(Tm[:, :, s, s + 1:16], 2, r), ALU.mult))
                link(ve.tensor_tensor(Tm[:, :, s + 1:16, s + 1:16], Tm[:, :, s + 1:16, s + 1:16], prod, ALU.subtract))
            link(ve.tensor_scalar(nsg, tsg, -1.0, 1.0, ALU.mult, ALU.add))
            ve.wait_ge(s_zero, 4)
            for par in range(2):
                p0 = par * 64
                o = BLK[p0:p0 + 64].rearrange("p j (a x) -> p a j x", a=3)[:, :, :, par * 16:par * 16 + 16]
                last = ve.tensor_tensor(o, E[p0:p0 + 64, :, :, 16:32], bc(nsg[p0:p0 + 64], 3, 16), ALU.mult)
            last.then_inc(s_blk, 1)
            ve.wait_ge(s_back, 1)
            src = PS[0:C, 1, :].rearrange("p (j m) -> p m j", j=8)
            for hd in range(HC):
                last = ve.tensor_scalar(BD[0:C, :, hd * 16 + 8:hd * 16 + 16], src, head[hd], None, ALU.mult)
            last.then_inc(s_bdv, 1)
            for b in range(1, 8, 2):
                ve.wait_ge(s_qt, b + 1)
                ve.tensor_copy(qt[0:C, b * 8:(b + 1) * 8, :], PS[0:C, b, 0:320].rearrange("p (m n) -> p m n", m=8))\
                  .then_inc(s_qte, 1)
            ve.wait_ge(s_qte, 8)
            for hd in (0, 1):
                for a in range(2):
                    last = ve.tensor_scalar(qb_out(a, hd), qb_in(a), head[hd], None, ALU.mult)
            last.then_inc(s_qbv, 1)
            for u in range(4):
                v = Mx[:, 2 * u:2 * u + 2, :, :, 0:TOKENS].rearrange("p t c a n -> p (t c a) n")
                m = mx[:, 2 * u:2 * u + 2, :].rearrange("p t x -> p (t x)")
                ve.wait_ge(s_mixe, 2 * u + 2)
                link(ve.tensor_reduce(m, v, AX, ALU.max))
                ve.tensor_tensor(v, v, bc(m, 2, TOKENS), ALU.subtract).then_inc(s_sub, 1)
            for u in range(4):
                v = Mx[:, 2 * u:2 * u + 2, :, :, 0:TOKENS].rearrange("p t c a n -> p (t c a) n")
                m = sme[:, 2 * u:2 * u + 2, :].rearrange("p t x -> p (t x)")
                q = rsm[:, 2 * u:2 * u + 2, :].rearrange("p t x -> p (t x)")
                ve.wait_ge(s_exp, u + 1)
                link(ve.tensor_reduce(m, v, AX, ALU.add))
                link(ve.reciprocal(q, m))
                ve.tensor_tensor(v, v, bc(q, 2, TOKENS), ALU.mult).then_inc(s_att, 1)
            ve.wait_ge(s_av, 1)
            for kc in range(KC):
                ve.tensor_copy(XTi[:, kc, :, 1, 0:TOKENS],
                               PS[0:C, 2 + kc, 0:320].rearrange("p (t n) -> p t n", t=T)[:, :, 0:TOKENS])\
                  .then_inc(s_oTv, 1)

            def residual(r, done, base):
                for t in range(T):
                    ve.wait_ge(done, base + t + 1)
                    last = ve.tensor_tensor(h[:, t, :], PS[:, t, 0:DIM], h[:, t, :], ALU.add)
                    last.then_inc(s_h, 1)
                ve.wait_ge(s_h, (r + 1) * T)

            ve.wait_ge(s_hb, 1)
            residual(0, s_prj, 0)
            layer_norm(1)

            for t in range(T):
                ve.wait_ge(s_tok, T + t + 1)
                ve.tensor_tensor(A[:, t, :], PS[:, t % 4, 0:2 * DIM], row[:, R_W1B:R_W1B + 2 * DIM], ALU.add)\
                  .then_inc(s_tokv, 1)
            for a in range(2):
                w = Wm[0:C, a * 16:(a + 1) * 16, :]
                ve.wait_ge(s_w_ps, a + 1)
                link(ve.scalar_tensor_tensor(w, PS[0:C, a, :].rearrange("p (m x) -> p m x", m=16),
                                             float(1.0 / np.sqrt(np.float32(TOKENS))),
                                             bc(con[0:C, K_NEG:K_NEG + 32], 1, 16), ALU.mult, ALU.add))
                link(ve.tensor_reduce(wmax[0:C, a * 16:(a + 1) * 16], w, AX, ALU.max))
                ve.tensor_tensor(w, w, bc(wmax[0:C, a * 16:(a + 1) * 16], 2, 32), ALU.subtract).then_inc(s_wsub, 1)
            for a in range(2):
                w = Wm[0:C, a * 16:(a + 1) * 16, :]
                ve.wait_ge(s_wexp, a + 1)
                link(ve.tensor_reduce(wsum[0:C, a * 16:(a + 1) * 16], w, AX, ALU.add))
                link(ve.reciprocal(wrec[0:C, a * 16:(a + 1) * 16], wsum[0:C, a * 16:(a + 1) * 16]))
                link(ve.tensor_tensor(w, w, bc(wrec[0:C, a * 16:(a + 1) * 16], 2, 32), ALU.mult))
            ve.wait_ge(s_zero, 5)
            for j in range(PAIRS):
                p0 = 32 * j
                last = ve.transpose(BD2[p0:p0 + 32, :, p0:p0 + 32], Wm[p0:p0 + 32, :, :])
            last.then_inc(s_wT, 1)
            ve.wait_ge(s_zb, 1)
            for t in range(T):
                ve.wait_ge(s_w2p, t + 1)
                last = ve.tensor_tensor(xn[:, t, :], PS[:, t, 0:DIM], xn[:, t, :], ALU.add)
                last.then_inc(s_s, 1)
            ve.wait_ge(s_s, T)

            NALL = float(IMAGES * TOKENS * DIM)

            def global_norm(r, p, parts, bank, wcol, bcol):
                link(ve.bn_aggr(gmv[0:p], stats[0:p].rearrange("p t x -> p (t x)")[:, 0:parts]))
                ve.tensor_copy(gst[0:p, 0:1], gmv[0:p, 0:1])
                link(ve.tensor_tensor(gg[0:p, 0:1], gmv[0:p, 0:1], gmv[0:p, 0:1], ALU.mult))
                ve.tensor_tensor(gst[0:p, 1:2], gg[0:p, 0:1], gmv[0:p, 1:2], ALU.add).then_inc(s_gst, 1)
                ve.wait_ge(s_gps, r + 1)
                used = 2 * TOKENS if p == 128 else p
                link(ve.tensor_scalar(gg[:, 0:2], PS[:, bank, 0:2], 1.0 / used, None, ALU.mult))
                link(ve.tensor_tensor(gg[:, 2:3], gg[:, 0:1], gg[:, 0:1], ALU.mult))
                link(ve.tensor_tensor(gg[:, 2:3], gg[:, 1:2], gg[:, 2:3], ALU.subtract))
                ve.tensor_scalar(gg[:, 2:3], gg[:, 2:3], NALL / (NALL - 1.0), None, ALU.mult).then_inc(s_gva, 1)
                ve.wait_ge(s_gsd, r + 1)
                link(ve.reciprocal(gg[:, 4:5], gg[:, 3:4]))
                link(ve.tensor_scalar(gsc[0:C], cq(wcol, C, KC), gg[0:C, 4:5], None, ALU.mult))
                link(ve.tensor_scalar(gbi[0:C], gsc[0:C], gg[0:C, 0:1], None, ALU.mult))
                ve.tensor_tensor(gbi[0:C], cq(bcol, C, KC), gbi[0:C], ALU.subtract).then_inc(s_gsc, 1)

            for t in range(T):
                last = ve.bn_stats(stats[:, t, :], xn[:, t, :])
            link(last)
            global_norm(0, 128, T * 6, 4, Q_LN1W, Q_LN1B)

            ve.wait_ge(s_x1, 1)
            ve.tensor_reduce(xbar[0:C], x1T[0:C, :, :].rearrange("p k (b n) -> p (k b) n", n=TOKENS)
                             .rearrange("p (k b) n -> p k b n", k=KC), AX, ALU.add).then_inc(s_xbar, 1)
            ve.tensor_copy(acc[0:C, :, :], x1T[0:C, :, :])
            ve.wait_ge(s_rps, 1)
            link(ve.scalar_tensor_tensor(sc16[0:IMAGES], PS[0:IMAGES, 5, 0:EXPERTS], 1.0 / TOKENS,
                                         row[0:IMAGES, R_RB:R_RB + EXPERTS], ALU.mult, ALU.add))
            link(ve.tensor_reduce(gone[0:IMAGES, 0:1], sc16[0:IMAGES], AX, ALU.max))
            ve.tensor_scalar(sc16[0:IMAGES], sc16[0:IMAGES], gone[0:IMAGES, 0:1], None, ALU.subtract).then_inc(s_nm, 1)
            ve.wait_ge(s_ge, 1)
            link(ve.tensor_reduce(gone[0:IMAGES, 1:2], ga[0:IMAGES], AX, ALU.add))
            link(ve.reciprocal(gone[0:IMAGES, 2:3], gone[0:IMAGES, 1:2]))
            link(ve.tensor_scalar(ga[0:IMAGES], ga[0:IMAGES], gone[0:IMAGES, 2:3], None, ALU.mult))
            link(ve.max(g8[0:IMAGES], ga[0:IMAGES]))
            link(ve.max_index(gi[0:IMAGES], g8[0:IMAGES], ga[0:IMAGES]))
            link(ve.tensor_copy(gi_f[0:IMAGES], gi[0:IMAGES]))
            link(ve.tensor_scalar(gm[0:IMAGES], con[0:IMAGES, K_I8:K_I8 + 8], gi_f[0:IMAGES, 0:1], None, ALU.is_equal))
            link(ve.scalar_tensor_tensor(gm[0:IMAGES], con[0:IMAGES, K_I8:K_I8 + 8], gi_f[0:IMAGES, 1:2],
                                         gm[0:IMAGES], ALU.is_equal, ALU.add))
            link(ve.tensor_tensor(gm[0:IMAGES], gm[0:IMAGES], ga[0:IMAGES], ALU.mult))
            ve.tensor_tensor(Gd[:, :, :], bc(gm[0:IMAGES], 2, IMAGES), bc(con[0:IMAGES, K_ID:K_ID + IMAGES], 1, EXPERTS),
                             ALU.mult).then_inc(s_gd, 1)
            ve.wait_ge(s_gb, 1)
            ve.sem_inc(s_acc, 1)
            with ve.Fori(0, EXPERTS // 2) as it:
                for b in range(2):
                    ve.wait_ge(s_edone, it * 2 + (b + 1))
                    for i in range(4):
                        kc, nh = divmod(i, 2)
                        y = ytmp[0:C, i % 2, :]
                        g = Gb[0:C, it * 2 + b, nh * 8:(nh + 1) * 8]
                        ve.scalar_tensor_tensor(y.rearrange("p (x n) -> p x n", n=TOKENS),
                                                PS[0:C, 4 + i, 0:COLS].rearrange("p (x n) -> p x n", n=TOKENS),
                                                col[0:C, it * 4 + (Q_PB + b * 2 + kc)].unsqueeze(1),
                                                bc(g, 2, TOKENS), ALU.add, ALU.mult).then_inc(s_ytmp, 1)
                        ve.wait_ge(s_ytmp, it * 8 + (b * 4 + i + 1))
                        ve.tensor_tensor(acc[0:C, kc, nh * COLS:(nh + 1) * COLS],
                                         acc[0:C, kc, nh * COLS:(nh + 1) * COLS], y, ALU.add).then_inc(s_acc, 1)
            ve.wait_ge(s_acc, 4 * EXPERTS + 1)
            for i in range(4):
                kc, nh = divmod(i, 2)
                last = ve.bn_stats(stats[0:C, i, :], acc[0:C, kc, nh * COLS:(nh + 1) * COLS])
            link(last)
            global_norm(1, C, 24, 0, Q_LN2W, Q_LN2B)
            residual(1, s_x2p, 0)
            layer_norm(2)

            ve.wait_ge(s_q2e, 4)
            link(ve.tensor_reduce(sq2[0:C], qT2[0:C], AX, ALU.add, apply_absolute_value=True))
            link(ve.tensor_scalar(sq2[0:C], sq2[0:C], 1e-12, None, ALU.max))
            ve.wait_ge(s_kvp, 1)
            for a in range(2):
                last = ve.tensor_scalar(sk2[0:C, a * 16:(a + 1) * 16], PS[0:C, 2 + a, a * 16:(a + 1) * 16], 1e-12,
                                        None, ALU.max)
            link(last)
            link(ve.reciprocal(sq2[0:C], sq2[0:C]))
            link(ve.reciprocal(sk2[0:C], sk2[0:C]))
            for a in range(2):
                last = ve.tensor_tensor(kvs[0:C, a * 16:(a + 1) * 16, :],
                                        PS[0:C, a, :].rearrange("p (m x) -> p m x", m=16),
                                        bc(sk2[0:C, a * 16:(a + 1) * 16], 2, 32), ALU.mult)
            link(last)
            link(ve.tensor_tensor(kvs[0:C], kvs[0:C], bc(sq2[0:C], 2, 32), ALU.mult))
            ve.wait_ge(s_zero, 6)
            for j in range(PAIRS):
                p0 = 32 * j
                ve.tensor_tensor(BD2[p0:p0 + 32, :, p0:p0 + 32], kvs[p0:p0 + 32],
                                 bc(con[p0:p0 + 32, K_PAIR:K_PAIR + 32], 1, 32), ALU.mult).then_inc(s_bd3, 1)
            ve.wait_ge(s_hb, 2)
            residual(2, s_prj, T)
            layer_norm(3)

            ve.wait_ge(s_lg, 1)
            lg = PS[:, 4, 0:64].rearrange("p (g e) -> p g e", g=T)
            link(ve.tensor_reduce(lmax, lg, AX, ALU.max))
            ve.tensor_tensor(pr[:, :, :], lg, bc(lmax, 2, EXPERTS), ALU.subtract).then_inc(s_lsub, 1)
            ve.wait_ge(s_lexp, 1)
            link(ve.tensor_reduce(lmax, pr[:, :, :], AX, ALU.add))
            link(ve.reciprocal(lmax, lmax))
            link(ve.tensor_tensor(pr[:, :, :], pr[:, :, :], bc(lmax, 2, EXPERTS), ALU.mult))
            for g in range(T):
                last = ve.max(v8[:, g, :], pr[:, g, :])
            link(last)
            for g in range(T):
                last = ve.max_index(i8[:, g, :], v8[:, g, :], pr[:, g, :])
            link(last)
            link(ve.tensor_copy(i8f[:, :, :], i8[:, :, :]))
            for k in range(2):
                last = ve.tensor_tensor(m12[:, k], bc(con[:, K_I8:K_I8 + 8], 1, T), bc(i8f[:, :, k], 2, EXPERTS),
                                        ALU.is_equal)
            link(last)
            mf = m12[:, :, :, :].rearrange("p k g e -> p (k g e)")
            ve.tensor_scalar(mf, mf, con[:, K_VALID:K_VALID + 1], None, ALU.mult).then_inc(s_m12, 1)
            ve.wait_ge(s_rk, 1)
            ve.wait_ge(s_m12, 1)
            link(ve.tensor_tensor(rank[:, :, :, :].rearrange("p k g e -> p (k g e)"), PS[:, 5, 0:128], mf, ALU.mult))
            link(ve.tensor_tensor(rank[:, 0], rank[:, 0], rank[:, 1], ALU.add))
            link(ve.tensor_scalar(rank[:, 0], rank[:, 0], -1.0, None, ALU.add))
            link(ve.tensor_tensor(gse[:, :, :], m12[:, 0], m12[:, 1], ALU.add))
            link(ve.tensor_tensor(gse[:, :, :], gse[:, :, :], pr[:, :, :], ALU.mult))
            GEf = T * EXPERTS
            rk = bc(rank[:, 0].rearrange("p g e -> p (g e)"), 2, CAP)
            dv = Q[:, 0:T * GE].rearrange("p (x c) -> p x c", c=CAP)
            cv = Q[:, T * GE:2 * T * GE].rearrange("p (x c) -> p x c", c=CAP)
            ve.tensor_tensor(dv, rk, bc(con[:, K_I23:K_I23 + CAP], 1, GEf), ALU.is_equal).then_inc(s_disp, 1)
            ve.wait_ge(s_disp, 1)
            ve.tensor_tensor(cv, dv, bc(gse[:, :, :].rearrange("p g e -> p (g e)"), 2, CAP), ALU.mult)\
              .then_inc(s_comb, 1)
            ve.sem_inc(s_y1, 2)
            with ve.Fori(0, EXPERTS // 2) as it:
                for b in range(2):
                    ve.wait_ge(s_edone, it * 2 + (EXPERTS + b + 1))
                    ve.tensor_copy(yT[0:C, :, :, it * 2 + b, :],
                                   PS[0:C, 6 + b, 0:KC * SLOTS].rearrange("p (k g c) -> p k g c", k=KC, g=T))\
                      .then_inc(s_y1, 1)
            for t in range(T):
                ve.wait_ge(s_fin, t + 1)
                ve.tensor_tensor(h[:, t, :], PS[:, t, 0:DIM], h[:, t, :], ALU.add).then_inc(s_res, 1)


def constants():
    k = np.zeros((128, K_ALL), np.float32)
    p = np.arange(128)
    k[:, K_ID:K_ID + 128] = np.eye(128)
    k[:, K_TRI:K_TRI + 128] = p[:, None] <= p[None, :]
    k[:, K_VALID:K_VALID + 128] = (p % HALF < TOKENS)[:, None]
    k[:, K_ONE:K_ONE + 128] = 1
    k[:, K_II:K_II + 64] = (p % 64)[:, None] == np.arange(64)
    same = ((p // HD) % 2)[:, None] == np.arange(32) // HD
    k[:, K_PAIR:K_PAIR + 32] = same
    k[:, K_NEG:K_NEG + 32] = np.where(same, 0.0, -1e30)
    k[:, K_HEAD:K_HEAD + HC] = (p // HD)[:, None] == np.arange(HC)
    for hd in range(HEADS):
        c0 = K_E1 + (hd // HC) * 64 + (hd % HC) * NCH
        k[hd, c0:c0 + NCH] = 1
    q = p % 64
    k[:, K_DN:K_DN + NCH] = ((q % NCH)[:, None] == np.arange(NCH)) & (q < HC * NCH)[:, None]
    k[:, K_I8:K_I8 + EXPERTS] = np.arange(EXPERTS)
    k[:, K_I23:K_I23 + CAP] = np.arange(CAP)
    k[0, K_IND:K_IND + 128] = (p % HALF > 0) & (p % HALF < TOKENS)
    k[1, K_IND:K_IND + 128] = p % HALF == 0
    k[:, K_EYE:K_EYE + 256] = np.eye(16).reshape(-1)
    return k


def layout(i):
    def chunks(w, parts, size):
        return w.reshape(parts, size, -1).transpose(1, 0, 2)

    pat = i["x"].reshape(IMAGES, 3, 6, 16, 6, 16).transpose(3, 5, 1, 0, 2, 4).reshape(PK, 128, T, 2, PATCHES)
    padded = np.zeros((128, PK, T, 2, HALF), np.float32)
    padded[..., 1:TOKENS] = pat.transpose(1, 0, 2, 3, 4)
    rows = np.concatenate([i["L0_attn_qkv_b"], i["L0_attn_proj_b"], i["L0_ffn_W1_b"][:2 * DIM], i["L0_ffn_W2_b"],
                           i["L0_ffn_r_b"], i["L1_attn_b_proj"]])
    cols = np.zeros((128, Q_ALL), np.float32)
    cols[:C, Q_QKB:Q_QKB + 4] = i["L0_attn_qkv_b"][:2 * DIM].reshape(4, C).T
    cols[:C, Q_VB:Q_VB + 2] = i["L0_ffn_W1_b"][2 * DIM:].reshape(2, C).T
    for at, name in ((Q_LN1W, "ln1_w"), (Q_LN1B, "ln1_b"), (Q_LN2W, "ln2_w"), (Q_LN2B, "ln2_b")):
        cols[:C, at:at + 2] = i["L0_ffn_" + name].reshape(2, C).T
    cols[:C, Q_PB:Q_PB + 16] = i["L0_ffn_proj_b"].reshape(2 * EXPERTS, C).T
    cols[:, Q_FCB:Q_FCB + 48] = i["L0_ffn_fc_b"].reshape(FC * EXPERTS, 128).T
    cols[:, Q_GS] = i["L0_attn_grassman_scale"]
    cols[:HEADS, Q_CB] = i["L0_attn_conv_b"]
    cols[:HEADS, Q_CW:Q_CW + 24] = i["L0_attn_conv_w"].reshape(HEADS, 2, HEADS).transpose(2, 1, 0).reshape(HEADS, 24)
    ew = lambda w: w.reshape(EXPERTS, KC, C, FF).transpose(0, 2, 1, 3).reshape(EXPERTS, C, KC * FF)
    eo = lambda w: w.reshape(EXPERTS, FC, 128, DIM).transpose(0, 2, 1, 3).reshape(EXPERTS, 128, FC * DIM)
    return {
        "patches": padded.reshape(128, PK, T * 128),
        "tok_w": chunks(i["L0_tok_W"].reshape(DIM, 16, 16, 3).reshape(DIM, 768).T, PK, 128),
        "cls_b": np.stack([i["L0_tok_b"], i["cls_tok"].reshape(DIM)]),
        "rows": rows,
        "cols": cols,
        "consts": constants(),
        "qkv_w": chunks(i["L0_attn_qkv_w"].T, KC, C),
        "proj_w": chunks(i["L0_attn_proj_w"].T, KC, C),
        "w1": chunks(i["L0_ffn_W1_w"], KC, C),
        "w2": chunks(i["L0_ffn_W2_w"], KC, C),
        "r_w": chunks(i["L0_ffn_r_w"], KC, C),
        "fc_w": ew(i["L0_ffn_fc_w"]),
        "pr_w": eo(i["L0_ffn_proj_w"]),
        "qkv2_w": chunks(i["L1_attn_w_qkv"].T, KC, C),
        "proj2_w": chunks(i["L1_attn_w_proj"].T, KC, C),
        "router_w": chunks(i["L1_ffn_w_router"], KC, C),
        "wi": ew(i["L1_ffn_wi"]),
        "wo": eo(i["L1_ffn_wo"]),
    }


def kernel(**inputs):
    import concourse.bacc as bacc
    from concourse.bass_utils import run_bass_kernel_spmd

    arrays = {f"in_{k}": np.ascontiguousarray(v) for k, v in layout({k: np.asarray(v) for k, v in inputs.items()}).items()}
    nc = bacc.Bacc("TRN2", target_bir_lowering=False, num_devices=1)
    args = [nc.dram_tensor(k, v.shape, mybir.dt.from_np(v.dtype), kind="ExternalInput").ap() for k, v in arrays.items()]
    scratch = nc.dram_tensor("scratch", (T, 2, KC, C, TOKENS), F32, kind="Internal").ap()
    out = nc.dram_tensor("out_0", (IMAGES, TOKENS, DIM), F32, kind="ExternalOutput").ap()
    vit_tower(nc, *args, scratch, out)
    return run_bass_kernel_spmd(nc, [arrays], core_ids=[0]).results[0]["out_0"]
```

```python
from contextlib import ExitStack

import numpy as np

import concourse.bass as bass
from concourse import mybir

F32 = mybir.dt.float32
U32 = mybir.dt.uint32
I32 = mybir.dt.int32
ALU = mybir.AluOpType
ACT = mybir.ActivationFunctionType
AX = mybir.AxisListType.X

IMAGES, TOKENS, DIM, HEADS, HD = 16, 37, 192, 12, 16
PATCHES = 36
T = IMAGES // 2
HALF = 64
KC = 2
C = DIM // KC
HC = HEADS // KC
PAIRS = HC // 2
COLS = T * TOKENS
ALLC = 2 * COLS
PK = 6
FF = 768
FC = FF // 128
EXPERTS = 8
NCH = 10
CH = 4
NP = NCH * CH
CAP = 23
SLOTS = T * CAP
MATS = 2 * 2 * KC * T

R_QKVB = 0
R_PROJB = R_QKVB + 3 * DIM
R_W1B = R_PROJB + DIM
R_W2B = R_W1B + 2 * DIM
R_RB = R_W2B + DIM
R_BP = R_RB + EXPERTS
R_ALL = R_BP + DIM
Q_QKB = 0
Q_VB = Q_QKB + 4
Q_LN1W = Q_VB + 2
Q_LN1B = Q_LN1W + 2
Q_LN2W = Q_LN1B + 2
Q_LN2B = Q_LN2W + 2
Q_PB = Q_LN2B + 2
Q_FCB = Q_PB + 2 * EXPERTS
Q_GS = Q_FCB + FC * EXPERTS
Q_CB = Q_GS + 1
Q_CW = Q_CB + 1
Q_ALL = Q_CW + 2 * HEADS
K_ID = 0
K_TRI = K_ID + 128
K_VALID = K_TRI + 128
K_ONE = K_VALID + 128
K_II = K_ONE + 128
K_PAIR = K_II + 64
K_NEG = K_PAIR + 32
K_HEAD = K_NEG + 32
K_E1 = K_HEAD + HC
K_DN = K_E1 + 128
K_I8 = K_DN + NCH
K_I23 = K_I8 + EXPERTS
K_IND = K_I23 + CAP
K_EYE = K_IND + 128
K_HALF = K_EYE + 256
K_POW2 = K_HALF + 2
K_ALL = K_POW2 + EXPERTS


def vit_tower(nc, patches, tok_w, cls_b, rows, cols, consts, qkv_w, proj_w, w1, w2, r_w, fc_w, pr_w,
              qkv2_w, proj2_w, router_w, wi, wo, scratch, out):
    ctx = ExitStack()
    with ctx:
        def sb(name, shape, dt=F32):
            return ctx.enter_context(nc.sbuf_tensor(name, shape, dt))

        def sem(name):
            return ctx.enter_context(nc.semaphore(name))

        def bc(ap, axis, n):
            v = ap.unsqueeze(axis)
            shape = list(v.shape)
            shape[axis] = n
            return v.broadcast_to(shape)

        PS = ctx.enter_context(nc.psum_tensor("PS", [128, 8, 512], F32))

        P = sb("P", [128, 2 * FC * ALLC])
        Q = sb("Q", [128, 8192])
        M = sb("M", [128, T * CH * 128])
        h = sb("h", [128, T, DIM])
        xn = sb("xn", [128, T, DIM])
        XT = sb("XT", [128, KC, T * 128])
        x1T = sb("x1T", [128, KC, ALLC])
        acc = sb("acc", [128, KC, ALLC])
        ytmp = sb("ytmp", [128, 2, COLS])
        row = sb("row", [128, R_ALL])
        col = sb("col", [128, Q_ALL])
        con = sb("con", [128, K_ALL])
        cb2 = sb("cb2", [2, DIM])
        qkT = sb("qkT", [128, MATS, NP])
        qt = sb("qt", [128, MATS, NP])
        vpad = sb("vpad", [128, T, HEADS * 32])
        tokw = sb("tokw", [128, PK, DIM])
        qkvw = sb("qkvw", [128, KC, 3 * DIM])
        projw = sb("projw", [128, KC, DIM])
        w1w = sb("w1w", [128, KC, 3 * DIM])
        w2w = sb("w2w", [128, KC, DIM])
        rw = sb("rw", [128, KC, EXPERTS])
        qkv2w = sb("qkv2w", [128, KC, 3 * DIM])
        proj2w = sb("proj2w", [128, KC, DIM])
        routw = sb("routw", [128, KC, EXPERTS])
        wi_sb = sb("wi_sb", [128, 2, KC * FF])
        wo_sb = sb("wo_sb", [128, 2, FC * DIM])
        mixT = sb("mixT", [128, KC, 64])
        small = sb("small", [128, 1024])

        at = [0]

        def sm(*shape):
            n = int(np.prod(shape))
            v = small[:, at[0]:at[0] + n]
            at[0] += n
            if len(shape) == 1:
                return v
            names = "abcd"[:len(shape)]
            return v.rearrange(f"p ({' '.join(names)}) -> p {' '.join(names)}",
                               **{x: s for x, s in zip(names, shape)})

        eps = sm(1)
        dummy = sm(1)
        invu = sm(3).unsqueeze(2)
        Rn = sb("Rn", [128, 2, 3, 16])
        rowm = sm(3, 16)
        rowp = sm(3, 16)
        lcolu = sm(3, 16)
        eps12 = sm(1)
        stats = sm(T, 6)
        mv = sm(T, 2)
        sd = sm(T)
        rstd = sm(T)
        tsg = sm(3, 16)
        nsg = sm(3, 16)
        inv3 = sm(3).unsqueeze(2)
        lcol = sm(3, 16)
        sq3 = sm(3, 16)
        rs3 = sm(3, 16)
        wpT = sm(HEADS)
        convb = sm(1)
        mx = sm(T, 8)
        sme = sm(T, 8)
        rsm = sm(T, 8)
        wmax = sm(32)
        wsum = sm(32)
        wrec = sm(32)
        gst = sm(2)
        gmv = sm(2)
        gg = sm(8)
        gsc = sm(KC)
        gbi = sm(KC)
        xbar = sm(KC, IMAGES)
        sc16 = sm(EXPERTS)
        ga = sm(EXPERTS)
        g8 = sm(8)
        gi_f = sm(8)
        gone = sm(8)
        gm = sm(EXPERTS)
        sq2 = sm(32)
        sk2 = sm(32)
        lmax = sm(T)
        fcb = sm(2, FC)
        gi = sb("gi", [128, 8], U32)
        Gd = sb("Gd", [16, EXPERTS, IMAGES])
        Gb = sb("Gb", [128, EXPERTS, IMAGES])
        used = sm(EXPERTS)
        used_bits = sb("used_bits", [1, 1], I32)
        pr = sb("pr", [128, T, EXPERTS])
        v8 = sb("v8", [128, T, 8])
        i8 = sb("i8", [128, T, 8], U32)
        i8f = sb("i8f", [128, T, 8])
        m12 = sb("m12", [128, 2, T, EXPERTS])
        rank = sb("rank", [128, 2, T, EXPERTS])
        gse = sb("gse", [128, T, EXPERTS])

        patT = P[:, 0:PK * T * 128].rearrange("p (k n) -> p k n", k=PK)
        BD = P[:, 0:MATS * 32].rearrange("p (m c) -> p m c", m=MATS)
        S2 = P[:, 0:T * 8 * TOKENS].rearrange("p (t n) -> p t n", t=T)
        attnT = P[:, 2368:2368 + T * 512].rearrange("p (t n) -> p t n", t=T)
        BD2 = P[:, 0:32 * 32].rearrange("p (m c) -> p m c", m=32)
        oS = P[:, 3072:3072 + 32 * TOKENS].rearrange("p (m n) -> p m n", m=32)
        O = P[:, 4256:4256 + T * DIM].rearrange("p (t d) -> p t d", t=T)
        hT = [P[:, b * FC * ALLC:(b + 1) * FC * ALLC].rearrange("p (f n) -> p f n", f=FC) for b in range(2)]
        A = Q[:, 0:T * 2 * DIM].rearrange("p (t n) -> p t n", t=T)
        Gs = Q[:, 3072:5120].rearrange("p (m n) -> p m n", m=MATS)
        E = Q[:, 5120:6656].rearrange("p (a r c) -> p a r c", a=3, r=16)
        Ef = Q[:, 5120:6656].rearrange("p (a n) -> p a n", a=3)
        Tm = Q[:, 6656:7424].rearrange("p (a r c) -> p a r c", a=3, r=16)
        Pb = Q[:, 7424:8192]
        Pu = P[:, 0:768]
        Qblk = Q[:, :].rearrange("p (a m c x) -> p a m c x", a=2, m=16, c=CH)
        vT = Q[:, 3072:4256].rearrange("p (m n) -> p m n", m=32)
        Wm = Q[:, 4256:5280].rearrange("p (m n) -> p m n", m=32)
        qT2 = vT
        Aabs = Q[:, 4256:4256 + T * DIM].rearrange("p (t n) -> p t n", t=T)
        kvs = Q[:, 5792:6816].rearrange("p (m n) -> p m n", m=32)
        GE = EXPERTS * CAP
        disp = Q[:, 0:T * GE].rearrange("p (g e c) -> p g e c", g=T, e=EXPERTS)
        comb = Q[:, T * GE:2 * T * GE].rearrange("p (g e c) -> p g e c", g=T, e=EXPERTS)
        xinT = Q[:, 2 * T * GE:4 * T * GE].rearrange("p (k e s) -> p k e s", k=KC, e=EXPERTS)
        combT = Q[:, 4 * T * GE:4 * T * GE + 2048].rearrange("p (g a n) -> p g a n", g=T, a=2)
        BLK = M[:, 0:16 * C].rearrange("p (j c) -> p j c", j=16)
        Mx = M[:, :].rearrange("p (t c a n) -> p t c a n", t=T, c=CH, a=2)
        yT = M[:, 0:2 * T * GE].rearrange("p (k g e c) -> p k g e c", k=KC, g=T, e=EXPERTS)
        hT1 = [P[:, b * FC * SLOTS:(b + 1) * FC * SLOTS].rearrange("p (f n) -> p f n", f=FC) for b in range(2)]
        yG = P[:, 2300:2300 + T * 2 * DIM].rearrange("p (g a n) -> p g a n", g=T, a=2)
        fcball = col[:, Q_FCB:Q_FCB + FC * EXPERTS].rearrange("p (e f) -> p e f", f=FC)
        ident = con[:, K_ID:K_ID + 128]
        id96 = con[0:C, K_ID:K_ID + C]
        idpar = con[0:C, K_ID:K_ID + C].rearrange("p (a x) -> p a x", a=PAIRS)
        parity = [con[0:C, K_PAIR + HD * i:K_PAIR + HD * i + 1] for i in range(2)]
        head = [con[0:C, K_HEAD + i:K_HEAD + i + 1] for i in range(HC)]
        eye = con[:, K_EYE:K_EYE + 256].rearrange("p (r c) -> p r c", r=16)
        XTi = XT[0:C, :, :].rearrange("p k (t a n) -> p k t a n", a=2, n=HALF)

        def cq(i, p=C, n=1):
            return col[0:p, i:i + n]

        def qb_out(a, hd):
            return Qblk[0:C, a, :, :, :].rearrange("p m c x -> p (m c) x")[:, :, hd * NCH:(hd + 1) * NCH]

        def qb_in(a):
            return qt[0:C, a * 32:a * 32 + 16, :].rearrange("p m (c n) -> p (m c) n", c=CH)

        s_const, s_pat, s_tokw, s_bias, s_attw, s_ffnw, s_l1w = [
            sem(n) for n in ("s_const", "s_pat", "s_tokw", "s_bias", "s_attw", "s_ffnw", "s_l1w")]
        s_w = [sem("s_w0"), sem("s_w1")]
        s_v = [sem("s_v0"), sem("s_v1")]
        s_patk = [sem(f"s_patk{k}") for k in range(PK)]
        dchain, achain, pchain = sem("dchain"), sem("achain"), sem("pchain")
        s_zero = sem("s_zero")
        s_emb = sem("s_emb")
        s_hcopy = sem("s_hcopy")
        s_var, s_sd, s_xn = sem("s_var"), sem("s_sd"), sem("s_xn")
        s_xtp, s_xt = sem("s_xtp"), sem("s_xt")
        s_hb = sem("s_hb")
        s_tok, s_tokv = sem("s_tok"), sem("s_tokv")
        s_chan, s_chanv = sem("s_chan"), sem("s_chanv")
        s_gram, s_gramv = sem("s_gram"), sem("s_gramv")
        s_et, s_etv, s_tv = sem("s_et"), sem("s_etv"), sem("s_tv")
        s_piv, s_sq, s_blk = sem("s_piv"), sem("s_sq"), sem("s_blk")
        s_back, s_bda, s_bdv = sem("s_back"), sem("s_bda"), sem("s_bdv")
        s_qt, s_qte = sem("s_qt"), sem("s_qte")
        s_qba, s_qbv, s_qbp = sem("s_qba"), sem("s_qbv"), sem("s_qbp")
        s_mixw, s_mixr, s_mix1 = sem("s_mixw"), sem("s_mixr"), sem("s_mix1")
        s_dots, s_s2, s_mixp, s_mixe = sem("s_dots"), sem("s_s2"), sem("s_mixp"), sem("s_mixe")
        s_sub, s_exp, s_att = sem("s_sub"), sem("s_exp"), sem("s_att")
        s_atp, s_atT = sem("s_atp"), sem("s_atT")
        s_av, s_oT = sem("s_av"), sem("s_oT")
        s_prj, s_h = sem("s_prj"), sem("s_h")
        s_w_ps, s_wsub, s_wexp, s_wT = sem("s_w_ps"), sem("s_wsub"), sem("s_wexp"), sem("s_wT")
        s_wv, s_os, s_scr, s_scr2 = sem("s_wv"), sem("s_os"), sem("s_scr"), sem("s_scr2")
        s_otp, s_ot = sem("s_otp"), sem("s_ot")
        s_zb = sem("s_zb")
        s_w2p, s_s = sem("s_w2p"), sem("s_s")
        s_gst, s_gps, s_gva, s_gsd, s_gsc = sem("s_gst"), sem("s_gps"), sem("s_gva"), sem("s_gsd"), sem("s_gsc")
        s_x1p, s_x1 = sem("s_x1p"), sem("s_x1")
        s_xbar, s_rps, s_nm, s_ge, s_gd, s_gbp, s_gb = [
            sem(n) for n in ("s_xbar", "s_rps", "s_nm", "s_ge", "s_gd", "s_gbp", "s_gb")]
        s_fcb, s_hp, s_gelu, s_ytmp, s_acc, s_edone = [
            sem(n) for n in ("s_fcb", "s_hp", "s_gelu", "s_ytmp", "s_acc", "s_edone")]
        s_used = sem("s_used")
        s_x2, s_x2p = sem("s_x2"), sem("s_x2p")
        s_q2, s_q2e, s_kv2, s_kv2e = sem("s_q2"), sem("s_q2e"), sem("s_kv2"), sem("s_kv2e")
        s_kvp, s_kvm, s_bd3, s_o2, s_o2e = sem("s_kvp"), sem("s_kvm"), sem("s_bd3"), sem("s_o2"), sem("s_o2e")
        s_lg, s_lsub, s_lexp, s_m12, s_rk = [sem(n) for n in ("s_lg", "s_lsub", "s_lexp", "s_m12", "s_rk")]
        s_disp, s_comb, s_xip, s_xin, s_ctp, s_ct = [
            sem(n) for n in ("s_disp", "s_comb", "s_xip", "s_xin", "s_ctp", "s_ct")]
        s_h1p, s_relu, s_y1p, s_y1 = sem("s_h1p"), sem("s_relu"), sem("s_y1p"), sem("s_y1")
        s_ygp, s_yg, s_fin, s_res, s_out = [sem(n) for n in ("s_ygp", "s_yg", "s_fin", "s_res", "s_out")]

        def is_used(bits, expert):
            return ((bits >> expert) & 1) != 0

        block = ctx.enter_context(nc.Block())

        @block.sync
        def _(sp):
            sp.dma_start(tokw[:, :, :], tok_w[:, :, :]).then_inc(s_tokw, 16)
            for k in range(PK):
                sp.dma_start(patT[:, k, :], patches[:, k, :]).then_inc(s_patk[k], 16)
            sp.dma_start(con[:, :], consts[:, :]).then_inc(s_const, 16)
            sp.dma_start(cb2[:, :], cls_b[:, :]).then_inc(s_const, 16)
            sp.dma_start(col[:, :], cols[:, :]).then_inc(s_bias, 16)
            sp.dma_start(row[:, :], rows.partition_broadcast(128)).then_inc(s_bias, 16)
            sp.dma_start(qkvw[0:C, :, :], qkv_w[:, :, :]).then_inc(s_attw, 16)
            sp.dma_start(projw[0:C, :, :], proj_w[:, :, :]).then_inc(s_attw, 16)
            sp.dma_start(w1w[0:C, :, :], w1[:, :, :]).then_inc(s_ffnw, 16)
            sp.dma_start(w2w[0:C, :, :], w2[:, :, :]).then_inc(s_ffnw, 16)
            sp.dma_start(rw[0:C, :, :], r_w[:, :, :]).then_inc(s_ffnw, 16)
            for b in range(2):
                sp.dma_start(wi_sb[0:C, b, :], fc_w[b, :, :]).then_inc(s_w[b], 16)
                sp.dma_start(wo_sb[:, b, :], pr_w[b, :, :]).then_inc(s_v[b], 16)
            sp.dma_start(qkv2w[0:C, :, :], qkv2_w[:, :, :]).then_inc(s_l1w, 16)
            sp.dma_start(proj2w[0:C, :, :], proj2_w[:, :, :]).then_inc(s_l1w, 16)
            sp.dma_start(routw[0:C, :, :], router_w[:, :, :]).then_inc(s_l1w, 16)

            for i in range(4):
                a, kc = divmod(i, 2)
                sp.wait_ge(s_os, i + 1)
                sp.dma_start(scratch[:, a, kc].rearrange("t p n -> p t n"),
                             oS[0:C, i * 8:(i + 1) * 8, :]).then_inc(s_scr, 16)
            sp.wait_ge(s_scr, 64)
            sp.wait_ge(s_zero, 6)
            back = scratch.rearrange("t a k p n -> t a (k p n)").rearrange("t a (m d) -> a m t d", d=DIM)
            for a in range(2):
                sp.dma_start(O[a * HALF:a * HALF + 36, :, :], back[a, 0:36]).then_inc(s_scr2, 16)
                sp.dma_start(O[a * HALF + 36:a * HALF + 37, :, :], back[a, 36:37]).then_inc(s_scr2, 16)

            for b in range(2):
                sp.wait_ge(s_w[b], 16)
                sp.wait_ge(s_v[b], 16)
            sp.wait_ge(s_used, 1)
            bits = sp.value_load(used_bits[0:1, 0:1], min_val=0, max_val=255)
            with sp.Fori(1, EXPERTS // 2) as it:
                for b in range(2):
                    with sp.If(is_used(bits, it * 2 + b)):
                        sp.wait_ge(s_edone, it * 2 + (b - 1))
                        sp.dma_start(wi_sb[0:C, b, :], fc_w[it * 2 + b, :, :]).then_inc(s_w[b], 16)
                        sp.dma_start(wo_sb[:, b, :], pr_w[it * 2 + b, :, :]).then_inc(s_v[b], 16)
                    with sp.Else():
                        sp.wait_ge(s_edone, it * 2 + (b - 1))
                        sp.sem_inc(s_w[b], 16)
                        sp.sem_inc(s_v[b], 16)
            with sp.Fori(0, EXPERTS // 2) as it:
                for b in range(2):
                    sp.wait_ge(s_edone, it * 2 + (EXPERTS + b - 1))
                    sp.dma_start(wi_sb[0:C, b, :], wi[it * 2 + b, :, :]).then_inc(s_w[b], 16)
                    sp.dma_start(wo_sb[:, b, :], wo[it * 2 + b, :, :]).then_inc(s_v[b], 16)

            for t in range(T):
                sp.wait_ge(s_res, t + 1)
                for a in range(2):
                    sp.dma_start(out[2 * t + a, :, :], h[a * HALF:a * HALF + TOKENS, t, :]).then_inc(s_out, 16)
            sp.wait_ge(s_out, 16 * IMAGES)

        @block.gpsimd
        def _(po):
            n = [0]

            def link(ins):
                n[0] += 1
                ins.then_inc(pchain, 1)
                po.wait_ge(pchain, n[0])

            po.memset(eps, 1e-5)
            po.memset(eps12, 1e-12).then_inc(s_zero, 1)
            po.memset(vpad[:, :, :], 0.0).then_inc(s_zero, 1)
            po.memset(qkT[:, :, :], 0.0).then_inc(s_zero, 1)
            po.memset(mixT[:, :, :], 0.0).then_inc(s_zero, 1)
            po.memset(BLK, 0.0).then_inc(s_zero, 1)
            po.wait_ge(s_const, 32)
            for a in range(3):
                last = po.tensor_copy(E[:, a, :, 16:32], eye)
            last.then_inc(s_etv, 1)
            po.wait_ge(s_bias, 32)
            po.wait_ge(s_xn, T)
            po.tensor_tensor(h[:, :, :], h[:, :, :], bc(row[:, R_PROJB:R_PROJB + DIM], 1, T), ALU.add).then_inc(s_hb, 1)
            po.wait_ge(s_back, 1)
            po.memset(Qblk[0:C, :, :, :, 60:64].rearrange("p a m c x -> p (a m c) x"), 0.0).then_inc(s_qbp, 1)
            po.memset(M[:, :].rearrange("p (x n) -> p x n", n=64)[:, :, 37:64], 0.0).then_inc(s_qbp, 1)
            po.wait_ge(s_av, 2)
            po.memset(O, 0.0).then_inc(s_zero, 1)
            po.wait_ge(s_xt, 8)
            po.tensor_tensor(xn[:, :, :], xn[:, :, :], bc(row[:, R_W2B:R_W2B + DIM], 1, T), ALU.add).then_inc(s_zb, 1)
            po.wait_ge(s_xn, 3 * T)
            po.tensor_tensor(h[:, :, :], h[:, :, :], bc(row[:, R_BP:R_BP + DIM], 1, T), ALU.add).then_inc(s_hb, 1)

        @block.tensor
        def _(pe):
            def transposes(r, tiles=range(T)):
                for t in tiles:
                    pe.wait_ge(s_xn, r * T + t + 1)
                    for kc in range(KC):
                        last = pe.transpose(PS[0:C, 4 + t // 2, kc * 256 + (t % 2) * 128:kc * 256 + (t % 2) * 128 + 128],
                                            xn[:, t, kc * C:(kc + 1) * C], ident)
                    if t % 2:
                        last.then_inc(s_xtp, 1)

            def projection(ready, per_half, w, base):
                for t in range(T):
                    if t % 4 == 0:
                        pe.wait_ge(ready, per_half * (t // 4 + 1))
                    if t >= 4:
                        pe.wait_ge(s_h, base + t - 3)
                    for kc in range(KC):
                        last = pe.matmul(PS[:, t % 4, 0:DIM], XT[0:C, kc, t * 128:(t + 1) * 128], w[0:C, kc, :],
                                         start=(kc == 0), stop=(kc == 1))
                    last.then_inc(s_prj, 1)

            pe.wait_ge(s_tokw, 16)
            for k in range(PK):
                pe.wait_ge(s_patk[k], 16)
                for t in range(T):
                    pe.matmul(PS[:, t, 0:DIM], patT[:, k, t * 128:(t + 1) * 128], tokw[:, k, :],
                              start=(k == 0), stop=False)
            pe.wait_ge(s_const, 32)
            for t in range(T):
                pe.matmul(PS[:, t, 0:DIM], con[0:2, K_IND:K_IND + 128], cb2[:, :], start=False,
                          stop=True).then_inc(s_emb, 1)
            pe.wait_ge(s_hcopy, T)
            pe.wait_ge(s_var, 1)
            transposes(0)
            pe.wait_ge(s_mixw, 1)
            pe.matmul(PS[:, 3, 0:HEADS], con[0:HEADS, K_E1:K_E1 + 128], wpT[0:HEADS, :], start=True, stop=True)
            pe.matmul(PS[:, 3, HEADS:HEADS + 1], con[0:HEADS, K_E1:K_E1 + 128], col[0:HEADS, Q_CB:Q_CB + 1],
                      start=True, stop=True).then_inc(s_mixr, 1)
            pe.wait_ge(s_attw, 32)
            pe.wait_ge(s_xt, 4)
            pe.wait_ge(s_mix1, 1)

            for t in range(T + 1):
                if t < T:
                    pe.wait_ge(s_xt, t // 2 + 1)
                    if t >= 2:
                        pe.wait_ge(s_tokv, t - 1)
                    for kc in range(KC):
                        pe.matmul(PS[:, t % 2, 0:2 * DIM], XT[0:C, kc, t * 128:(t + 1) * 128],
                                  qkvw[0:C, kc, 0:2 * DIM], start=(kc == 0), stop=(kc == 1))
                    for kc in range(KC):
                        last = pe.matmul(PS[:, 2 + t % 2, 0:DIM], XT[0:C, kc, t * 128:(t + 1) * 128],
                                         qkvw[0:C, kc, 2 * DIM:3 * DIM], start=(kc == 0), stop=(kc == 1))
                    last.then_inc(s_tok, 1)
                if t >= 1:
                    u = t - 1
                    pe.wait_ge(s_tokv, u + 1)
                    if u < 4:
                        pe.wait_ge(s_xt, u + 1)
                    else:
                        pe.wait_ge(s_chanv, u - 3)
                    for i in range(4):
                        last = pe.transpose(PS[0:C, 4 + u % 4, i * 128:(i + 1) * 128], A[:, u, i * C:(i + 1) * C], ident)
                    last.then_inc(s_chan, 1)
            pe.wait_ge(s_chanv, T)
            for a in range(2):
                for qk in range(2):
                    s = a * 2 + qk
                    for kc in range(KC):
                        for t in range(T):
                            for j in range(PAIRS):
                                v = A[a * HALF:a * HALF + TOKENS, t, (qk * 2 + kc) * C + 32 * j:(qk * 2 + kc) * C + 32 * j + 32]
                                last = pe.matmul(PS[32 * j:32 * j + 32, s, (kc * 8 + t) * 32:(kc * 8 + t) * 32 + 32],
                                                 v, v, start=True, stop=True)
                    last.then_inc(s_gram, 1)
            pe.wait_ge(s_gramv, 4)
            for r in range(16):
                for par in range(2):
                    last = pe.matmul(PS[par * 64:par * 64 + 64, 6 + r // 8, (r % 8) * 48:(r % 8) * 48 + 48],
                                     Gs[0:C, :, par * 16 + r], idpar[:, :, par * 16:par * 16 + 16],
                                     start=True, stop=True)
                if r % 8 == 7:
                    last.then_inc(s_et, 1)
            for r in range(16):
                for par in range(2):
                    last = pe.matmul(PS[par * 64:par * 64 + 64, 4 + r // 8, (r % 8) * 48:(r % 8) * 48 + 48],
                                     qkT[0:C, :, r], idpar[:, :, par * 16:par * 16 + 16], start=True, stop=True)
                if r % 8 == 7:
                    last.then_inc(s_et, 1)
            pe.wait_ge(s_blk, 1)
            for j in range(16):
                for p in range(PAIRS):
                    last = pe.matmul(PS[32 * p:32 * p + 32, j // 8, (j % 8) * 64:(j % 8) * 64 + 64],
                                     BLK[:, j, 32 * p:32 * p + 32], con[:, K_II:K_II + 64], start=True, stop=True)
            last.then_inc(s_back, 1)
            pe.wait_ge(s_bda, 1)
            pe.wait_ge(s_bdv, 1)
            for b in range(8):
                for i in range(8):
                    m = b * 8 + i
                    for p in range(PAIRS):
                        last = pe.matmul(PS[32 * p:32 * p + 32, b, i * NP:(i + 1) * NP],
                                         BD[32 * p:32 * p + 32, m, :], qkT[32 * p:32 * p + 32, m, :], start=True, stop=True)
                last.then_inc(s_qt, 1)
            pe.wait_ge(s_qte, 8)
            pe.wait_ge(s_qba, 1)
            pe.wait_ge(s_qbv, 1)
            pe.wait_ge(s_qbp, 2)
            for t in range(T + 1):
                if t < T:
                    if t >= 4:
                        pe.wait_ge(s_mixe, t - 3)
                    for c in range(CH):
                        for a in range(2):
                            for kc in range(KC):
                                last = pe.matmul(
                                    PS[kc * 64:kc * 64 + 64, t % 4, (c * 2 + a) * TOKENS:(c * 2 + a + 1) * TOKENS],
                                    Qblk[0:C, a, kc * 8 + t, c, :], qt[0:C, a * 32 + 16 + kc * 8 + t, 0:TOKENS],
                                    start=True, stop=True)
                    last.then_inc(s_dots, 1)
                if t >= 1:
                    pe.wait_ge(s_s2, t)
                    pe.matmul(PS[:, (t - 1) % 4, 0:8 * TOKENS], mixT[:, :, :].rearrange("p k x -> p (k x)"),
                              S2[:, t - 1, :], start=True, stop=True).then_inc(s_mixp, 1)
            for t in range(T + 1):
                if t < T:
                    pe.wait_ge(s_att, t // 2 + 1)
                    if t >= 2:
                        pe.wait_ge(s_atT, t - 1)
                    for c in range(CH):
                        last = pe.transpose(PS[:, 4 + t % 2, c * 128:(c + 1) * 128],
                                            Mx[:, t, c].rearrange("p a n -> p (a n)"), ident)
                    last.then_inc(s_atp, 1)
                if t >= 1:
                    u = t - 1
                    pe.wait_ge(s_atT, u + 1)
                    if u == 4:
                        pe.wait_ge(s_oT, 2)
                    rhs = attnT[:, u, :].rearrange("p (c x) -> p c x", c=CH)
                    for kc in range(KC):
                        for par in range(2):
                            for j in range(PAIRS):
                                for a in range(2):
                                    c0 = (kc * PAIRS + j) * 64 + par * 16
                                    r0 = kc * 64 + (2 * j + par) * NCH
                                    o0 = (kc * 4 + u % 4) * NP
                                    last = pe.matmul(PS[32 * j:32 * j + 32, 6 + a, o0:o0 + NP],
                                                     vpad[a * HALF:a * HALF + TOKENS, u, c0:c0 + 32],
                                                     rhs[a * HALF:a * HALF + TOKENS, :, r0:r0 + NCH],
                                                     start=(par == 0), stop=(par == 1))
                    if u % 4 == 3:
                        last.then_inc(s_av, 1)
            projection(s_oT, 2, projw, 0)

            transposes(1)
            pe.wait_ge(s_ffnw, 48)
            pe.wait_ge(s_h, T)
            for t in range(T):
                pe.wait_ge(s_xt, 4 + t // 2 + 1)
                if t >= 4:
                    pe.wait_ge(s_tokv, T + t - 3)
                for kc in range(KC):
                    last = pe.matmul(PS[:, t % 4, 0:2 * DIM], XT[0:C, kc, t * 128:(t + 1) * 128],
                                     w1w[0:C, kc, 0:2 * DIM], start=(kc == 0), stop=(kc == 1))
                last.then_inc(s_tok, 1)
            for i in range(4):
                a, kc = divmod(i, 2)
                for k in range(KC):
                    last = pe.matmul(PS[0:C, 4 + i, 0:COLS], w1w[0:C, k, 2 * DIM + kc * C:2 * DIM + (kc + 1) * C],
                                     XTi[:, k, :, a, 0:TOKENS], start=(k == 0), stop=(k == 1))
                last.then_inc(s_chan, 1)
            pe.wait_ge(s_tokv, 2 * T)
            for a in range(2):
                for kc in range(KC):
                    for t in range(T):
                        for j in range(PAIRS):
                            q0 = kc * C + 32 * j
                            last = pe.matmul(PS[32 * j:32 * j + 32, a, (kc * 8 + t) * 32:(kc * 8 + t) * 32 + 32],
                                             A[a * HALF:a * HALF + TOKENS, t, q0:q0 + 32],
                                             A[a * HALF:a * HALF + TOKENS, t, DIM + q0:DIM + q0 + 32],
                                             start=True, stop=True)
                last.then_inc(s_w_ps, 1)
            pe.wait_ge(s_chanv, 12)
            for b in range(4):
                pe.wait_ge(s_wT, b // 2 + 1)
                for i in range(8):
                    m = b * 8 + i
                    for p in range(PAIRS):
                        last = pe.matmul(PS[32 * p:32 * p + 32, 2 + b, i * TOKENS:(i + 1) * TOKENS],
                                         BD2[32 * p:32 * p + 32, m, :], vT[32 * p:32 * p + 32, m, :], start=True, stop=True)
                last.then_inc(s_wv, 1)
            pe.wait_ge(s_scr2, 64)
            for t in range(T):
                for kc in range(KC):
                    last = pe.transpose(PS[0:C, 4 + t // 2, kc * 256 + (t % 2) * 128:kc * 256 + (t % 2) * 128 + 128],
                                        O[:, t, kc * C:(kc + 1) * C], ident)
                if t % 2:
                    last.then_inc(s_xtp, 1)
            for t in range(T):
                pe.wait_ge(s_xt, 8 + t // 2 + 1)
                if t >= 4:
                    pe.wait_ge(s_s, t - 3)
                for kc in range(KC):
                    last = pe.matmul(PS[:, t % 4, 0:DIM], XT[0:C, kc, t * 128:(t + 1) * 128], w2w[0:C, kc, :],
                                     start=(kc == 0), stop=(kc == 1))
                last.then_inc(s_w2p, 1)
            pe.wait_ge(s_xt, 12)
            for t in range(T):
                pe.wait_ge(s_s, t + 1)
                for kc in range(KC):
                    last = pe.transpose(PS[0:C, 4 + t // 2, kc * 256 + (t % 2) * 128:kc * 256 + (t % 2) * 128 + 128],
                                        xn[:, t, kc * C:(kc + 1) * C], ident)
            last.then_inc(s_x1p, 1)
            pe.wait_ge(s_gst, 1)
            pe.matmul(PS[:, 0, 0:2], con[:, K_VALID:K_VALID + 128], gst, start=True, stop=True).then_inc(s_gps, 1)
            pe.wait_ge(s_xbar, 1)
            for kc in range(KC):
                last = pe.matmul(PS[0:IMAGES, 1, 0:EXPERTS], xbar[0:C, kc, :], rw[0:C, kc, :],
                                 start=(kc == 0), stop=(kc == 1))
            last.then_inc(s_rps, 1)
            pe.wait_ge(s_gd, 1)
            pe.matmul(PS[0:C, 2, 0:128], con[0:IMAGES, K_ONE:K_ONE + C], Gd[:, :, :].rearrange("p e b -> p (e b)"),
                      start=True, stop=True).then_inc(s_gbp, 1)
            pe.wait_ge(s_gb, 1)

            pe.wait_ge(s_used, 1)
            bits = pe.value_load(used_bits[0:1, 0:1], min_val=0, max_val=255)
            with pe.Fori(0, EXPERTS // 2) as it:
                for b in range(2):
                    with pe.If(is_used(bits, it * 2 + b)):
                        pe.wait_ge(s_w[b], it * 16 + 16)
                        for i in range(2 * FC):
                            f, nh = divmod(i, 2)
                            if i >= 4:
                                pe.wait_ge(s_gelu, it * 24 + (b * 12 + i - 3))
                            for kc in range(KC):
                                last = pe.matmul(PS[:, i % 4, 0:COLS],
                                                 wi_sb[0:C, b, kc * FF + f * 128:kc * FF + (f + 1) * 128],
                                                 x1T[0:C, kc, nh * COLS:(nh + 1) * COLS], start=(kc == 0), stop=(kc == 1))
                            last.then_inc(s_hp, 1)
                        pe.wait_ge(s_v[b], it * 16 + 16)
                        pe.wait_ge(s_acc, it * 8 + (4 * b + 1))
                        for f in range(FC):
                            pe.wait_ge(s_gelu, it * 24 + (b * 12 + 2 * f + 2))
                            for kc in range(KC):
                                for nh in range(2):
                                    last = pe.matmul(PS[0:C, 4 + kc * 2 + nh, 0:COLS],
                                                     wo_sb[:, b, f * DIM + kc * C:f * DIM + (kc + 1) * C],
                                                     hT[b][:, f, nh * COLS:(nh + 1) * COLS],
                                                     start=(f == 0), stop=(f == FC - 1))
                        last.then_inc(s_edone, 1)
                    with pe.Else():
                        pe.drain().then_inc(s_hp, 2 * FC)
                        pe.drain().then_inc(s_edone, 1)

            pe.wait_ge(s_gst, 2)
            pe.matmul(PS[:, 0, 0:2], con[0:C, K_ONE:K_ONE + 128], gst[0:C], start=True, stop=True).then_inc(s_gps, 1)
            pe.wait_ge(s_x2, 2)
            for t in range(T):
                if t >= 4:
                    pe.wait_ge(s_h, T + t - 3)
                for kc in range(KC):
                    last = pe.matmul(PS[:, t % 4, kc * C:(kc + 1) * C], XT[0:C, kc, t * 128:(t + 1) * 128], id96,
                                     start=True, stop=True, is_transpose=True)
                last.then_inc(s_x2p, 1)

            transposes(2)
            pe.wait_ge(s_l1w, 48)
            pe.wait_ge(s_xt, 16)
            for i in range(4):
                a, kc = divmod(i, 2)
                for k in range(KC):
                    last = pe.matmul(PS[0:C, 4 + i, 0:COLS], qkv2w[0:C, k, kc * C:(kc + 1) * C],
                                     XTi[:, k, :, a, 0:TOKENS], start=(k == 0), stop=(k == 1))
                last.then_inc(s_q2, 1)
            for t in range(T):
                if t >= 4:
                    pe.wait_ge(s_kv2e, t - 3)
                    pe.wait_ge(s_kv2, t)
                for kc in range(KC):
                    last = pe.matmul(PS[:, t % 4, 0:2 * DIM], XT[0:C, kc, t * 128:(t + 1) * 128],
                                     qkv2w[0:C, kc, DIM:3 * DIM], start=(kc == 0), stop=(kc == 1))
                last.then_inc(s_kv2, 1)
            pe.wait_ge(s_kv2e, T)
            for kc in range(KC):
                for t in range(T):
                    last = pe.matmul(PS[0:C, 2, (kc * 8 + t) * 2:(kc * 8 + t) * 2 + 2],
                                     Aabs[:, t, kc * C:(kc + 1) * C], con[:, K_HALF:K_HALF + 2], start=True, stop=True)
            last.then_inc(s_kvp, 1)
            for a in range(2):
                for kc in range(KC):
                    for t in range(T):
                        for j in range(PAIRS):
                            k0 = kc * C + 32 * j
                            last = pe.matmul(PS[32 * j:32 * j + 32, a, (kc * 8 + t) * 32:(kc * 8 + t) * 32 + 32],
                                             A[a * HALF:a * HALF + TOKENS, t, k0:k0 + 32],
                                             A[a * HALF:a * HALF + TOKENS, t, DIM + k0:DIM + k0 + 32],
                                             start=True, stop=True)
                last.then_inc(s_kvm, 1)
            pe.wait_ge(s_q2e, 4)
            for b in range(4):
                pe.wait_ge(s_bd3, b // 2 + 1)
                for i in range(8):
                    m = b * 8 + i
                    for p in range(PAIRS):
                        last = pe.matmul(PS[32 * p:32 * p + 32, 4 + b, i * TOKENS:(i + 1) * TOKENS],
                                         BD2[32 * p:32 * p + 32, m, :], qT2[32 * p:32 * p + 32, m, :], start=True, stop=True)
                last.then_inc(s_o2, 1)
            pe.wait_ge(s_o2e, 4)
            projection(s_o2e, 2, proj2w, 2 * T)

            transposes(3, range(4))
            for t in range(T):
                if t == 4:
                    transposes(3, range(4, T))
                if t == 0:
                    pe.wait_ge(s_h, 2 * T + 5)
                pe.wait_ge(s_xt, 16 + t // 2 + 1)
                for kc in range(KC):
                    last = pe.matmul(PS[:, 0, t * 8:t * 8 + 8], XT[0:C, kc, t * 128:(t + 1) * 128], routw[0:C, kc, :],
                                     start=(kc == 0), stop=(kc == 1))
            last.then_inc(s_lg, 1)
            pe.wait_ge(s_m12, 1)
            f1 = m12[:, 0].rearrange("p g e -> p (g e)")
            f2 = m12[:, 1].rearrange("p g e -> p (g e)")
            pe.matmul(PS[:, 5, 0:64], con[:, K_TRI:K_TRI + 128], f1, start=True, stop=True)
            pe.matmul(PS[:, 5, 64:128], con[:, K_ONE:K_ONE + 128], f1, start=True, stop=False)
            pe.matmul(PS[:, 5, 64:128], con[:, K_TRI:K_TRI + 128], f2, start=False, stop=True).then_inc(s_rk, 1)
            pe.wait_ge(s_disp, 1)
            for g in range(T):
                for kc in range(KC):
                    last = pe.matmul(PS[0:C, g, kc * GE:(kc + 1) * GE], xn[:, g, kc * C:(kc + 1) * C],
                                     disp[:, g].rearrange("p e c -> p (e c)"), start=True, stop=True)
                last.then_inc(s_xip, 1)
            pe.wait_ge(s_comb, 1)
            for b in range(4):
                pe.wait_ge(s_xin, b + 1)
                for i in range(4):
                    g, hf = 2 * b + i // 2, i % 2
                    src = comb[:, g].rearrange("p e c -> p (e c)")[:, hf * 92:(hf + 1) * 92]
                    last = pe.transpose(PS[0:92, b, i * 128:(i + 1) * 128], src, ident)
                last.then_inc(s_ctp, 1)
            pe.wait_ge(s_ct, 4)
            pe.wait_ge(s_xin, 8)
            with pe.Fori(0, EXPERTS // 2) as it:
                for b in range(2):
                    pe.wait_ge(s_w[b], it * 16 + 80)
                    for i in range(3):
                        for u in range(2):
                            f = 2 * i + u
                            for kc in range(KC):
                                last = pe.matmul(PS[:, 3 * b + i, u * SLOTS:(u + 1) * SLOTS],
                                                 wi_sb[0:C, b, kc * FF + f * 128:kc * FF + (f + 1) * 128],
                                                 xinT[0:C, kc, it * 2 + b, :], start=(kc == 0), stop=(kc == 1))
                        last.then_inc(s_h1p, 1)
                    pe.wait_ge(s_v[b], it * 16 + 80)
                    pe.wait_ge(s_y1, it * 2 + (b + 1))
                    for kc in range(KC):
                        for f in range(FC):
                            if kc == 0 and f % 2 == 0:
                                pe.wait_ge(s_relu, it * 6 + (3 * b + f // 2 + 1))
                            last = pe.matmul(PS[0:C, 6 + b, kc * SLOTS:(kc + 1) * SLOTS],
                                             wo_sb[:, b, f * DIM + kc * C:f * DIM + (kc + 1) * C],
                                             hT1[b][:, f, :], start=(f == 0), stop=(f == FC - 1))
                    last.then_inc(s_edone, 1)
            pe.wait_ge(s_y1, EXPERTS + 2)
            for g in range(T):
                for hf in range(2):
                    for kc in range(KC):
                        src = yT[0:C, kc, g].rearrange("p e c -> p (e c)")[:, hf * 92:(hf + 1) * 92]
                        last = pe.matmul(PS[0:92, g, hf * DIM + kc * C:hf * DIM + (kc + 1) * C], src, id96,
                                         start=True, stop=True, is_transpose=True)
                last.then_inc(s_ygp, 1)
            for g in range(T):
                pe.wait_ge(s_yg, g + 1)
                for hf in range(2):
                    last = pe.matmul(PS[:, g, 0:DIM], combT[0:92, g, hf, :], yG[0:92, g, hf, :],
                                     start=(hf == 0), stop=(hf == 1))
                last.then_inc(s_fin, 1)

        @block.scalar
        def _(ac):
            n = [0]

            def link(ins):
                n[0] += 1
                ins.then_inc(achain, 1)
                ac.wait_ge(achain, n[0])

            def evac_xt(r, banks):
                for b in banks:
                    ac.wait_ge(s_xtp, r * 4 + b + 1)
                    ac.activation(XT[0:C, :, b * 256:(b + 1) * 256],
                                  PS[0:C, 4 + b, :].rearrange("p (k x) -> p k x", k=KC), ACT.Copy).then_inc(s_xt, 1)

            def sqrt_ln(r):
                for hf in range(2):
                    ac.wait_ge(s_var, 2 * r + hf + 1)
                    ac.activation(sd[:, 4 * hf:4 * hf + 4], mv[:, 4 * hf:4 * hf + 4, 1], ACT.Sqrt, bias=eps)\
                      .then_inc(s_sd, 1)

            def preload(func):
                ac.activation(dummy, eps, func)

            ac.wait_ge(s_zero, 4)
            preload(ACT.Sqrt)
            for t in range(T):
                ac.wait_ge(s_emb, t + 1)
                ac.activation(h[:, t, :], PS[:, t, 0:DIM], ACT.Copy).then_inc(s_hcopy, 1)
            sqrt_ln(0)
            evac_xt(0, range(4))
            qkm = qkT[0:C, :, :].rearrange("p (a x t) n -> p a x t n", a=2, t=T)
            for t in range(T):
                ac.wait_ge(s_chan, t + 1)
                src = PS[0:C, 4 + t % 4, :].rearrange("p (x a n) -> p a x n", a=2, n=HALF)
                for a in range(2):
                    last = ac.activation(qkm[:, a, :, t, 0:TOKENS], src[:, a, :, 0:TOKENS], ACT.Copy)
                last.then_inc(s_chanv, 1)
            for s in range(4):
                ac.wait_ge(s_gram, s + 1)
                ac.activation(Gs[0:C, s * 16:(s + 1) * 16, :], PS[0:C, s, :].rearrange("p (m x) -> p m x", m=16),
                              ACT.Copy).then_inc(s_gramv, 1)
            for b in range(2):
                ac.wait_ge(s_et, b + 1)
                ac.activation(E[:, :, b * 8:(b + 1) * 8, 0:16],
                              PS[:, 6 + b, 0:384].rearrange("p (r a c) -> p a r c", r=8, a=3), ACT.Copy)\
                  .then_inc(s_etv, 1)
            for b in range(2):
                ac.wait_ge(s_et, 3 + b)
                ac.activation(Tm[:, :, b * 8:(b + 1) * 8, :],
                              PS[:, 4 + b, 0:384].rearrange("p (r a c) -> p a r c", r=8, a=3), ACT.Copy)\
                  .then_inc(s_tv, 1)
            for s in range(16):
                ac.wait_ge(s_piv, s + 1)
                ac.activation(sq3[:, :, s:s + 1], E[:, :, s, s:s + 1], ACT.Sqrt).then_inc(s_sq, 1)
            preload(ACT.Exp)
            ac.wait_ge(s_back, 1)
            src = PS[0:C, 0, :].rearrange("p (j m) -> p m j", j=8)
            for par in range(2):
                last = ac.activation(BD[0:C, :, par * 16:par * 16 + 8], src, ACT.Copy, scale=parity[par])
            last.then_inc(s_bda, 1)
            for b in range(0, 8, 2):
                ac.wait_ge(s_qt, b + 1)
                ac.activation(qt[0:C, b * 8:(b + 1) * 8, :], PS[0:C, b, 0:320].rearrange("p (m n) -> p m n", m=8),
                              ACT.Copy).then_inc(s_qte, 1)
            ac.wait_ge(s_qte, 8)
            for hd in (4, 5):
                for a in range(2):
                    last = ac.activation(qb_out(a, hd), qb_in(a), ACT.Copy, scale=head[hd])
            last.then_inc(s_qba, 1)
            def mix_evac(t):
                ac.wait_ge(s_mixp, t + 1)
                ac.activation(Mx[:, t, :, :, 0:TOKENS].rearrange("p c a n -> p (c a) n"),
                              PS[:, t % 4, 0:8 * TOKENS].rearrange("p (x n) -> p x n", n=TOKENS), ACT.Identity,
                              bias=convb).then_inc(s_mixe, 1)

            def exp_pair(u):
                ac.wait_ge(s_sub, u + 1)
                v = Mx[:, 2 * u:2 * u + 2, :, :, 0:TOKENS].rearrange("p t c a n -> p (t c a) n")
                ac.activation(v, v, ACT.Exp).then_inc(s_exp, 1)

            ac.wait_ge(s_mix1, 2)
            ac.wait_ge(s_qbp, 2)
            for t in range(T + 2):
                if t < T:
                    ac.wait_ge(s_dots, t + 1)
                    ac.activation(S2[:, t, :], PS[:, t % 4, 0:8 * TOKENS], ACT.Square).then_inc(s_s2, 1)
                if 1 <= t <= T:
                    mix_evac(t - 1)
                if t >= 3 and t % 2:
                    exp_pair((t - 3) // 2)
            preload(ACT.Sqrt)
            for t in range(T + 1):
                if t < T:
                    ac.wait_ge(s_atp, t + 1)
                    ac.activation(attnT[:, t, :], PS[:, 4 + t % 2, :], ACT.Copy).then_inc(s_atT, 1)
                if t % 4 == 0 and t > 0:
                    hf = t // 4 - 1
                    ac.wait_ge(s_av, hf + 1)
                    for a in range(2):
                        for kc in range(KC):
                            last = ac.activation(
                                XTi[:, kc, hf * 4:hf * 4 + 4, a, 0:TOKENS],
                                PS[0:C, 6 + a, kc * 160:(kc + 1) * 160].rearrange("p (t n) -> p t n", t=4)[:, :, 0:TOKENS],
                                ACT.Copy)
                        last.then_inc(s_oT, 1)

            sqrt_ln(1)
            preload(ACT.Exp)
            evac_xt(1, range(4))
            for i in range(4):
                ac.wait_ge(s_chan, 8 + i + 1)
                ac.activation(vT[0:C, i * 8:(i + 1) * 8, :], PS[0:C, 4 + i, 0:COLS].rearrange("p (t n) -> p t n", t=T),
                              ACT.Identity, bias=cq(Q_VB + i % 2)).then_inc(s_chanv, 1)
            for a in range(2):
                ac.wait_ge(s_wsub, a + 1)
                ac.activation(Wm[0:C, a * 16:(a + 1) * 16, :], Wm[0:C, a * 16:(a + 1) * 16, :], ACT.Exp)\
                  .then_inc(s_wexp, 1)
            preload(ACT.Sqrt)
            ac.wait_ge(s_zero, 6)
            for b in range(4):
                ac.wait_ge(s_wv, b + 1)
                ac.activation(oS[0:C, b * 8:(b + 1) * 8, :], PS[0:C, 2 + b, 0:COLS].rearrange("p (t n) -> p t n", t=T),
                              ACT.Copy).then_inc(s_os, 1)
            evac_xt(2, range(4))
            ac.wait_ge(s_gva, 1)
            ac.activation(gg[:, 3:4], gg[:, 2:3], ACT.Sqrt, bias=eps12).then_inc(s_gsd, 1)
            preload(ACT.Exp)
            ac.wait_ge(s_x1p, 1)
            ac.wait_ge(s_gsc, 1)
            for b in range(4):
                for kc in range(KC):
                    last = ac.activation(
                        x1T[0:C, kc, b * 148:(b + 1) * 148].rearrange("p (x n) -> p x n", n=TOKENS),
                        PS[0:C, 4 + b, kc * 256:(kc + 1) * 256].rearrange("p (x n) -> p x n", n=HALF)[:, :, 0:TOKENS],
                        ACT.Identity, bias=gbi[0:C, kc:kc + 1], scale=gsc[0:C, kc:kc + 1])
            last.then_inc(s_x1, 1)
            ac.wait_ge(s_nm, 1)
            ac.activation(ga[0:IMAGES, :], sc16[0:IMAGES, :], ACT.Exp).then_inc(s_ge, 1)
            preload(ACT.Gelu_apprx_tanh)
            ac.wait_ge(s_gbp, 1)
            ac.activation(Gb[0:C, :, :].rearrange("p e b -> p (e b)"), PS[0:C, 2, 0:128], ACT.Copy).then_inc(s_gb, 1)
            ac.wait_ge(s_used, 1)
            bits = ac.value_load(used_bits[0:1, 0:1], min_val=0, max_val=255)
            with ac.Fori(0, EXPERTS // 2) as it:
                for b in range(2):
                    with ac.If(is_used(bits, it * 2 + b)):
                        ac.activation(fcb[:, b, :], fcball[:, it * 2 + b, :], ACT.Copy).then_inc(s_fcb, 1)
                        ac.wait_ge(s_fcb, it * 2 + (b + 1))
                        for i in range(2 * FC):
                            f, nh = divmod(i, 2)
                            ac.wait_ge(s_hp, it * 24 + (b * 12 + i + 1))
                            ac.activation(hT[b][:, f, nh * COLS:(nh + 1) * COLS], PS[:, i % 4, 0:COLS],
                                          ACT.Gelu_apprx_tanh,
                                          bias=fcb[:, b, f:f + 1]).then_inc(s_gelu, 1)
                    with ac.Else():
                        ac.drain().then_inc(s_gelu, 2 * FC)
                        ac.drain().then_inc(s_fcb, 1)
            preload(ACT.Sqrt)
            ac.wait_ge(s_gva, 2)
            ac.activation(gg[:, 3:4], gg[:, 2:3], ACT.Sqrt, bias=eps12).then_inc(s_gsd, 1)
            ac.wait_ge(s_gsc, 2)
            for kc in range(KC):
                ac.activation(XT[0:C, kc, :].rearrange("p (x n) -> p x n", n=HALF)[:, :, 0:TOKENS],
                              acc[0:C, kc, :].rearrange("p (x n) -> p x n", n=TOKENS), ACT.Identity,
                              bias=gbi[0:C, kc:kc + 1], scale=gsc[0:C, kc:kc + 1]).then_inc(s_x2, 1)

            sqrt_ln(2)
            evac_xt(3, range(4))
            for i in range(4):
                ac.wait_ge(s_q2, i + 1)
                ac.activation(qT2[0:C, i * 8:(i + 1) * 8, :], PS[0:C, 4 + i, 0:COLS].rearrange("p (t n) -> p t n", t=T),
                              ACT.Copy).then_inc(s_q2e, 1)
            for t in range(T):
                ac.wait_ge(s_kv2, t + 1)
                ac.activation(A[:, t, :], PS[:, t % 4, 0:2 * DIM], ACT.Copy)
                ac.activation(Aabs[:, t, :], PS[:, t % 4, 0:DIM], ACT.Abs).then_inc(s_kv2e, 1)
            for i in range(4):
                a, kc = divmod(i, 2)
                ac.wait_ge(s_o2, i + 1)
                ac.activation(XTi[:, kc, :, a, 0:TOKENS], PS[0:C, 4 + i, 0:COLS].rearrange("p (t n) -> p t n", t=T),
                              ACT.Copy).then_inc(s_o2e, 1)

            sqrt_ln(3)
            preload(ACT.Exp)
            evac_xt(4, range(4))
            ac.wait_ge(s_lsub, 1)
            ac.activation(pr[:, :, :], pr[:, :, :], ACT.Exp).then_inc(s_lexp, 1)
            for g in range(T):
                ac.wait_ge(s_xip, g + 1)
                ac.activation(xinT[0:C, :, :, g * CAP:(g + 1) * CAP],
                              PS[0:C, g, 0:KC * GE].rearrange("p (k e c) -> p k e c", k=KC, e=EXPERTS),
                              ACT.Copy).then_inc(s_xin, 1)
            for b in range(4):
                ac.wait_ge(s_ctp, b + 1)
                ac.activation(combT[0:92, 2 * b:2 * b + 2, :, :].rearrange("p g a n -> p (g a n)"), PS[0:92, b, :],
                              ACT.Copy).then_inc(s_ct, 1)
            with ac.Fori(0, EXPERTS // 2) as it:
                for b in range(2):
                    ac.wait_ge(s_edone, it * 2 + EXPERTS)
                    for i in range(3):
                        ac.wait_ge(s_h1p, it * 6 + (3 * b + i + 1))
                        ac.activation(hT1[b][:, 2 * i:2 * i + 2, :].rearrange("p f n -> p (f n)"),
                                      PS[:, 3 * b + i, 0:2 * SLOTS], ACT.Relu).then_inc(s_relu, 1)
            for g in range(T):
                ac.wait_ge(s_ygp, g + 1)
                ac.activation(yG[0:92, g, :, :].rearrange("p a n -> p (a n)"), PS[0:92, g, 0:2 * DIM],
                              ACT.Copy).then_inc(s_yg, 1)

        @block.vector
        def _(ve):
            n = [0]

            def link(ins):
                n[0] += 1
                ins.then_inc(dchain, 1)
                ve.wait_ge(dchain, n[0])

            def normalise(r, hf):
                ts = range(4 * hf, 4 * hf + 4)
                for t in ts:
                    if r == 0:
                        ve.wait_ge(s_hcopy, t + 1)
                    last = ve.bn_stats(stats[:, t, :], h[:, t, :])
                link(last)
                for t in ts:
                    last = ve.bn_aggr(mv[:, t, :], stats[:, t, :])
                last.then_inc(s_var, 1)
                ve.wait_ge(s_sd, 2 * r + hf + 1)
                link(ve.reciprocal(rstd[:, 4 * hf:4 * hf + 4], sd[:, 4 * hf:4 * hf + 4]))
                for t in ts:
                    ve.tensor_scalar(xn[:, t, :], h[:, t, :], mv[:, t, 0:1], rstd[:, t:t + 1], ALU.subtract,
                                     ALU.mult).then_inc(s_xn, 1)

            def residual_norm(r, done, base):
                for hf in range(2):
                    for t in range(4 * hf, 4 * hf + 4):
                        ve.wait_ge(done, base + t + 1)
                        ve.tensor_tensor(h[:, t, :], PS[:, t % 4, 0:DIM], h[:, t, :], ALU.add).then_inc(s_h, 1)
                    ve.wait_ge(s_h, (r - 1) * T + 4 * hf + 4)
                    normalise(r, hf)

            normalise(0, 0)
            normalise(0, 1)
            ve.wait_ge(s_bias, 32)
            link(ve.tensor_tensor(wpT[0:HEADS, :], cq(Q_CW, HEADS, HEADS), cq(Q_CW + HEADS, HEADS, HEADS), ALU.add))
            ve.tensor_scalar(wpT[0:HEADS, :], wpT[0:HEADS, :], cq(Q_GS, HEADS), None, ALU.mult).then_inc(s_mixw, 1)
            ve.wait_ge(s_mixr, 1)
            ve.wait_ge(s_zero, 4)
            ve.tensor_copy(convb, PS[:, 3, HEADS:HEADS + 1])
            ve.tensor_tensor(mixT[:, :, 0:60].rearrange("p k (o n) -> p k o n", o=HC),
                             bc(PS[:, 3, 0:HEADS].rearrange("p (k o) -> p k o", k=KC), 3, NCH),
                             bc(bc(con[:, K_DN:K_DN + NCH], 1, HC), 1, KC), ALU.mult).then_inc(s_mix1, 2)

            for t in range(T):
                ve.wait_ge(s_tok, t + 1)
                b = t % 2
                ve.tensor_tensor(A[:, t, :], PS[:, b, 0:2 * DIM], row[:, R_QKVB:R_QKVB + 2 * DIM], ALU.add)
                ve.tensor_tensor(vpad[:, t, :].rearrange("p (x c) -> p x c", c=32)[:, :, 0:HD],
                                 PS[:, 2 + b, 0:DIM].rearrange("p (x c) -> p x c", c=HD),
                                 row[:, R_QKVB + 2 * DIM:R_QKVB + 3 * DIM].rearrange("p (x c) -> p x c", c=HD),
                                 ALU.add).then_inc(s_tokv, 1)

            def mark(ins):
                n[0] += 1
                ins.then_inc(dchain, 1)
                return n[0]

            ve.wait_ge(s_etv, 3)
            e_done = t_done = None
            for s in range(17):
                u = s - 1
                re, ru, w = 15 - s, 15 - u, 16 - u
                if s < 16:
                    if e_done:
                        ve.wait_ge(dchain, e_done)
                    ve.sem_inc(s_piv, 1)
                if s < 15:
                    e0 = mark(ve.reciprocal(inv3, E[:, :, s, s:s + 1]))
                if u >= 0:
                    if u == 0:
                        ve.wait_ge(s_tv, 2)
                    if t_done:
                        ve.wait_ge(dchain, t_done)
                    ve.wait_ge(dchain, r_done)
                    top, R = Tm[:, :, u, u:16], Rn[:, u % 2, :, 0:w]
                    minus = mark(ve.tensor_tensor(rowm[:, :, 0:w], top, R, ALU.subtract))
                    plus = mark(ve.scalar_tensor_tensor(rowp[:, :, 0:w], Tm[:, :, u, u:u + 1].broadcast_to([128, 3, w]),
                                                        0.0, R, ALU.is_ge, ALU.mult))
                if u >= 0:
                    ve.wait_ge(dchain, plus)
                    t1 = mark(ve.scalar_tensor_tensor(top, rowp[:, :, 0:w], 2.0, rowm[:, :, 0:w], ALU.mult, ALU.add))
                if s < 15:
                    ve.wait_ge(dchain, e0)
                    e1 = mark(ve.tensor_tensor(lcol[:, :, 0:re], E[:, :, s + 1:16, s],
                                               inv3.broadcast_to([128, 3, re]), ALU.mult))
                if 0 <= u < 15:
                    ve.wait_ge(dchain, t1)
                    t0 = mark(ve.reciprocal(invu, Tm[:, :, u, u:u + 1]))
                if s < 15:
                    ve.wait_ge(dchain, e1)
                    prod = Pb[:, 0:3 * re * 16].rearrange("p (a r c) -> p a r c", a=3, r=re)
                    e2 = mark(ve.tensor_tensor(prod, bc(lcol[:, :, 0:re], 3, 16), bc(E[:, :, s, s + 1:s + 17], 2, re),
                                               ALU.mult))
                if 0 <= u < 15:
                    ve.wait_ge(dchain, t0)
                    t2 = mark(ve.tensor_tensor(lcolu[:, :, 0:ru], Tm[:, :, u + 1:16, u],
                                               invu.broadcast_to([128, 3, ru]), ALU.mult))
                if s < 15:
                    ve.wait_ge(dchain, e2)
                    below = E[:, :, s + 1:16, s + 1:s + 17]
                    e_done = mark(ve.tensor_tensor(below, below, prod, ALU.subtract))
                if 0 <= u < 15:
                    ve.wait_ge(dchain, t2)
                    produ = Pu[:, 0:3 * ru * ru].rearrange("p (a r c) -> p a r c", a=3, r=ru)
                    t3 = mark(ve.tensor_tensor(produ, bc(lcolu[:, :, 0:ru], 3, ru), bc(Tm[:, :, u, u + 1:16], 2, ru),
                                               ALU.mult))
                if s < 16:
                    ve.wait_ge(s_sq, s + 1)
                    r0 = mark(ve.reciprocal(rs3[:, :, s:s + 1], sq3[:, :, s:s + 1]))
                if 0 <= u < 15:
                    ve.wait_ge(dchain, t3)
                    belowu = Tm[:, :, u + 1:16, u + 1:16]
                    t_done = mark(ve.tensor_tensor(belowu, belowu, produ, ALU.subtract))
                if s < 16:
                    ve.wait_ge(dchain, r0)
                    r_done = mark(ve.tensor_tensor(Rn[:, s % 2, :, 0:16 - s], E[:, :, s, s:16],
                                                   rs3[:, :, s:s + 1].broadcast_to([128, 3, 16 - s]), ALU.mult))
            ve.wait_ge(dchain, t1)
            diag = Tm[:, :, :, :].rearrange("p a r c -> p a (r c)")[:, :, 0:256:17]
            link(ve.tensor_scalar(tsg, diag, 0.0, -2.0, ALU.is_ge, ALU.mult))
            link(ve.scalar_tensor_tensor(nsg, tsg, 1.0, rs3, ALU.add, ALU.mult))
            ve.wait_ge(s_zero, 5)
            for par in range(2):
                p0 = par * 64
                o = BLK[p0:p0 + 64].rearrange("p j (a x) -> p a j x", a=3)[:, :, :, par * 16:par * 16 + 16]
                last = ve.tensor_tensor(o, E[p0:p0 + 64, :, :, 16:32], bc(nsg[p0:p0 + 64], 3, 16), ALU.mult)
            last.then_inc(s_blk, 1)
            ve.wait_ge(s_back, 1)
            src = PS[0:C, 1, :].rearrange("p (j m) -> p m j", j=8)
            for par in range(2):
                last = ve.tensor_scalar(BD[0:C, :, par * 16 + 8:par * 16 + 16], src, parity[par], None, ALU.mult)
            last.then_inc(s_bdv, 1)
            for b in range(1, 8, 2):
                ve.wait_ge(s_qt, b + 1)
                ve.tensor_copy(qt[0:C, b * 8:(b + 1) * 8, :], PS[0:C, b, 0:320].rearrange("p (m n) -> p m n", m=8))\
                  .then_inc(s_qte, 1)
            ve.wait_ge(s_qte, 8)
            for hd in range(4):
                for a in range(2):
                    last = ve.tensor_scalar(qb_out(a, hd), qb_in(a), head[hd], None, ALU.mult)
            last.then_inc(s_qbv, 1)
            for u in range(5):
                if u < 4:
                    v = Mx[:, 2 * u:2 * u + 2, :, :, 0:TOKENS].rearrange("p t c a n -> p (t c a) n")
                    m = mx[:, 2 * u:2 * u + 2, :].rearrange("p t x -> p (t x)")
                    ve.wait_ge(s_mixe, 2 * u + 2)
                    link(ve.tensor_reduce(m, v, AX, ALU.max))
                    ve.tensor_tensor(v, v, bc(m, 2, TOKENS), ALU.subtract).then_inc(s_sub, 1)
                if u >= 1:
                    b = u - 1
                    v = Mx[:, 2 * b:2 * b + 2, :, :, 0:TOKENS].rearrange("p t c a n -> p (t c a) n")
                    m = sme[:, 2 * b:2 * b + 2, :].rearrange("p t x -> p (t x)")
                    q = rsm[:, 2 * b:2 * b + 2, :].rearrange("p t x -> p (t x)")
                    ve.wait_ge(s_exp, b + 1)
                    link(ve.tensor_reduce(m, v, AX, ALU.add))
                    link(ve.reciprocal(q, m))
                    ve.tensor_tensor(v, v, bc(q, 2, TOKENS), ALU.mult).then_inc(s_att, 1)

            ve.wait_ge(s_hb, 1)
            residual_norm(1, s_prj, 0)

            for t in range(T):
                ve.wait_ge(s_tok, T + t + 1)
                ve.tensor_tensor(A[:, t, :], PS[:, t % 4, 0:2 * DIM], row[:, R_W1B:R_W1B + 2 * DIM], ALU.add)\
                  .then_inc(s_tokv, 1)
            for a in range(2):
                w = Wm[0:C, a * 16:(a + 1) * 16, :]
                ve.wait_ge(s_w_ps, a + 1)
                link(ve.scalar_tensor_tensor(w, PS[0:C, a, :].rearrange("p (m x) -> p m x", m=16),
                                             float(1.0 / np.sqrt(np.float32(TOKENS))),
                                             bc(con[0:C, K_NEG:K_NEG + 32], 1, 16), ALU.mult, ALU.add))
                link(ve.tensor_reduce(wmax[0:C, a * 16:(a + 1) * 16], w, AX, ALU.max))
                ve.tensor_tensor(w, w, bc(wmax[0:C, a * 16:(a + 1) * 16], 2, 32), ALU.subtract).then_inc(s_wsub, 1)
            for a in range(2):
                w = Wm[0:C, a * 16:(a + 1) * 16, :]
                ve.wait_ge(s_wexp, a + 1)
                link(ve.tensor_reduce(wsum[0:C, a * 16:(a + 1) * 16], w, AX, ALU.add))
                link(ve.reciprocal(wrec[0:C, a * 16:(a + 1) * 16], wsum[0:C, a * 16:(a + 1) * 16]))
                link(ve.tensor_tensor(w, w, bc(wrec[0:C, a * 16:(a + 1) * 16], 2, 32), ALU.mult))
                ve.transpose(BD2[0:C, a * 16:(a + 1) * 16, :], w).then_inc(s_wT, 1)
            ve.wait_ge(s_zb, 1)
            for t in range(T):
                ve.wait_ge(s_w2p, t + 1)
                ve.tensor_tensor(xn[:, t, :], PS[:, t % 4, 0:DIM], xn[:, t, :], ALU.add).then_inc(s_s, 1)
                if t >= 1:
                    ve.wait_ge(s_s, t)
                    ve.bn_stats(stats[:, t - 1, :], xn[:, t - 1, :])
            ve.wait_ge(s_s, T)
            link(ve.bn_stats(stats[:, T - 1, :], xn[:, T - 1, :]))

            NALL = float(IMAGES * TOKENS * DIM)

            def global_norm(r, p, parts, bank, wcol, bcol):
                link(ve.bn_aggr(gmv[0:p], stats[0:p].rearrange("p t x -> p (t x)")[:, 0:parts]))
                ve.tensor_copy(gst[0:p, 0:1], gmv[0:p, 0:1])
                link(ve.tensor_tensor(gg[0:p, 0:1], gmv[0:p, 0:1], gmv[0:p, 0:1], ALU.mult))
                ve.tensor_tensor(gst[0:p, 1:2], gg[0:p, 0:1], gmv[0:p, 1:2], ALU.add).then_inc(s_gst, 1)
                ve.wait_ge(s_gps, r + 1)
                used = 2 * TOKENS if p == 128 else p
                link(ve.tensor_scalar(gg[:, 0:2], PS[:, bank, 0:2], 1.0 / used, None, ALU.mult))
                link(ve.tensor_tensor(gg[:, 2:3], gg[:, 0:1], gg[:, 0:1], ALU.mult))
                link(ve.tensor_tensor(gg[:, 2:3], gg[:, 1:2], gg[:, 2:3], ALU.subtract))
                ve.tensor_scalar(gg[:, 2:3], gg[:, 2:3], NALL / (NALL - 1.0), None, ALU.mult).then_inc(s_gva, 1)
                ve.wait_ge(s_gsd, r + 1)
                link(ve.reciprocal(gg[:, 4:5], gg[:, 3:4]))
                link(ve.tensor_scalar(gsc[0:C], cq(wcol, C, KC), gg[0:C, 4:5], None, ALU.mult))
                link(ve.tensor_scalar(gbi[0:C], gsc[0:C], gg[0:C, 0:1], None, ALU.mult))
                ve.tensor_tensor(gbi[0:C], cq(bcol, C, KC), gbi[0:C], ALU.subtract).then_inc(s_gsc, 1)

            global_norm(0, 128, T * 6, 0, Q_LN1W, Q_LN1B)

            ve.wait_ge(s_x1, 1)
            ve.tensor_reduce(xbar[0:C], x1T[0:C, :, :].rearrange("p k (b n) -> p (k b) n", n=TOKENS)
                             .rearrange("p (k b) n -> p k b n", k=KC), AX, ALU.add).then_inc(s_xbar, 1)
            ve.tensor_copy(acc[0:C, :, :], x1T[0:C, :, :])
            ve.wait_ge(s_rps, 1)
            link(ve.scalar_tensor_tensor(sc16[0:IMAGES], PS[0:IMAGES, 1, 0:EXPERTS], 1.0 / TOKENS,
                                         row[0:IMAGES, R_RB:R_RB + EXPERTS], ALU.mult, ALU.add))
            link(ve.tensor_reduce(gone[0:IMAGES, 0:1], sc16[0:IMAGES], AX, ALU.max))
            ve.tensor_scalar(sc16[0:IMAGES], sc16[0:IMAGES], gone[0:IMAGES, 0:1], None, ALU.subtract).then_inc(s_nm, 1)
            ve.wait_ge(s_ge, 1)
            link(ve.tensor_reduce(gone[0:IMAGES, 1:2], ga[0:IMAGES], AX, ALU.add))
            link(ve.reciprocal(gone[0:IMAGES, 2:3], gone[0:IMAGES, 1:2]))
            link(ve.tensor_scalar(ga[0:IMAGES], ga[0:IMAGES], gone[0:IMAGES, 2:3], None, ALU.mult))
            link(ve.max(g8[0:IMAGES], ga[0:IMAGES]))
            link(ve.max_index(gi[0:IMAGES], g8[0:IMAGES], ga[0:IMAGES]))
            link(ve.tensor_copy(gi_f[0:IMAGES], gi[0:IMAGES]))
            link(ve.tensor_scalar(gm[0:IMAGES], con[0:IMAGES, K_I8:K_I8 + 8], gi_f[0:IMAGES, 0:1], None, ALU.is_equal))
            link(ve.scalar_tensor_tensor(gm[0:IMAGES], con[0:IMAGES, K_I8:K_I8 + 8], gi_f[0:IMAGES, 1:2],
                                         gm[0:IMAGES], ALU.is_equal, ALU.add))
            link(ve.tensor_tensor(gm[0:IMAGES], gm[0:IMAGES], ga[0:IMAGES], ALU.mult))
            ve.tensor_tensor(Gd[:, :, :], bc(gm[0:IMAGES], 2, IMAGES), bc(con[0:IMAGES, K_ID:K_ID + IMAGES], 1, EXPERTS),
                             ALU.mult).then_inc(s_gd, 1)
            ve.wait_ge(s_gb, 1)
            link(ve.tensor_reduce(used[0:1], Gb[0:1, :, :], AX, ALU.max))
            link(ve.scalar_tensor_tensor(used[0:1], used[0:1], 0.0, con[0:1, K_POW2:K_POW2 + EXPERTS],
                                         ALU.is_gt, ALU.mult))
            link(ve.tensor_reduce(gone[0:1, 3:4], used[0:1], AX, ALU.add))
            ve.tensor_copy(used_bits[0:1, 0:1], gone[0:1, 3:4]).then_inc(s_used, 1)
            ve.wait_ge(s_used, 1)
            bits = ve.value_load(used_bits[0:1, 0:1], min_val=0, max_val=255)
            ve.sem_inc(s_acc, 1)
            with ve.Fori(0, EXPERTS // 2) as it:
                for b in range(2):
                    with ve.If(is_used(bits, it * 2 + b)):
                        ve.wait_ge(s_edone, it * 2 + (b + 1))
                        for i in range(4):
                            kc, nh = divmod(i, 2)
                            y = ytmp[0:C, i % 2, :]
                            g = Gb[0:C, it * 2 + b, nh * 8:(nh + 1) * 8]
                            ve.scalar_tensor_tensor(y.rearrange("p (x n) -> p x n", n=TOKENS),
                                                    PS[0:C, 4 + i, 0:COLS].rearrange("p (x n) -> p x n", n=TOKENS),
                                                    col[0:C, it * 4 + (Q_PB + b * 2 + kc)].unsqueeze(1),
                                                    bc(g, 2, TOKENS), ALU.add, ALU.mult).then_inc(s_ytmp, 1)
                            ve.wait_ge(s_ytmp, it * 8 + (b * 4 + i + 1))
                            ve.tensor_tensor(acc[0:C, kc, nh * COLS:(nh + 1) * COLS],
                                             acc[0:C, kc, nh * COLS:(nh + 1) * COLS], y, ALU.add).then_inc(s_acc, 1)
                    with ve.Else():
                        ve.drain().then_inc(s_acc, 4)
                        ve.drain().then_inc(s_ytmp, 4)
            ve.wait_ge(s_acc, 4 * EXPERTS + 1)
            for i in range(4):
                kc, nh = divmod(i, 2)
                last = ve.bn_stats(stats[0:C, i, :], acc[0:C, kc, nh * COLS:(nh + 1) * COLS])
            link(last)
            global_norm(1, C, 24, 0, Q_LN2W, Q_LN2B)
            residual_norm(2, s_x2p, 0)

            ve.wait_ge(s_q2e, 4)
            link(ve.tensor_reduce(sq2[0:C], qT2[0:C], AX, ALU.add, apply_absolute_value=True))
            link(ve.tensor_scalar(sq2[0:C], sq2[0:C], 1e-12, None, ALU.max))
            ve.wait_ge(s_kvp, 1)
            link(ve.tensor_scalar(sk2[0:C].rearrange("p (a m) -> p m a", a=2),
                                  PS[0:C, 2, 0:32].rearrange("p (m a) -> p m a", a=2), 1e-12, None, ALU.max))
            link(ve.reciprocal(sq2[0:C], sq2[0:C]))
            link(ve.reciprocal(sk2[0:C], sk2[0:C]))
            link(ve.tensor_tensor(sk2[0:C], sk2[0:C], sq2[0:C], ALU.mult))
            link(ve.tensor_tensor(kvs[0:C], bc(con[0:C, K_PAIR:K_PAIR + 32], 1, 32), bc(sk2[0:C], 2, 32), ALU.mult))
            for a in range(2):
                ve.wait_ge(s_kvm, a + 1)
                ve.tensor_tensor(BD2[0:C, a * 16:(a + 1) * 16, :], PS[0:C, a, :].rearrange("p (m x) -> p m x", m=16),
                                 kvs[0:C, a * 16:(a + 1) * 16, :], ALU.mult).then_inc(s_bd3, 1)
            ve.wait_ge(s_hb, 2)
            residual_norm(3, s_prj, T)

            ve.wait_ge(s_lg, 1)
            lg = PS[:, 0, 0:64].rearrange("p (g e) -> p g e", g=T)
            link(ve.tensor_reduce(lmax, lg, AX, ALU.max))
            ve.tensor_tensor(pr[:, :, :], lg, bc(lmax, 2, EXPERTS), ALU.subtract).then_inc(s_lsub, 1)
            ve.wait_ge(s_lexp, 1)
            link(ve.tensor_reduce(lmax, pr[:, :, :], AX, ALU.add))
            link(ve.reciprocal(lmax, lmax))
            link(ve.tensor_tensor(pr[:, :, :], pr[:, :, :], bc(lmax, 2, EXPERTS), ALU.mult))
            for g in range(T):
                last = ve.max(v8[:, g, :], pr[:, g, :])
            link(last)
            for g in range(T):
                last = ve.max_index(i8[:, g, :], v8[:, g, :], pr[:, g, :])
            link(last)
            link(ve.tensor_copy(i8f[:, :, :], i8[:, :, :]))
            for k in range(2):
                last = ve.tensor_tensor(m12[:, k], bc(con[:, K_I8:K_I8 + 8], 1, T), bc(i8f[:, :, k], 2, EXPERTS),
                                        ALU.is_equal)
            link(last)
            mf = m12[:, :, :, :].rearrange("p k g e -> p (k g e)")
            ve.tensor_scalar(mf, mf, con[:, K_VALID:K_VALID + 1], None, ALU.mult).then_inc(s_m12, 1)
            ve.wait_ge(s_rk, 1)
            ve.wait_ge(s_m12, 1)
            link(ve.tensor_tensor(rank[:, :, :, :].rearrange("p k g e -> p (k g e)"), PS[:, 5, 0:128], mf, ALU.mult))
            link(ve.tensor_tensor(rank[:, 0], rank[:, 0], rank[:, 1], ALU.add))
            link(ve.tensor_scalar(rank[:, 0], rank[:, 0], -1.0, None, ALU.add))
            link(ve.tensor_tensor(gse[:, :, :], m12[:, 0], m12[:, 1], ALU.add))
            link(ve.tensor_tensor(gse[:, :, :], gse[:, :, :], pr[:, :, :], ALU.mult))
            GEf = T * EXPERTS
            rk = bc(rank[:, 0].rearrange("p g e -> p (g e)"), 2, CAP)
            dv = Q[:, 0:T * GE].rearrange("p (x c) -> p x c", c=CAP)
            cv = Q[:, T * GE:2 * T * GE].rearrange("p (x c) -> p x c", c=CAP)
            ve.tensor_tensor(dv, rk, bc(con[:, K_I23:K_I23 + CAP], 1, GEf), ALU.is_equal).then_inc(s_disp, 1)
            ve.wait_ge(s_disp, 1)
            ve.tensor_tensor(cv, dv, bc(gse[:, :, :].rearrange("p g e -> p (g e)"), 2, CAP), ALU.mult)\
              .then_inc(s_comb, 1)
            ve.sem_inc(s_y1, 2)
            with ve.Fori(0, EXPERTS // 2) as it:
                for b in range(2):
                    ve.wait_ge(s_edone, it * 2 + (EXPERTS + b + 1))
                    ve.tensor_copy(yT[0:C, :, :, it * 2 + b, :],
                                   PS[0:C, 6 + b, 0:KC * SLOTS].rearrange("p (k g c) -> p k g c", k=KC, g=T))\
                      .then_inc(s_y1, 1)
            for t in range(T):
                ve.wait_ge(s_fin, t + 1)
                ve.tensor_tensor(h[:, t, :], PS[:, t, 0:DIM], h[:, t, :], ALU.add).then_inc(s_res, 1)


def constants():
    k = np.zeros((128, K_ALL), np.float32)
    p = np.arange(128)
    k[:, K_ID:K_ID + 128] = np.eye(128)
    k[:, K_TRI:K_TRI + 128] = p[:, None] <= p[None, :]
    k[:, K_VALID:K_VALID + 128] = (p % HALF < TOKENS)[:, None]
    k[:, K_ONE:K_ONE + 128] = 1
    k[:, K_II:K_II + 64] = (p % 64)[:, None] == np.arange(64)
    same = ((p // HD) % 2)[:, None] == np.arange(32) // HD
    k[:, K_PAIR:K_PAIR + 32] = same
    k[:, K_NEG:K_NEG + 32] = np.where(same, 0.0, -1e30)
    k[:, K_HEAD:K_HEAD + HC] = (p // HD)[:, None] == np.arange(HC)
    for hd in range(HEADS):
        c0 = K_E1 + (hd // HC) * 64 + (hd % HC) * NCH
        k[hd, c0:c0 + NCH] = 1
    q = p % 64
    k[:, K_DN:K_DN + NCH] = ((q % NCH)[:, None] == np.arange(NCH)) & (q < HC * NCH)[:, None]
    k[:, K_I8:K_I8 + EXPERTS] = np.arange(EXPERTS)
    k[:, K_I23:K_I23 + CAP] = np.arange(CAP)
    k[0, K_IND:K_IND + 128] = (p % HALF > 0) & (p % HALF < TOKENS)
    k[1, K_IND:K_IND + 128] = p % HALF == 0
    k[:, K_EYE:K_EYE + 256] = np.eye(16).reshape(-1)
    for a in range(2):
        k[a * HALF:a * HALF + TOKENS, K_HALF + a] = 1
    k[:, K_POW2:K_POW2 + EXPERTS] = 2 ** np.arange(EXPERTS)
    return k


def layout(i):
    def chunks(w, parts, size):
        return w.reshape(parts, size, -1).transpose(1, 0, 2)

    pat = i["x"].reshape(IMAGES, 3, 6, 16, 6, 16).transpose(3, 5, 1, 0, 2, 4).reshape(PK, 128, T, 2, PATCHES)
    padded = np.zeros((128, PK, T, 2, HALF), np.float32)
    padded[..., 1:TOKENS] = pat.transpose(1, 0, 2, 3, 4)
    rows = np.concatenate([i["L0_attn_qkv_b"], i["L0_attn_proj_b"], i["L0_ffn_W1_b"][:2 * DIM], i["L0_ffn_W2_b"],
                           i["L0_ffn_r_b"], i["L1_attn_b_proj"]])
    cols = np.zeros((128, Q_ALL), np.float32)
    cols[:C, Q_QKB:Q_QKB + 4] = i["L0_attn_qkv_b"][:2 * DIM].reshape(4, C).T
    cols[:C, Q_VB:Q_VB + 2] = i["L0_ffn_W1_b"][2 * DIM:].reshape(2, C).T
    for at, name in ((Q_LN1W, "ln1_w"), (Q_LN1B, "ln1_b"), (Q_LN2W, "ln2_w"), (Q_LN2B, "ln2_b")):
        cols[:C, at:at + 2] = i["L0_ffn_" + name].reshape(2, C).T
    cols[:C, Q_PB:Q_PB + 16] = i["L0_ffn_proj_b"].reshape(2 * EXPERTS, C).T
    cols[:, Q_FCB:Q_FCB + 48] = i["L0_ffn_fc_b"].reshape(FC * EXPERTS, 128).T
    cols[:, Q_GS] = i["L0_attn_grassman_scale"]
    cols[:HEADS, Q_CB] = i["L0_attn_conv_b"]
    cols[:HEADS, Q_CW:Q_CW + 24] = i["L0_attn_conv_w"].reshape(HEADS, 2, HEADS).transpose(2, 1, 0).reshape(HEADS, 24)
    ew = lambda w: w.reshape(EXPERTS, KC, C, FF).transpose(0, 2, 1, 3).reshape(EXPERTS, C, KC * FF)
    eo = lambda w: w.reshape(EXPERTS, FC, 128, DIM).transpose(0, 2, 1, 3).reshape(EXPERTS, 128, FC * DIM)
    return {
        "patches": padded.reshape(128, PK, T * 128),
        "tok_w": chunks(i["L0_tok_W"].reshape(DIM, 16, 16, 3).reshape(DIM, 768).T, PK, 128),
        "cls_b": np.stack([i["L0_tok_b"], i["cls_tok"].reshape(DIM)]),
        "rows": rows,
        "cols": cols,
        "consts": constants(),
        "qkv_w": chunks(i["L0_attn_qkv_w"].T, KC, C),
        "proj_w": chunks(i["L0_attn_proj_w"].T, KC, C),
        "w1": chunks(i["L0_ffn_W1_w"], KC, C),
        "w2": chunks(i["L0_ffn_W2_w"], KC, C),
        "r_w": chunks(i["L0_ffn_r_w"], KC, C),
        "fc_w": ew(i["L0_ffn_fc_w"]),
        "pr_w": eo(i["L0_ffn_proj_w"]),
        "qkv2_w": chunks(i["L1_attn_w_qkv"].T, KC, C),
        "proj2_w": chunks(i["L1_attn_w_proj"].T, KC, C),
        "router_w": chunks(i["L1_ffn_w_router"], KC, C),
        "wi": ew(i["L1_ffn_wi"]),
        "wo": eo(i["L1_ffn_wo"]),
    }


def kernel(**inputs):
    import concourse.bacc as bacc
    from concourse.bass_utils import run_bass_kernel_spmd

    arrays = {f"in_{k}": np.ascontiguousarray(v) for k, v in layout({k: np.asarray(v) for k, v in inputs.items()}).items()}
    nc = bacc.Bacc("TRN2", target_bir_lowering=False, num_devices=1)
    args = [nc.dram_tensor(k, v.shape, mybir.dt.from_np(v.dtype), kind="ExternalInput").ap() for k, v in arrays.items()]
    scratch = nc.dram_tensor("scratch", (T, 2, KC, C, TOKENS), F32, kind="Internal").ap()
    out = nc.dram_tensor("out_0", (IMAGES, TOKENS, DIM), F32, kind="ExternalOutput").ap()
    vit_tower(nc, *args, scratch, out)
    return run_bass_kernel_spmd(nc, [arrays], core_ids=[0]).results[0]["out_0"]
```

```python
from contextlib import ExitStack

import numpy as np

import concourse.bass as bass
from concourse import mybir

F32 = mybir.dt.float32
U32 = mybir.dt.uint32
I32 = mybir.dt.int32
ALU = mybir.AluOpType
ACT = mybir.ActivationFunctionType
AX = mybir.AxisListType.X

IMAGES, TOKENS, DIM, HEADS, HD = 16, 37, 192, 12, 16
PATCHES = 36
T = IMAGES // 2
HALF = 64
KC = 2
C = DIM // KC
HC = HEADS // KC
PAIRS = HC // 2
COLS = T * TOKENS
ALLC = 2 * COLS
PK = 6
FF = 768
FC = FF // 128
EXPERTS = 8
NCH = 10
CH = 4
NP = NCH * CH
CAP = 23
SLOTS = T * CAP
FILL = (16, 20)
QI = IMAGES // 4
QCOLS = QI * TOKENS
MATS = 2 * 2 * KC * T

R_QKVB = 0
R_PROJB = R_QKVB + 3 * DIM
R_W1B = R_PROJB + DIM
R_W2B = R_W1B + 2 * DIM
R_RB = R_W2B + DIM
R_BP = R_RB + EXPERTS
R_ALL = R_BP + DIM
Q_QKB = 0
Q_VB = Q_QKB + 4
Q_LN1W = Q_VB + 2
Q_LN1B = Q_LN1W + 2
Q_LN2W = Q_LN1B + 2
Q_LN2B = Q_LN2W + 2
Q_PB = Q_LN2B + 2
Q_FCB = Q_PB + 2 * EXPERTS
Q_GS = Q_FCB + FC * EXPERTS
Q_CB = Q_GS + 1
Q_CW = Q_CB + 1
Q_TB = Q_CW + 2 * HEADS
Q_CLS = Q_TB + KC
Q_ALL = Q_CLS + KC
K_ID = 0
K_TRI = K_ID + 128
K_VALID = K_TRI + 128
K_ONE = K_VALID + 128
K_II = K_ONE + 128
K_PAIR = K_II + 64
K_NEG = K_PAIR + 32
K_HEAD = K_NEG + 32
K_E1 = K_HEAD + HC
K_DN = K_E1 + 128
K_I8 = K_DN + NCH
K_I23 = K_I8 + EXPERTS
K_EYE = K_I23 + CAP
K_HALF = K_EYE + 256
K_CODE = K_HALF + 2
K_CODE3 = K_CODE + 4 * EXPERTS
K_POW4 = K_CODE3 + EXPERTS
K_MEANV = K_POW4 + EXPERTS
K_MEANC = K_MEANV + 128
K_ALL = K_MEANC + 128


def vit_tower(nc, patches, tok_w, rows, cols, consts, qkv_w, proj_w, w1, w2, r_w, fc_w, pr_w,
              qkv2_w, proj2_w, router_w, wi, wo, scratch, out):
    ctx = ExitStack()
    with ctx:
        def sb(name, shape, dt=F32):
            return ctx.enter_context(nc.sbuf_tensor(name, shape, dt))

        def sem(name):
            return ctx.enter_context(nc.semaphore(name))

        def bc(ap, axis, n):
            v = ap.unsqueeze(axis)
            shape = list(v.shape)
            shape[axis] = n
            return v.broadcast_to(shape)

        PS = ctx.enter_context(nc.psum_tensor("PS", [128, 8, 512], F32))

        P = sb("P", [128, 2 * FC * ALLC])
        Q = sb("Q", [128, 8192])
        M = sb("M", [128, T * CH * 128])
        h = sb("h", [128, T, DIM])
        xn = sb("xn", [128, T, DIM])
        XT = sb("XT", [128, KC, T * 128])
        x1T = sb("x1T", [128, KC, ALLC])
        acc = sb("acc", [128, KC, ALLC])
        row = sb("row", [128, R_ALL])
        col = sb("col", [128, Q_ALL])
        con = sb("con", [128, K_ALL])
        qkT = sb("qkT", [128, MATS, NP])
        qt = sb("qt", [128, MATS, NP])
        vpad = sb("vpad", [128, T, HEADS * 32])
        tokw = sb("tokw", [128, PK, DIM])
        qkvw = sb("qkvw", [128, KC, 3 * DIM])
        projw = sb("projw", [128, KC, DIM])
        w1w = sb("w1w", [128, KC, 3 * DIM])
        w2w = sb("w2w", [128, KC, DIM])
        rw = sb("rw", [128, KC, EXPERTS])
        qkv2w = sb("qkv2w", [128, KC, 3 * DIM])
        proj2w = sb("proj2w", [128, KC, DIM])
        routw = sb("routw", [128, KC, EXPERTS])
        wi_sb = sb("wi_sb", [128, 2, KC * FF])
        wo_sb = sb("wo_sb", [128, 2, FC * DIM])
        Lc = sb("Lc", [128, 15, 3, 16])
        Pf = sb("Pf", [128, 3 * 64])
        mixT = sb("mixT", [128, KC, 64])
        small = sb("small", [128, 1024])

        at = [0]

        def sm(*shape):
            n = int(np.prod(shape))
            v = small[:, at[0]:at[0] + n]
            at[0] += n
            if len(shape) == 1:
                return v
            names = "abcd"[:len(shape)]
            return v.rearrange(f"p ({' '.join(names)}) -> p {' '.join(names)}",
                               **{x: s for x, s in zip(names, shape)})

        eps = sm(1)
        dummies = sm(12)
        invu = sm(3).unsqueeze(2)
        Rn = sb("Rn", [128, 2, 3, 16])
        rowm = sm(3, 16)
        rowp = sm(3, 16)
        lcolu = sm(3, 16)
        eps12 = sm(1)
        stats = sm(T, 6)
        mv = sm(T, 2)
        sd = sm(T)
        rstd = sm(T)
        tsg = sm(3, 16)
        nsg = sm(3, 16)
        inv3 = sm(3).unsqueeze(2)
        sq3 = sm(3, 16)
        rs3 = sm(3, 16)
        wpT = sm(HEADS)
        convb = sm(1)
        mx = sm(T, 8)
        sme = sm(T, 8)
        rsm = sm(T, 8)
        wmax = sm(32)
        wsum = sm(32)
        wrec = sm(32)
        gst = sm(2)
        gmv = sm(2)
        gg = sm(8)
        gsc = sm(KC)
        gbi = sm(KC)
        xbar = sm(KC, IMAGES)
        sc16 = sm(EXPERTS)
        ga = sm(EXPERTS)
        g8 = sm(8)
        gi_f = sm(8)
        gone = sm(8)
        gm = sm(EXPERTS)
        sq2 = sm(32)
        sk2 = sm(32)
        lmax = sm(T)
        fcb = sm(2, FC)
        gi = sb("gi", [128, 8], U32)
        Gd = sb("Gd", [16, EXPERTS, IMAGES])
        Gb = sb("Gb", [128, EXPERTS, IMAGES])
        quarters = sm(EXPERTS, 4)
        csum = sm(EXPERTS)
        cmax = sm(EXPERTS)
        several = sm(EXPERTS)
        used_codes = sb("used_codes", [1, 1], I32)
        filled = sm(3, EXPERTS)
        fill_codes = sb("fill_codes", [1, 1], I32)
        pr = sb("pr", [128, T, EXPERTS])
        v8 = sb("v8", [128, T, 8])
        i8 = sb("i8", [128, T, 8], U32)
        i8f = sb("i8f", [128, T, 8])
        m12 = sb("m12", [128, 2, T, EXPERTS])
        rank = sb("rank", [128, 2, T, EXPERTS])
        gse = sb("gse", [128, T, EXPERTS])

        ytmp = qkT[:, :, :].rearrange("p m n -> p (m n)")[:, 0:4 * COLS].rearrange("p (i n) -> p i n", i=4)
        patT = P[:, 0:PK * IMAGES * PATCHES].rearrange("p (k n) -> p k n", k=PK)
        BD = P[:, 0:MATS * 32].rearrange("p (m c) -> p m c", m=MATS)
        S2 = P[:, 0:T * 8 * TOKENS].rearrange("p (t n) -> p t n", t=T)
        attnT = P[:, 2368:2368 + T * 512].rearrange("p (t n) -> p t n", t=T)
        BD2 = P[:, 0:32 * 32].rearrange("p (m c) -> p m c", m=32)
        oS = P[:, 3072:3072 + 32 * TOKENS].rearrange("p (m n) -> p m n", m=32)
        O = P[:, 4256:4256 + T * DIM].rearrange("p (t d) -> p t d", t=T)
        hT = [P[:, b * FC * ALLC:(b + 1) * FC * ALLC].rearrange("p (f n) -> p f n", f=FC) for b in range(2)]
        A = Q[:, 0:T * 2 * DIM].rearrange("p (t n) -> p t n", t=T)
        Gs = Q[:, 3072:5120].rearrange("p (m n) -> p m n", m=MATS)
        E = Q[:, 5120:6656].rearrange("p (a r c) -> p a r c", a=3, r=16)
        Tm = Q[:, 6656:7424].rearrange("p (a r c) -> p a r c", a=3, r=16)
        Pb = Q[:, 7424:8192]
        Pu = P[:, 0:768]
        Qblk = Q[:, :].rearrange("p (a m c x) -> p a m c x", a=2, m=16, c=CH)
        vT = Q[:, 3072:4256].rearrange("p (m n) -> p m n", m=32)
        Wm = Q[:, 4256:5280].rearrange("p (m n) -> p m n", m=32)
        qT2 = vT
        Aabs = Q[:, 4256:4256 + T * DIM].rearrange("p (t n) -> p t n", t=T)
        kvs = Q[:, 5792:6816].rearrange("p (m n) -> p m n", m=32)
        GE = EXPERTS * CAP
        disp = Q[:, 0:T * GE].rearrange("p (g e c) -> p g e c", g=T, e=EXPERTS)
        comb = Q[:, T * GE:2 * T * GE].rearrange("p (g e c) -> p g e c", g=T, e=EXPERTS)
        xinT = Q[:, 2 * T * GE:4 * T * GE].rearrange("p (k e s) -> p k e s", k=KC, e=EXPERTS)
        combT = Q[:, 4 * T * GE:4 * T * GE + 2048].rearrange("p (g a n) -> p g a n", g=T, a=2)
        BLK = M[:, 0:16 * C].rearrange("p (j c) -> p j c", j=16)
        Mx = M[:, :].rearrange("p (t c a n) -> p t c a n", t=T, c=CH, a=2)
        yT = M[:, 0:2 * T * GE].rearrange("p (k g e c) -> p k g e c", k=KC, g=T, e=EXPERTS)
        hT1 = [P[:, b * FC * SLOTS:(b + 1) * FC * SLOTS].rearrange("p (f n) -> p f n", f=FC) for b in range(2)]
        yG = P[:, 2300:2300 + T * 2 * DIM].rearrange("p (g a n) -> p g a n", g=T, a=2)
        x1q = x1T[:, :, :].rearrange("p k (q n) -> p k q n", q=4)
        accq = acc[:, :, :].rearrange("p k (q n) -> p k q n", q=4)
        Gbq = Gb[:, :, :].rearrange("p e (q i) -> p e q i", q=4)
        fcball = col[:, Q_FCB:Q_FCB + FC * EXPERTS].rearrange("p (e f) -> p e f", f=FC)
        ident = con[:, K_ID:K_ID + 128]
        id96 = con[0:C, K_ID:K_ID + C]
        idpar = con[0:C, K_ID:K_ID + C].rearrange("p (a x) -> p a x", a=PAIRS)
        parity = [con[0:C, K_PAIR + HD * i:K_PAIR + HD * i + 1] for i in range(2)]
        head = [con[0:C, K_HEAD + i:K_HEAD + i + 1] for i in range(HC)]
        eye = con[:, K_EYE:K_EYE + 256].rearrange("p (r c) -> p r c", r=16)
        XTi = XT[0:C, :, :].rearrange("p k (t a n) -> p k t a n", a=2, n=HALF)

        def xt_round(r):
            return r if r < 2 else r + 1

        def xt_bank(e, b):
            return 4 + b if e in (0, 2) else b % 2

        def qk_bank(t):
            return 2 + t % 6

        def emb_in(kc, nh):
            return PS[0:C, 4 + 2 * nh + kc, 0:8 * PATCHES].rearrange("p (x n) -> p x n", n=PATCHES)

        def emb_out(kc, nh):
            return XT[0:C, kc, nh * 512:(nh + 1) * 512].rearrange("p (x n) -> p x n", n=HALF)[:, :, 1:TOKENS]

        def x1_in(b, kc):
            return PS[0:C, 4 + b, kc * 256:(kc + 1) * 256].rearrange("p (x n) -> p x n", n=HALF)[:, :, 0:TOKENS]

        def x1_out(b, kc):
            return x1T[0:C, kc, b * 148:(b + 1) * 148].rearrange("p (x n) -> p x n", n=TOKENS)

        def cq(i, p=C, n=1):
            return col[0:p, i:i + n]

        def qb_out(a, hd):
            return Qblk[0:C, a, :, :, :].rearrange("p m c x -> p (m c) x")[:, :, hd * NCH:(hd + 1) * NCH]

        def qb_in(a):
            return qt[0:C, a * 32:a * 32 + 16, :].rearrange("p m (c n) -> p (m c) n", c=CH)

        NALL = float(IMAGES * TOKENS * DIM)
        QK_BANKS = (0, 1, 4, 5, 2, 3, 6, 7)

        s_col, s_ident, s_const, s_row, s_attw, s_ffnw, s_l1w = [
            sem(n) for n in ("s_col", "s_ident", "s_const", "s_row", "s_attw", "s_ffnw", "s_l1w")]
        s_w = [sem("s_w0"), sem("s_w1")]
        s_v = [sem("s_v0"), sem("s_v1")]
        s_patk = [sem(f"s_patk{k}") for k in range(PK)]
        s_tokw = [sem(f"s_tokw{k}") for k in range(PK)]
        dchain, achain, pchain = sem("dchain"), sem("achain"), sem("pchain")
        s_zero = sem("s_zero")
        s_emb = sem("s_emb")
        s_xpad, s_cls = sem("s_xpad"), sem("s_cls")
        s_ea, s_ed = sem("s_ea"), sem("s_ed")
        s_emt = sem("s_emt")
        s_hcopy = sem("s_hcopy")
        s_var, s_sd, s_xn = sem("s_var"), sem("s_sd"), sem("s_xn")
        s_xtp, s_xt = sem("s_xtp"), sem("s_xt")
        s_hb = sem("s_hb")
        s_tok, s_tokv = sem("s_tok"), sem("s_tokv")
        s_chan, s_chanv = sem("s_chan"), sem("s_chanv")
        s_prj, s_h = sem("s_prj"), sem("s_h")
        s_gram, s_gramv = sem("s_gram"), sem("s_gramv")
        s_et = sem("s_et")
        s_etv, s_tv = sem("s_etv"), sem("s_tv")
        s_piv, s_sq = sem("s_piv"), sem("s_sq")
        s_lc, s_inv = sem("s_lc"), sem("s_inv")
        s_blk, s_back = sem("s_blk"), sem("s_back")
        s_bda, s_bdv = sem("s_bda"), sem("s_bdv")
        s_qt = sem("s_qt")
        s_qea, s_qed = sem("s_qea"), sem("s_qed")
        s_qba, s_qbv = sem("s_qba"), sem("s_qbv")
        s_qbp = sem("s_qbp")
        s_mixw, s_mixr, s_mix1 = sem("s_mixw"), sem("s_mixr"), sem("s_mix1")
        s_dots, s_s2 = sem("s_dots"), sem("s_s2")
        s_mixp, s_mixe = sem("s_mixp"), sem("s_mixe")
        s_sub, s_exp, s_att = sem("s_sub"), sem("s_exp"), sem("s_att")
        s_atp, s_atT = sem("s_atp"), sem("s_atT")
        s_av, s_oT = sem("s_av"), sem("s_oT")
        s_w_ps, s_wsub, s_wexp, s_wT = [
            sem(n) for n in ("s_w_ps", "s_wsub", "s_wexp", "s_wT")]
        s_wv, s_os = sem("s_wv"), sem("s_os")
        s_scr = [sem("s_scr0"), sem("s_scr1")]
        s_scr2 = sem("s_scr2")
        s_w2p, s_zb, s_s = sem("s_w2p"), sem("s_zb"), sem("s_s")
        s_gst, s_gps, s_gva, s_gsd, s_gsc = [
            sem(n) for n in ("s_gst", "s_gps", "s_gva", "s_gsd", "s_gsc")]
        s_x1p, s_x1 = sem("s_x1p"), sem("s_x1")
        s_x2, s_x2p = sem("s_x2"), sem("s_x2p")
        s_xbar, s_rps, s_nm, s_ge = [
            sem(n) for n in ("s_xbar", "s_rps", "s_nm", "s_ge")]
        s_gd, s_gbp, s_gb = sem("s_gd"), sem("s_gbp"), sem("s_gb")
        s_used = sem("s_used")
        s_fcb = sem("s_fcb")
        s_hp, s_gelu = sem("s_hp"), sem("s_gelu")
        s_yp = sem("s_yp")
        s_ytmp, s_acc, s_bst = sem("s_ytmp"), sem("s_acc"), sem("s_bst")
        s_q2, s_q2e = sem("s_q2"), sem("s_q2e")
        s_kv2, s_kv2e = sem("s_kv2"), sem("s_kv2e")
        s_kvp, s_kvm, s_bd3 = sem("s_kvp"), sem("s_kvm"), sem("s_bd3")
        s_o2, s_o2e = sem("s_o2"), sem("s_o2e")
        s_lg, s_lsub, s_lexp = sem("s_lg"), sem("s_lsub"), sem("s_lexp")
        s_m12, s_rk = sem("s_m12"), sem("s_rk")
        s_filled = sem("s_filled")
        s_disp, s_comb = sem("s_disp"), sem("s_comb")
        s_xip, s_xin = sem("s_xip"), sem("s_xin")
        s_ctp, s_ct = sem("s_ctp"), sem("s_ct")
        s_h1p, s_relu = sem("s_h1p"), sem("s_relu")
        s_edone, s_y1 = sem("s_edone"), sem("s_y1")
        s_ygp, s_yg = sem("s_ygp"), sem("s_yg")
        s_fin, s_res = sem("s_fin"), sem("s_res")
        s_out = sem("s_out")

        def code_of(codes, expert):
            return (codes >> (expert * 3)) & 7

        def quarter_of(codes, expert):
            return (code_of(codes, expert) - 1).with_bounds(min_val=0, max_val=3)

        block = ctx.enter_context(nc.Block())

        @block.sync
        def _(sp):
            for k in range(PK):
                sp.dma_start(tokw[:, k, :], tok_w[:, k, :]).then_inc(s_tokw[k], 16)
                sp.dma_start(patT[:, k, :], patches[:, k, :]).then_inc(s_patk[k], 16)
            sp.dma_start(col[:, :], cols[:, :]).then_inc(s_col, 16)
            sp.dma_start(con[:, 0:K_TRI], consts[:, 0:K_TRI]).then_inc(s_ident, 16)
            sp.dma_start(con[:, K_TRI:K_ALL], consts[:, K_TRI:K_ALL]).then_inc(s_const, 16)
            sp.dma_start(row[:, :], rows.partition_broadcast(128)).then_inc(s_row, 16)
            sp.dma_start(qkvw[0:C, :, :], qkv_w[:, :, :]).then_inc(s_attw, 16)
            sp.dma_start(projw[0:C, :, :], proj_w[:, :, :]).then_inc(s_attw, 16)
            sp.dma_start(w1w[0:C, :, :], w1[:, :, :]).then_inc(s_ffnw, 16)
            sp.dma_start(w2w[0:C, :, :], w2[:, :, :]).then_inc(s_ffnw, 16)
            sp.dma_start(rw[0:C, :, :], r_w[:, :, :]).then_inc(s_ffnw, 16)
            for b in range(2):
                sp.dma_start(wi_sb[0:C, b, :], fc_w[b, :, :]).then_inc(s_w[b], 16)
                sp.dma_start(wo_sb[:, b, :], pr_w[b, :, :]).then_inc(s_v[b], 16)
            sp.dma_start(qkv2w[0:C, :, :], qkv2_w[:, :, :]).then_inc(s_l1w, 16)
            sp.dma_start(proj2w[0:C, :, :], proj2_w[:, :, :]).then_inc(s_l1w, 16)
            sp.dma_start(routw[0:C, :, :], router_w[:, :, :]).then_inc(s_l1w, 16)

            for i in range(4):
                a, kc = divmod(i, 2)
                sp.wait_ge(s_os, i + 1)
                sp.dma_start(scratch[:, a, kc].rearrange("t p n -> p t n"),
                             oS[0:C, i * 8:(i + 1) * 8, :]).then_inc(s_scr[a], 16)
            sp.wait_ge(s_zero, 6)
            back = scratch.rearrange("t a k p n -> t a (k p n)").rearrange("t a (m d) -> a m t d", d=DIM)
            for a in range(2):
                sp.wait_ge(s_scr[a], 32)
                sp.dma_start(O[a * HALF:a * HALF + 36, :, :], back[a, 0:36]).then_inc(s_scr2, 16)
                sp.dma_start(O[a * HALF + 36:a * HALF + 37, :, :], back[a, 36:37]).then_inc(s_scr2, 16)

            for b in range(2):
                sp.wait_ge(s_w[b], 16)
                sp.wait_ge(s_v[b], 16)
            sp.wait_ge(s_used, 1)
            codes = sp.value_load(used_codes[0:1, 0:1], min_val=0, max_val=8 ** EXPERTS - 1)
            with sp.Fori(1, EXPERTS // 2) as it:
                for b in range(2):
                    with sp.If(code_of(codes, it * 2 + b) != 0):
                        sp.wait_ge(s_yp, it * 8 + (4 * b - 4))
                        sp.dma_start(wi_sb[0:C, b, :], fc_w[it * 2 + b, :, :]).then_inc(s_w[b], 16)
                        sp.dma_start(wo_sb[:, b, :], pr_w[it * 2 + b, :, :]).then_inc(s_v[b], 16)
                    with sp.Else():
                        sp.wait_ge(s_yp, it * 8 + (4 * b - 4))
                        sp.sem_inc(s_w[b], 16)
                        sp.sem_inc(s_v[b], 16)
            for b in range(2):
                sp.wait_ge(s_yp, 4 * (EXPERTS + b - 1))
                sp.dma_start(wi_sb[0:C, b, :], wi[b, :, :]).then_inc(s_w[b], 16)
                sp.dma_start(wo_sb[:, b, :], wo[b, :, :]).then_inc(s_v[b], 16)
            with sp.Fori(1, EXPERTS // 2) as it:
                for b in range(2):
                    sp.wait_ge(s_edone, it * 2 + b)
                    sp.dma_start(wi_sb[0:C, b, :], wi[it * 2 + b, :, :]).then_inc(s_w[b], 16)
                    sp.dma_start(wo_sb[:, b, :], wo[it * 2 + b, :, :]).then_inc(s_v[b], 16)

            for t in range(T):
                sp.wait_ge(s_res, t + 1)
                for a in range(2):
                    sp.dma_start(out[2 * t + a, :, :], h[a * HALF:a * HALF + TOKENS, t, :]).then_inc(s_out, 16)
            sp.wait_ge(s_out, 16 * IMAGES)

        @block.gpsimd
        def _(po):
            n = [0]

            def link(ins):
                n[0] += 1
                ins.then_inc(pchain, 1)
                po.wait_ge(pchain, n[0])

            po.memset(eps, 1e-5)
            po.memset(eps12, 1e-12).then_inc(s_zero, 1)
            for kc in range(KC):
                last = po.memset(XTi[:, kc, :, :, TOKENS:HALF], 0.0)
            last.then_inc(s_xpad, 1)
            po.memset(vpad[:, :, :], 0.0).then_inc(s_zero, 1)
            po.memset(qkT[:, :, :], 0.0).then_inc(s_zero, 1)
            po.memset(mixT[:, :, :], 0.0).then_inc(s_zero, 1)
            po.memset(BLK, 0.0).then_inc(s_zero, 1)
            po.wait_ge(s_col, 16)
            for kc in range(KC):
                last = po.tensor_copy(XTi[:, kc, :, :, 0:1].rearrange("p t a n -> p (t a) n"),
                                      bc(col[0:C, Q_CLS + kc:Q_CLS + kc + 1], 1, IMAGES))
            last.then_inc(s_cls, 1)
            po.wait_ge(s_const, 16)
            for a in range(3):
                last = po.tensor_copy(E[:, a, :, 16:32], eye)
            last.then_inc(s_etv, 1)
            po.wait_ge(s_row, 16)
            po.wait_ge(s_xn, T)
            po.tensor_tensor(h[:, :, :], h[:, :, :], bc(row[:, R_PROJB:R_PROJB + DIM], 1, T), ALU.add).then_inc(s_hb, 1)
            F = E[:, :, :, 16:32]
            for s in range(15):
                re = 15 - s
                po.wait_ge(s_lc, s + 1)
                prod = Pf[:, 0:3 * re * (s + 1)].rearrange("p (a r c) -> p a r c", a=3, r=re)
                below = F[:, :, s + 1:16, 0:s + 1]
                link(po.tensor_tensor(prod, bc(Lc[:, s, :, 0:re], 3, s + 1), bc(F[:, :, s, 0:s + 1], 2, re), ALU.mult))
                link(po.tensor_tensor(below, below, prod, ALU.subtract))
            po.sem_inc(s_inv, 1)
            po.wait_ge(s_back, 1)
            po.memset(Qblk[0:C, :, :, :, 60:64].rearrange("p a m c x -> p (a m c) x"), 0.0).then_inc(s_qbp, 1)
            po.memset(M[:, :].rearrange("p (x n) -> p x n", n=64)[:, :, 37:64], 0.0).then_inc(s_qbp, 1)
            po.wait_ge(s_av, 2)
            po.memset(O, 0.0).then_inc(s_zero, 1)
            po.wait_ge(s_xt, 8)
            po.tensor_tensor(xn[:, :, :], xn[:, :, :], bc(row[:, R_W2B:R_W2B + DIM], 1, T), ALU.add).then_inc(s_zb, 1)
            po.wait_ge(s_xn, 3 * T)
            po.tensor_tensor(h[:, :, :], h[:, :, :], bc(row[:, R_BP:R_BP + DIM], 1, T), ALU.add).then_inc(s_hb, 1)

        @block.tensor
        def _(pe):
            def keep_clock(bank, count):
                for _ in range(count):
                    pe.matmul(PS[:, bank, 0:128], ident, ident, start=True, stop=True)

            def transposes(r, tiles=range(T)):
                for t in tiles:
                    pe.wait_ge(s_xn, r * T + t + 1)
                    if r >= 1 and t >= 4:
                        pe.wait_ge(s_xt, 4 * xt_round(r) + t // 2 - 1)
                    for kc in range(KC):
                        last = pe.transpose(PS[0:C, xt_bank(xt_round(r), t // 2),
                                               kc * 256 + (t % 2) * 128:kc * 256 + (t % 2) * 128 + 128],
                                            xn[:, t, kc * C:(kc + 1) * C], ident)
                    if t % 2:
                        last.then_inc(s_xtp, 1)

            def projection(ready, per_half, w):
                for t in range(T):
                    if t % 4 == 0:
                        pe.wait_ge(ready, per_half * (t // 4 + 1))
                    for kc in range(KC):
                        last = pe.matmul(PS[:, t, 0:DIM], XT[0:C, kc, t * 128:(t + 1) * 128], w[0:C, kc, :],
                                         start=(kc == 0), stop=(kc == 1))
                    last.then_inc(s_prj, 1)

            for k in range(PK):
                pe.wait_ge(s_tokw[k], 16)
                pe.wait_ge(s_patk[k], 16)
                for nh in range(2):
                    for kc in range(KC):
                        last = pe.matmul(PS[0:C, 4 + 2 * nh + kc, 0:8 * PATCHES], tokw[:, k, kc * C:(kc + 1) * C],
                                         patT[:, k, nh * 8 * PATCHES:(nh + 1) * 8 * PATCHES],
                                         start=(k == 0), stop=(k == PK - 1))
                        if k == PK - 1:
                            last.then_inc(s_emb, 1)
            pe.wait_ge(s_ident, 16)
            pe.wait_ge(s_cls, 1)
            pe.wait_ge(s_xpad, 1)
            for t in range(T):
                pe.wait_ge(s_ea, t // 4 + 1)
                pe.wait_ge(s_ed, t // 4 + 1)
                if t >= 4:
                    pe.wait_ge(s_hcopy, t - 3)
                for kc in range(KC):
                    last = pe.matmul(PS[:, t % 4, kc * C:(kc + 1) * C], XT[0:C, kc, t * 128:(t + 1) * 128], id96,
                                     start=True, stop=True, is_transpose=True)
                last.then_inc(s_emt, 1)
            pe.wait_ge(s_const, 16)
            pe.wait_ge(s_mixw, 1)
            pe.matmul(PS[:, 7, 0:HEADS], con[0:HEADS, K_E1:K_E1 + 128], wpT[0:HEADS, :], start=True, stop=True)
            pe.matmul(PS[:, 7, HEADS:HEADS + 1], con[0:HEADS, K_E1:K_E1 + 128], col[0:HEADS, Q_CB:Q_CB + 1],
                      start=True, stop=True).then_inc(s_mixr, 1)
            transposes(0, range(4))
            pe.wait_ge(s_attw, 32)
            pe.wait_ge(s_hcopy, T)

            for t in range(T + 1):
                if t == 2:
                    pe.wait_ge(s_mix1, 1)
                    transposes(0, range(4, T))
                if t < T:
                    pe.wait_ge(s_xt, t // 2 + 1)
                    if t >= 2:
                        pe.wait_ge(s_tokv, t - 1)
                    for kc in range(KC):
                        pe.matmul(PS[:, t % 2, 0:2 * DIM], XT[0:C, kc, t * 128:(t + 1) * 128],
                                  qkvw[0:C, kc, 0:2 * DIM], start=(kc == 0), stop=(kc == 1))
                    for kc in range(KC):
                        last = pe.matmul(PS[:, 2 + t % 2, 0:DIM], XT[0:C, kc, t * 128:(t + 1) * 128],
                                         qkvw[0:C, kc, 2 * DIM:3 * DIM], start=(kc == 0), stop=(kc == 1))
                    last.then_inc(s_tok, 1)
                if t >= 1:
                    u = t - 1
                    pe.wait_ge(s_tokv, u + 1)
                    if u < 4:
                        pe.wait_ge(s_xt, u + 1)
                    else:
                        pe.wait_ge(s_chanv, u - 3)
                    for i in range(4):
                        last = pe.transpose(PS[0:C, 4 + u % 4, i * 128:(i + 1) * 128], A[:, u, i * C:(i + 1) * C], ident)
                    last.then_inc(s_chan, 1)
            pe.wait_ge(s_tokv, T)
            for a in range(2):
                for qk in range(2):
                    s = a * 2 + qk
                    for kc in range(KC):
                        for t in range(T):
                            for j in range(PAIRS):
                                v = A[a * HALF:a * HALF + TOKENS, t, (qk * 2 + kc) * C + 32 * j:(qk * 2 + kc) * C + 32 * j + 32]
                                last = pe.matmul(PS[32 * j:32 * j + 32, s, (kc * 8 + t) * 32:(kc * 8 + t) * 32 + 32],
                                                 v, v, start=True, stop=True)
                    last.then_inc(s_gram, 1)
            def top_rows(rows):
                for r in rows:
                    for par in range(2):
                        last = pe.matmul(PS[par * 64:par * 64 + 64, 4 + r // 8, (r % 8) * 48:(r % 8) * 48 + 48],
                                         qkT[0:C, :, r], idpar[:, :, par * 16:par * 16 + 16], start=True, stop=True)
                    if r % 8 == 7:
                        last.then_inc(s_et, 1)

            pe.wait_ge(s_chanv, T)
            top_rows(range(3))
            pe.wait_ge(s_gramv, 4)
            for r in range(16):
                for par in range(2):
                    last = pe.matmul(PS[par * 64:par * 64 + 64, 6 + r // 8, (r % 8) * 48:(r % 8) * 48 + 48],
                                     Gs[0:C, :, par * 16 + r], idpar[:, :, par * 16:par * 16 + 16],
                                     start=True, stop=True)
                if r % 8 == 7:
                    last.then_inc(s_et, 1)
            top_rows(range(3, 16))
            for step in (14, 15):
                pe.wait_ge(s_lc, step)
                keep_clock(3, 8)
            pe.wait_ge(s_blk, 1)
            for j in range(16):
                for p in range(PAIRS):
                    last = pe.matmul(PS[32 * p:32 * p + 32, j // 8, (j % 8) * 64:(j % 8) * 64 + 64],
                                     BLK[:, j, 32 * p:32 * p + 32], con[:, K_II:K_II + 64], start=True, stop=True)
            last.then_inc(s_back, 1)
            pe.wait_ge(s_bda, 1)
            pe.wait_ge(s_bdv, 1)
            for b in QK_BANKS:
                for i in range(8):
                    m = b * 8 + i
                    for p in range(PAIRS):
                        last = pe.matmul(PS[32 * p:32 * p + 32, b, i * NP:(i + 1) * NP],
                                         BD[32 * p:32 * p + 32, m, :], qkT[32 * p:32 * p + 32, m, :], start=True, stop=True)
                last.then_inc(s_qt, 1)
            pe.wait_ge(s_qea, 4)
            pe.wait_ge(s_qed, 4)
            pe.wait_ge(s_qba, 2)
            pe.wait_ge(s_qbv, 2)
            pe.wait_ge(s_qbp, 2)
            for t in range(T + 1):
                if t < T:
                    if t >= 4:
                        pe.wait_ge(s_mixe, t - 3)
                    for c in range(CH):
                        for a in range(2):
                            for kc in range(KC):
                                last = pe.matmul(
                                    PS[kc * 64:kc * 64 + 64, t % 4, (c * 2 + a) * TOKENS:(c * 2 + a + 1) * TOKENS],
                                    Qblk[0:C, a, kc * 8 + t, c, :], qt[0:C, a * 32 + 16 + kc * 8 + t, 0:TOKENS],
                                    start=True, stop=True)
                    last.then_inc(s_dots, 1)
                if t >= 1:
                    pe.wait_ge(s_s2, t)
                    pe.matmul(PS[:, (t - 1) % 4, 0:8 * TOKENS], mixT[:, :, :].rearrange("p k x -> p (k x)"),
                              S2[:, t - 1, :], start=True, stop=True).then_inc(s_mixp, 1)
            for t in range(T + 1):
                if t < T:
                    pe.wait_ge(s_att, t // 2 + 1)
                    if t >= 2:
                        pe.wait_ge(s_atT, t - 1)
                    for c in range(CH):
                        last = pe.transpose(PS[:, 4 + t % 2, c * 128:(c + 1) * 128],
                                            Mx[:, t, c].rearrange("p a n -> p (a n)"), ident)
                    last.then_inc(s_atp, 1)
                if t >= 1:
                    u = t - 1
                    pe.wait_ge(s_atT, u + 1)
                    if u == 4:
                        pe.wait_ge(s_oT, 2)
                    rhs = attnT[:, u, :].rearrange("p (c x) -> p c x", c=CH)
                    for kc in range(KC):
                        for par in range(2):
                            for j in range(PAIRS):
                                for a in range(2):
                                    c0 = (kc * PAIRS + j) * 64 + par * 16
                                    r0 = kc * 64 + (2 * j + par) * NCH
                                    o0 = (kc * 4 + u % 4) * NP
                                    last = pe.matmul(PS[32 * j:32 * j + 32, 6 + a, o0:o0 + NP],
                                                     vpad[a * HALF:a * HALF + TOKENS, u, c0:c0 + 32],
                                                     rhs[a * HALF:a * HALF + TOKENS, :, r0:r0 + NCH],
                                                     start=(par == 0), stop=(par == 1))
                    if u % 4 == 3:
                        last.then_inc(s_av, 1)
            projection(s_oT, 2, projw)

            transposes(1, range(4))
            pe.wait_ge(s_ffnw, 48)
            for t in range(T):
                if t == 2:
                    transposes(1, range(4, T))
                pe.wait_ge(s_xt, 4 + t // 2 + 1)
                if t >= 6:
                    pe.wait_ge(s_tokv, T + t - 5)
                else:
                    pe.wait_ge(s_h, t + 3)
                for kc in range(KC):
                    last = pe.matmul(PS[:, qk_bank(t), 0:2 * DIM], XT[0:C, kc, t * 128:(t + 1) * 128],
                                     w1w[0:C, kc, 0:2 * DIM], start=(kc == 0), stop=(kc == 1))
                last.then_inc(s_tok, 1)
            for i in range(4):
                a, kc = divmod(i, 2)
                pe.wait_ge(s_tokv, T + i + 3)
                for k in range(KC):
                    last = pe.matmul(PS[0:C, 4 + i, 0:COLS], w1w[0:C, k, 2 * DIM + kc * C:2 * DIM + (kc + 1) * C],
                                     XTi[:, k, :, a, 0:TOKENS], start=(k == 0), stop=(k == 1))
                last.then_inc(s_chan, 1)
            pe.wait_ge(s_tokv, 2 * T)
            for a in range(2):
                for kc in range(KC):
                    for t in range(T):
                        for j in range(PAIRS):
                            q0 = kc * C + 32 * j
                            last = pe.matmul(PS[32 * j:32 * j + 32, a, (kc * 8 + t) * 32:(kc * 8 + t) * 32 + 32],
                                             A[a * HALF:a * HALF + TOKENS, t, q0:q0 + 32],
                                             A[a * HALF:a * HALF + TOKENS, t, DIM + q0:DIM + q0 + 32],
                                             start=True, stop=True)
                last.then_inc(s_w_ps, 1)
            pe.wait_ge(s_chanv, 12)
            for b in range(4):
                pe.wait_ge(s_wT, b // 2 + 1)
                for i in range(8):
                    m = b * 8 + i
                    for p in range(PAIRS):
                        last = pe.matmul(PS[32 * p:32 * p + 32, 2 + b, i * TOKENS:(i + 1) * TOKENS],
                                         BD2[32 * p:32 * p + 32, m, :], vT[32 * p:32 * p + 32, m, :], start=True, stop=True)
                last.then_inc(s_wv, 1)
            keep_clock(6, 20)
            pe.wait_ge(s_scr2, 64)
            for t in range(T):
                for kc in range(KC):
                    last = pe.transpose(PS[0:C, 4 + t // 2, kc * 256 + (t % 2) * 128:kc * 256 + (t % 2) * 128 + 128],
                                        O[:, t, kc * C:(kc + 1) * C], ident)
                if t % 2:
                    last.then_inc(s_xtp, 1)
            for t in range(T):
                pe.wait_ge(s_xt, 8 + t // 2 + 1)
                if t >= 4:
                    pe.wait_ge(s_s, t - 3)
                for kc in range(KC):
                    last = pe.matmul(PS[:, t % 4, 0:DIM], XT[0:C, kc, t * 128:(t + 1) * 128], w2w[0:C, kc, :],
                                     start=(kc == 0), stop=(kc == 1))
                last.then_inc(s_w2p, 1)
            pe.wait_ge(s_xt, 12)
            for t in range(T):
                pe.wait_ge(s_s, t + 1)
                for kc in range(KC):
                    last = pe.transpose(PS[0:C, 4 + t // 2, kc * 256 + (t % 2) * 128:kc * 256 + (t % 2) * 128 + 128],
                                        xn[:, t, kc * C:(kc + 1) * C], ident)
            last.then_inc(s_x1p, 1)
            pe.wait_ge(s_gst, 1)
            pe.matmul(PS[:, 0, 0:2], con[:, K_MEANV:K_MEANV + 128], gst, start=True, stop=True).then_inc(s_gps, 1)
            pe.wait_ge(s_xbar, 1)
            for kc in range(KC):
                last = pe.matmul(PS[0:IMAGES, 1, 0:EXPERTS], xbar[0:C, kc, :], rw[0:C, kc, :],
                                 start=(kc == 0), stop=(kc == 1))
            last.then_inc(s_rps, 1)
            keep_clock(3, 6)
            pe.wait_ge(s_gd, 1)
            pe.matmul(PS[0:C, 2, 0:128], con[0:IMAGES, K_ONE:K_ONE + C], Gd[:, :, :].rearrange("p e b -> p (e b)"),
                      start=True, stop=True).then_inc(s_gbp, 1)
            pe.wait_ge(s_gb, 1)

            pe.wait_ge(s_used, 1)
            codes = pe.value_load(used_codes[0:1, 0:1], min_val=0, max_val=8 ** EXPERTS - 1)
            with pe.Fori(0, EXPERTS // 2) as it:
                with pe.If(((codes >> (it * 6)) & 63) != 0):
                    for b in range(2):
                        with pe.If(code_of(codes, it * 2 + b) > 4):
                            pe.wait_ge(s_w[b], it * 16 + 16)
                            for i in range(2 * FC):
                                f, nh = divmod(i, 2)
                                if i >= 4:
                                    pe.wait_ge(s_gelu, it * 24 + (b * 12 + i - 3))
                                for kc in range(KC):
                                    last = pe.matmul(PS[:, i % 4, 0:COLS],
                                                     wi_sb[0:C, b, kc * FF + f * 128:kc * FF + (f + 1) * 128],
                                                     x1T[0:C, kc, nh * COLS:(nh + 1) * COLS], start=(kc == 0), stop=(kc == 1))
                                last.then_inc(s_hp, 1)
                            pe.wait_ge(s_v[b], it * 16 + 16)
                            pe.wait_ge(s_acc, it * 8 + (4 * b + 1))
                            for i in range(4):
                                kc, nh = divmod(i, 2)
                                for f in range(FC):
                                    if i == 0:
                                        pe.wait_ge(s_gelu, it * 24 + (b * 12 + 2 * f + 2))
                                    last = pe.matmul(PS[0:C, 4 + i, 0:COLS],
                                                     wo_sb[:, b, f * DIM + kc * C:f * DIM + (kc + 1) * C],
                                                     hT[b][:, f, nh * COLS:(nh + 1) * COLS],
                                                     start=(f == 0), stop=(f == FC - 1))
                                last.then_inc(s_yp, 1)
                        with pe.Else():
                            with pe.If(code_of(codes, it * 2 + b) != 0):
                                pe.wait_ge(s_w[b], it * 16 + 16)
                                quarter = quarter_of(codes, it * 2 + b)
                                for f in range(FC):
                                    if f >= 4:
                                        pe.wait_ge(s_gelu, it * 24 + (b * 12 + 2 * f - 6))
                                    for kc in range(KC):
                                        last = pe.matmul(PS[:, f % 4, 0:QCOLS],
                                                         wi_sb[0:C, b, kc * FF + f * 128:kc * FF + (f + 1) * 128],
                                                         x1q[0:C, kc, quarter, :], start=(kc == 0), stop=(kc == 1))
                                    last.then_inc(s_hp, 2)
                                pe.wait_ge(s_v[b], it * 16 + 16)
                                pe.wait_ge(s_acc, it * 8 + (4 * b + 1))
                                for kc in range(KC):
                                    for f in range(FC):
                                        if kc == 0:
                                            pe.wait_ge(s_gelu, it * 24 + (b * 12 + 2 * f + 2))
                                        last = pe.matmul(PS[0:C, 4 + kc, 0:QCOLS],
                                                         wo_sb[:, b, f * DIM + kc * C:f * DIM + (kc + 1) * C],
                                                         hT[b][:, f, 0:QCOLS], start=(f == 0), stop=(f == FC - 1))
                                    last.then_inc(s_yp, 2)
                            with pe.Else():
                                pe.drain().then_inc(s_hp, 2 * FC)
                                pe.sem_inc(s_yp, 4)
                with pe.Else():
                    pe.drain().then_inc(s_hp, 2 * 2 * FC)
                    pe.sem_inc(s_yp, 2 * 4)

            pe.sem_inc(s_edone, 1)

            pe.wait_ge(s_gst, 2)
            pe.matmul(PS[:, 0, 0:2], con[0:C, K_MEANC:K_MEANC + 128], gst[0:C], start=True, stop=True).then_inc(s_gps, 1)
            pe.wait_ge(s_x2, 2)
            for t in range(T):
                for kc in range(KC):
                    last = pe.matmul(PS[:, t, kc * C:(kc + 1) * C], XT[0:C, kc, t * 128:(t + 1) * 128], id96,
                                     start=True, stop=True, is_transpose=True)
                last.then_inc(s_x2p, 1)

            def k_v(tiles):
                for t in tiles:
                    pe.wait_ge(s_xt, 12 + t // 2 + 1)
                    if t >= 6:
                        pe.wait_ge(s_kv2e, t - 5)
                    else:
                        pe.wait_ge(s_h, T + t + 3)
                    for kc in range(KC):
                        last = pe.matmul(PS[:, qk_bank(t), 0:2 * DIM], XT[0:C, kc, t * 128:(t + 1) * 128],
                                         qkv2w[0:C, kc, DIM:3 * DIM], start=(kc == 0), stop=(kc == 1))
                    last.then_inc(s_kv2, 1)

            transposes(2, range(4))
            pe.wait_ge(s_l1w, 48)
            k_v(range(3))
            transposes(2, range(4, T))
            k_v(range(3, 4))
            pe.wait_ge(s_xt, 16)
            for i in range(4):
                a, kc = divmod(i, 2)
                if a:
                    pe.wait_ge(s_kv2e, 3 + kc)
                for k in range(KC):
                    last = pe.matmul(PS[0:C, 4 * a + kc, 0:COLS], qkv2w[0:C, k, kc * C:(kc + 1) * C],
                                     XTi[:, k, :, a, 0:TOKENS], start=(k == 0), stop=(k == 1))
                last.then_inc(s_q2, 1)
            k_v(range(4, T))
            pe.wait_ge(s_q2e, 3)
            for t in range(T):
                pe.wait_ge(s_kv2e, t + 1)
                for kc in range(KC):
                    last = pe.matmul(PS[0:C, 4, (kc * 8 + t) * 2:(kc * 8 + t) * 2 + 2],
                                     Aabs[:, t, kc * C:(kc + 1) * C], con[:, K_HALF:K_HALF + 2], start=True, stop=True)
            last.then_inc(s_kvp, 1)
            pe.wait_ge(s_q2e, 2)
            for a in range(2):
                for kc in range(KC):
                    for t in range(T):
                        for j in range(PAIRS):
                            k0 = kc * C + 32 * j
                            last = pe.matmul(PS[32 * j:32 * j + 32, a, (kc * 8 + t) * 32:(kc * 8 + t) * 32 + 32],
                                             A[a * HALF:a * HALF + TOKENS, t, k0:k0 + 32],
                                             A[a * HALF:a * HALF + TOKENS, t, DIM + k0:DIM + k0 + 32],
                                             start=True, stop=True)
                last.then_inc(s_kvm, 1)
            pe.wait_ge(s_q2e, 4)
            for b in range(4):
                pe.wait_ge(s_bd3, b // 2 + 1)
                for i in range(8):
                    m = b * 8 + i
                    for p in range(PAIRS):
                        last = pe.matmul(PS[32 * p:32 * p + 32, 4 + b, i * TOKENS:(i + 1) * TOKENS],
                                         BD2[32 * p:32 * p + 32, m, :], qT2[32 * p:32 * p + 32, m, :], start=True, stop=True)
                last.then_inc(s_o2, 1)
            pe.wait_ge(s_o2e, 4)
            projection(s_o2e, 2, proj2w)

            transposes(3, range(4))
            for t in range(T):
                if t == 4:
                    transposes(3, range(4, T))
                if t == 0:
                    pe.wait_ge(s_h, 2 * T + 3)
                pe.wait_ge(s_xt, 16 + t // 2 + 1)
                for kc in range(KC):
                    last = pe.matmul(PS[:, 2, t * 8:t * 8 + 8], XT[0:C, kc, t * 128:(t + 1) * 128], routw[0:C, kc, :],
                                     start=(kc == 0), stop=(kc == 1))
            last.then_inc(s_lg, 1)
            keep_clock(3, 14)
            pe.wait_ge(s_m12, 1)
            f1 = m12[:, 0].rearrange("p g e -> p (g e)")
            f2 = m12[:, 1].rearrange("p g e -> p (g e)")
            pe.matmul(PS[:, 5, 0:64], con[:, K_TRI:K_TRI + 128], f1, start=True, stop=True)
            pe.matmul(PS[:, 5, 64:128], con[:, K_ONE:K_ONE + 128], f1, start=True, stop=False)
            pe.matmul(PS[:, 5, 64:128], con[:, K_TRI:K_TRI + 128], f2, start=False, stop=True).then_inc(s_rk, 1)
            pe.matmul(PS[:, 6, 0:64], con[:, K_ONE:K_ONE + 128], f1, start=True, stop=False)
            pe.matmul(PS[:, 6, 0:64], con[:, K_ONE:K_ONE + 128], f2, start=False, stop=True).then_inc(s_rk, 1)
            for g in range(T):
                pe.wait_ge(s_disp, g // 4 + 1)
                for kc in range(KC):
                    last = pe.matmul(PS[0:C, g, kc * GE:(kc + 1) * GE], xn[:, g, kc * C:(kc + 1) * C],
                                     disp[:, g].rearrange("p e c -> p (e c)"), start=True, stop=True)
                last.then_inc(s_xip, 1)
            pe.wait_ge(s_comb, 1)
            for b in range(4):
                pe.wait_ge(s_xin, b + 5)
                for i in range(4):
                    g, hf = 2 * b + i // 2, i % 2
                    src = comb[:, g].rearrange("p e c -> p (e c)")[:, hf * 92:(hf + 1) * 92]
                    last = pe.transpose(PS[0:92, 4 + b, i * 128:(i + 1) * 128], src, ident)
                last.then_inc(s_ctp, 1)
            pe.wait_ge(s_xin, 8)
            pe.wait_ge(s_filled, 1)
            fills = pe.value_load(fill_codes[0:1, 0:1], min_val=0, max_val=4 ** EXPERTS - 1)

            def expert(it, b, n):
                for i in range(3):
                    for u in range(2):
                        f = 2 * i + u
                        for kc in range(KC):
                            last = pe.matmul(PS[:, 3 * b + i, u * SLOTS:u * SLOTS + n * T],
                                             wi_sb[0:C, b, kc * FF + f * 128:kc * FF + (f + 1) * 128],
                                             xinT[0:C, kc, it * 2 + b, 0:n * T], start=(kc == 0), stop=(kc == 1))
                    last.then_inc(s_h1p, 1)
                pe.wait_ge(s_v[b], it * 16 + 80)
                pe.wait_ge(s_ct, 4)
                pe.wait_ge(s_y1, it * 2 + (b + 1))
                for kc in range(KC):
                    for f in range(FC):
                        if kc == 0 and f % 2 == 0:
                            pe.wait_ge(s_relu, it * 6 + (3 * b + f // 2 + 1))
                        last = pe.matmul(PS[0:C, 6 + b, kc * SLOTS:kc * SLOTS + n * T],
                                         wo_sb[:, b, f * DIM + kc * C:f * DIM + (kc + 1) * C],
                                         hT1[b][:, f, 0:n * T], start=(f == 0), stop=(f == FC - 1))
                last.then_inc(s_edone, 1)

            with pe.Fori(0, EXPERTS // 2) as it:
                for b in range(2):
                    pe.wait_ge(s_w[b], it * 16 + 80)
                    fill = (fills >> ((it * 2 + b) * 2)) & 3
                    with pe.If(fill > 1):
                        expert(it, b, CAP)
                    with pe.Else():
                        with pe.If(fill > 0):
                            expert(it, b, FILL[1])
                        with pe.Else():
                            expert(it, b, FILL[0])
            pe.wait_ge(s_y1, EXPERTS + 2)
            for g in range(T):
                for hf in range(2):
                    for kc in range(KC):
                        src = yT[0:C, kc, g].rearrange("p e c -> p (e c)")[:, hf * 92:(hf + 1) * 92]
                        last = pe.matmul(PS[0:92, g, hf * DIM + kc * C:hf * DIM + (kc + 1) * C], src, id96,
                                         start=True, stop=True, is_transpose=True)
                last.then_inc(s_ygp, 1)
            for g in range(T):
                pe.wait_ge(s_yg, g + 1)
                for hf in range(2):
                    last = pe.matmul(PS[:, g, 0:DIM], combT[0:92, g, hf, :], yG[0:92, g, hf, :],
                                     start=(hf == 0), stop=(hf == 1))
                last.then_inc(s_fin, 1)

        @block.scalar
        def _(ac):
            n = [0]

            def link(ins):
                n[0] += 1
                ins.then_inc(achain, 1)
                ac.wait_ge(achain, n[0])

            def evac_xt(r, banks):
                for b in banks:
                    ac.wait_ge(s_xtp, r * 4 + b + 1)
                    ac.activation(XT[0:C, :, b * 256:(b + 1) * 256],
                                  PS[0:C, xt_bank(r, b), :].rearrange("p (k x) -> p k x", k=KC), ACT.Copy).then_inc(s_xt, 1)

            def sqrt_ln(r, hf):
                ac.wait_ge(s_var, 2 * r + hf + 1)
                ac.activation(sd[:, 4 * hf:4 * hf + 4], mv[:, 4 * hf:4 * hf + 4, 1], ACT.Sqrt, bias=eps).then_inc(s_sd, 1)

            preloads = [0]

            def preload(func):
                preloads[0] += 1
                ac.activation(dummies[:, preloads[0] - 1:preloads[0]], eps, func)

            ac.wait_ge(s_zero, 4)
            preload(ACT.Sqrt)
            ac.wait_ge(s_col, 16)
            for nh in range(2):
                ac.wait_ge(s_emb, 2 * nh + 1)
                ac.activation(emb_out(0, nh), emb_in(0, nh), ACT.Identity, bias=cq(Q_TB, C)).then_inc(s_ea, 1)
            for t in range(T):
                ac.wait_ge(s_emt, t + 1)
                ac.activation(h[:, t, :], PS[:, t % 4, 0:DIM], ACT.Copy).then_inc(s_hcopy, 1)
            for hf in range(2):
                sqrt_ln(0, hf)
                evac_xt(0, range(2 * hf, 2 * hf + 2))
            qkm = qkT[0:C, :, :].rearrange("p (a x t) n -> p a x t n", a=2, t=T)
            for t in range(T):
                ac.wait_ge(s_chan, t + 1)
                src = PS[0:C, 4 + t % 4, :].rearrange("p (x a n) -> p a x n", a=2, n=HALF)
                for a in range(2):
                    last = ac.activation(qkm[:, a, :, t, 0:TOKENS], src[:, a, :, 0:TOKENS], ACT.Copy)
                last.then_inc(s_chanv, 1)
            for s in range(4):
                ac.wait_ge(s_gram, s + 1)
                ac.activation(Gs[0:C, s * 16:(s + 1) * 16, :], PS[0:C, s, :].rearrange("p (m x) -> p m x", m=16),
                              ACT.Copy).then_inc(s_gramv, 1)
            for b in range(2):
                ac.wait_ge(s_et, b + 1)
                ac.activation(E[:, :, b * 8:(b + 1) * 8, 0:16],
                              PS[:, 6 + b, 0:384].rearrange("p (r a c) -> p a r c", r=8, a=3), ACT.Copy)\
                  .then_inc(s_etv, 1)
            for b in range(2):
                ac.wait_ge(s_et, 3 + b)
                ac.activation(Tm[:, :, b * 8:(b + 1) * 8, :],
                              PS[:, 4 + b, 0:384].rearrange("p (r a c) -> p a r c", r=8, a=3), ACT.Copy)\
                  .then_inc(s_tv, 1)
            for s in range(16):
                ac.wait_ge(s_piv, s + 1)
                ac.activation(sq3[:, :, s:s + 1], E[:, :, s, s:s + 1], ACT.Sqrt).then_inc(s_sq, 1)
            preload(ACT.Exp)
            ac.wait_ge(s_back, 1)
            src = PS[0:C, 0, :].rearrange("p (j m) -> p m j", j=8)
            for par in range(2):
                last = ac.activation(BD[0:C, :, par * 16:par * 16 + 8], src, ACT.Copy, scale=parity[par])
            last.then_inc(s_bda, 1)
            for n, b in enumerate(QK_BANKS):
                if n % 2 == 0:
                    ac.wait_ge(s_qt, n + 1)
                    ac.activation(qt[0:C, b * 8:(b + 1) * 8, :], PS[0:C, b, 0:320].rearrange("p (m n) -> p m n", m=8),
                                  ACT.Copy).then_inc(s_qea, 1)
                elif n < 4:
                    a = n // 2
                    ac.wait_ge(s_qea, a + 1)
                    ac.wait_ge(s_qed, a + 1)
                    for hd in (4, 5):
                        last = ac.activation(qb_out(a, hd), qb_in(a), ACT.Copy, scale=head[hd])
                    last.then_inc(s_qba, 1)
            def mix_evac(t):
                ac.wait_ge(s_mixp, t + 1)
                ac.activation(Mx[:, t, :, :, 0:TOKENS].rearrange("p c a n -> p (c a) n"),
                              PS[:, t % 4, 0:8 * TOKENS].rearrange("p (x n) -> p x n", n=TOKENS), ACT.Identity,
                              bias=convb).then_inc(s_mixe, 1)

            def exp_pair(u):
                ac.wait_ge(s_sub, u + 1)
                v = Mx[:, 2 * u:2 * u + 2, :, :, 0:TOKENS].rearrange("p t c a n -> p (t c a) n")
                ac.activation(v, v, ACT.Exp).then_inc(s_exp, 1)

            ac.wait_ge(s_mix1, 2)
            ac.wait_ge(s_qbp, 2)
            for t in range(T + 2):
                if t < T:
                    ac.wait_ge(s_dots, t + 1)
                    ac.activation(S2[:, t, :], PS[:, t % 4, 0:8 * TOKENS], ACT.Square).then_inc(s_s2, 1)
                if 1 <= t <= T:
                    mix_evac(t - 1)
                if t >= 3 and t % 2:
                    exp_pair((t - 3) // 2)
            for t in range(T + 1):
                if t < T:
                    ac.wait_ge(s_atp, t + 1)
                    ac.activation(attnT[:, t, :], PS[:, 4 + t % 2, :], ACT.Copy).then_inc(s_atT, 1)
                if t == 1:
                    preload(ACT.Sqrt)
                if t % 4 == 0 and t > 0:
                    hf = t // 4 - 1
                    ac.wait_ge(s_av, hf + 1)
                    for a in range(2):
                        for kc in range(KC):
                            last = ac.activation(
                                XTi[:, kc, hf * 4:hf * 4 + 4, a, 0:TOKENS],
                                PS[0:C, 6 + a, kc * 160:(kc + 1) * 160].rearrange("p (t n) -> p t n", t=4)[:, :, 0:TOKENS],
                                ACT.Copy)
                        last.then_inc(s_oT, 1)

            for hf in range(2):
                sqrt_ln(1, hf)
                evac_xt(1, range(2 * hf, 2 * hf + 2))
            preload(ACT.Exp)
            for i in range(4):
                ac.wait_ge(s_chan, 8 + i + 1)
                ac.activation(vT[0:C, i * 8:(i + 1) * 8, :], PS[0:C, 4 + i, 0:COLS].rearrange("p (t n) -> p t n", t=T),
                              ACT.Identity, bias=cq(Q_VB + i % 2)).then_inc(s_chanv, 1)
            for a in range(2):
                ac.wait_ge(s_wsub, a + 1)
                ac.activation(Wm[0:C, a * 16:(a + 1) * 16, :], Wm[0:C, a * 16:(a + 1) * 16, :], ACT.Exp)\
                  .then_inc(s_wexp, 1)
            preload(ACT.Sqrt)
            evac_xt(2, range(4))
            ac.wait_ge(s_gva, 1)
            ac.activation(gg[:, 3:4], gg[:, 2:3], ACT.Sqrt, bias=eps12, scale=-NALL / (NALL - 1.0)).then_inc(s_gsd, 1)
            preload(ACT.Exp)
            ac.wait_ge(s_x1p, 1)
            ac.wait_ge(s_gsc, 1)
            for b in range(2):
                for kc in range(KC):
                    last = ac.activation(x1_out(b, kc), x1_in(b, kc), ACT.Identity, bias=gbi[0:C, kc:kc + 1],
                                         scale=gsc[0:C, kc:kc + 1])
            last.then_inc(s_x1, 1)
            ac.wait_ge(s_nm, 1)
            ac.activation(ga[0:IMAGES, :], sc16[0:IMAGES, :], ACT.Exp).then_inc(s_ge, 1)
            preload(ACT.Gelu_apprx_tanh)
            ac.wait_ge(s_gbp, 1)
            ac.activation(Gb[0:C, :, :].rearrange("p e b -> p (e b)"), PS[0:C, 2, 0:128], ACT.Copy).then_inc(s_gb, 1)
            ac.wait_ge(s_used, 1)
            codes = ac.value_load(used_codes[0:1, 0:1], min_val=0, max_val=8 ** EXPERTS - 1)
            with ac.Fori(0, EXPERTS // 2) as it:
                with ac.If(((codes >> (it * 6)) & 63) != 0):
                    for b in range(2):
                        with ac.If(code_of(codes, it * 2 + b) > 4):
                            ac.activation(fcb[:, b, :], fcball[:, it * 2 + b, :], ACT.Copy).then_inc(s_fcb, 1)
                            ac.wait_ge(s_fcb, it * 2 + (b + 1))
                            for i in range(2 * FC):
                                f, nh = divmod(i, 2)
                                ac.wait_ge(s_hp, it * 24 + (b * 12 + i + 1))
                                ac.activation(hT[b][:, f, nh * COLS:(nh + 1) * COLS], PS[:, i % 4, 0:COLS],
                                              ACT.Gelu_apprx_tanh,
                                              bias=fcb[:, b, f:f + 1]).then_inc(s_gelu, 1)
                        with ac.Else():
                            with ac.If(code_of(codes, it * 2 + b) != 0):
                                ac.activation(fcb[:, b, :], fcball[:, it * 2 + b, :], ACT.Copy).then_inc(s_fcb, 1)
                                ac.wait_ge(s_fcb, it * 2 + (b + 1))
                                for f in range(FC):
                                    ac.wait_ge(s_hp, it * 24 + (b * 12 + 2 * f + 2))
                                    ac.activation(hT[b][:, f, 0:QCOLS], PS[:, f % 4, 0:QCOLS], ACT.Gelu_apprx_tanh,
                                                  bias=fcb[:, b, f:f + 1]).then_inc(s_gelu, 2)
                            with ac.Else():
                                ac.drain().then_inc(s_gelu, 2 * FC)
                                ac.sem_inc(s_fcb, 1)
                with ac.Else():
                    ac.drain().then_inc(s_gelu, 2 * 2 * FC)
                    ac.sem_inc(s_fcb, 2)
            preload(ACT.Sqrt)
            ac.wait_ge(s_gva, 2)
            ac.activation(gg[:, 3:4], gg[:, 2:3], ACT.Sqrt, bias=eps12, scale=-NALL / (NALL - 1.0)).then_inc(s_gsd, 1)
            ac.wait_ge(s_gsc, 2)
            for kc in range(KC):
                ac.activation(XT[0:C, kc, :].rearrange("p (x n) -> p x n", n=HALF)[:, :, 0:TOKENS],
                              acc[0:C, kc, :].rearrange("p (x n) -> p x n", n=TOKENS), ACT.Identity,
                              bias=gbi[0:C, kc:kc + 1], scale=gsc[0:C, kc:kc + 1]).then_inc(s_x2, 1)

            sqrt_ln(2, 0)
            def kv_out(tiles):
                for t in tiles:
                    ac.wait_ge(s_kv2, t + 1)
                    ac.activation(A[:, t, :], PS[:, qk_bank(t), 0:2 * DIM], ACT.Copy)
                    ac.activation(Aabs[:, t, :], PS[:, qk_bank(t), 0:DIM], ACT.Abs).then_inc(s_kv2e, 1)

            evac_xt(3, range(2))
            sqrt_ln(2, 1)
            kv_out(range(2))
            evac_xt(3, range(2, 4))
            kv_out(range(2, 4))
            for i in range(4):
                ac.wait_ge(s_q2, i + 1)
                ac.activation(qT2[0:C, i * 8:(i + 1) * 8, :], PS[0:C, 4 * (i // 2) + i % 2, 0:COLS].rearrange("p (t n) -> p t n", t=T),
                              ACT.Copy).then_inc(s_q2e, 1)
            kv_out(range(4, T))
            for i in range(4):
                a, kc = divmod(i, 2)
                ac.wait_ge(s_o2, i + 1)
                ac.activation(XTi[:, kc, :, a, 0:TOKENS], PS[0:C, 4 + i, 0:COLS].rearrange("p (t n) -> p t n", t=T),
                              ACT.Copy).then_inc(s_o2e, 1)

            for hf in range(2):
                sqrt_ln(3, hf)
                evac_xt(4, range(2 * hf, 2 * hf + 2))
            preload(ACT.Exp)
            ac.wait_ge(s_lsub, 1)
            ac.activation(pr[:, :, :], pr[:, :, :], ACT.Exp).then_inc(s_lexp, 1)
            for g in range(T):
                ac.wait_ge(s_xip, g + 1)
                ac.activation(xinT[0:C, :, :, g:SLOTS:T],
                              PS[0:C, g, 0:KC * GE].rearrange("p (k e c) -> p k e c", k=KC, e=EXPERTS),
                              ACT.Copy).then_inc(s_xin, 1)
            for b in range(4):
                ac.wait_ge(s_ctp, b + 1)
                ac.activation(combT[0:92, 2 * b:2 * b + 2, :, :].rearrange("p g a n -> p (g a n)"), PS[0:92, 4 + b, :],
                              ACT.Copy).then_inc(s_ct, 1)
            with ac.Fori(0, EXPERTS // 2) as it:
                for b in range(2):
                    ac.wait_ge(s_edone, it * 2 + 1)
                    for i in range(3):
                        ac.wait_ge(s_h1p, it * 6 + (3 * b + i + 1))
                        ac.activation(hT1[b][:, 2 * i:2 * i + 2, :].rearrange("p f n -> p (f n)"),
                                      PS[:, 3 * b + i, 0:2 * SLOTS], ACT.Relu).then_inc(s_relu, 1)
            for g in range(T):
                ac.wait_ge(s_ygp, g + 1)
                ac.activation(yG[0:92, g, :, :].rearrange("p a n -> p (a n)"), PS[0:92, g, 0:2 * DIM],
                              ACT.Copy).then_inc(s_yg, 1)

        @block.vector
        def _(ve):
            n = [0]

            def link(ins):
                n[0] += 1
                ins.then_inc(dchain, 1)
                ve.wait_ge(dchain, n[0])

            def scale_tiles(r, hf):
                ts = range(4 * hf, 4 * hf + 4)
                for t in ts:
                    last = ve.bn_aggr(mv[:, t, :], stats[:, t, :])
                last.then_inc(s_var, 1)
                ve.wait_ge(s_sd, 2 * r + hf + 1)
                link(ve.reciprocal(rstd[:, 4 * hf:4 * hf + 4], sd[:, 4 * hf:4 * hf + 4]))
                for t in ts:
                    ve.tensor_scalar(xn[:, t, :], h[:, t, :], mv[:, t, 0:1], rstd[:, t:t + 1], ALU.subtract,
                                     ALU.mult).then_inc(s_xn, 1)

            def normalise_embedding(hf):
                for t in range(4 * hf, 4 * hf + 4):
                    ve.wait_ge(s_hcopy, t + 1)
                    last = ve.bn_stats(stats[:, t, :], h[:, t, :])
                link(last)
                scale_tiles(0, hf)

            def residual_norm(r, done, base):
                for hf in range(2):
                    for t in range(4 * hf, 4 * hf + 4):
                        ve.wait_ge(done, base + t + 1)
                        ve.tensor_tensor(h[:, t, :], PS[:, t, 0:DIM], h[:, t, :], ALU.add).then_inc(s_h, 1)
                        if t % 4:
                            ve.wait_ge(s_h, (r - 1) * T + t)
                            ve.bn_stats(stats[:, t - 1, :], h[:, t - 1, :])
                    ve.wait_ge(s_h, (r - 1) * T + 4 * hf + 4)
                    link(ve.bn_stats(stats[:, 4 * hf + 3, :], h[:, 4 * hf + 3, :]))
                    scale_tiles(r, hf)

            ve.wait_ge(s_col, 16)
            link(ve.tensor_tensor(wpT[0:HEADS, :], cq(Q_CW, HEADS, HEADS), cq(Q_CW + HEADS, HEADS, HEADS), ALU.add))
            ve.tensor_scalar(wpT[0:HEADS, :], wpT[0:HEADS, :], cq(Q_GS, HEADS), None, ALU.mult).then_inc(s_mixw, 1)
            for nh in range(2):
                ve.wait_ge(s_emb, 2 * nh + 2)
                ve.tensor_scalar(emb_out(1, nh), emb_in(1, nh), cq(Q_TB + 1, C), None, ALU.add).then_inc(s_ed, 1)
            normalise_embedding(0)
            ve.wait_ge(s_mixr, 1)
            ve.wait_ge(s_zero, 4)
            ve.tensor_copy(convb, PS[:, 7, HEADS:HEADS + 1])
            ve.tensor_tensor(mixT[:, :, 0:60].rearrange("p k (o n) -> p k o n", o=HC),
                             bc(PS[:, 7, 0:HEADS].rearrange("p (k o) -> p k o", k=KC), 3, NCH),
                             bc(bc(con[:, K_DN:K_DN + NCH], 1, HC), 1, KC), ALU.mult).then_inc(s_mix1, 2)
            normalise_embedding(1)
            ve.wait_ge(s_row, 16)

            for t in range(T):
                ve.wait_ge(s_tok, t + 1)
                b = t % 2
                ve.tensor_tensor(A[:, t, :], PS[:, b, 0:2 * DIM], row[:, R_QKVB:R_QKVB + 2 * DIM], ALU.add)
                ve.tensor_tensor(vpad[:, t, :].rearrange("p (x c) -> p x c", c=32)[:, :, 0:HD],
                                 PS[:, 2 + b, 0:DIM].rearrange("p (x c) -> p x c", c=HD),
                                 row[:, R_QKVB + 2 * DIM:R_QKVB + 3 * DIM].rearrange("p (x c) -> p x c", c=HD),
                                 ALU.add).then_inc(s_tokv, 1)

            def mark(ins):
                n[0] += 1
                ins.then_inc(dchain, 1)
                return n[0]

            ve.wait_ge(s_etv, 3)
            e_done = t_done = None
            for s in range(17):
                u = s - 1
                re, ru, w = 15 - s, 15 - u, 16 - u
                if s < 16:
                    if e_done:
                        ve.wait_ge(dchain, e_done)
                    ve.sem_inc(s_piv, 1)
                if s < 15:
                    e0 = mark(ve.reciprocal(inv3, E[:, :, s, s:s + 1]))
                if u >= 0:
                    if u == 0:
                        ve.wait_ge(s_tv, 2)
                    if t_done:
                        ve.wait_ge(dchain, t_done)
                    ve.wait_ge(dchain, r_done)
                    top, R = Tm[:, :, u, u:16], Rn[:, u % 2, :, 0:w]
                    minus = mark(ve.tensor_tensor(rowm[:, :, 0:w], top, R, ALU.subtract))
                    plus = mark(ve.scalar_tensor_tensor(rowp[:, :, 0:w], Tm[:, :, u, u:u + 1].broadcast_to([128, 3, w]),
                                                        0.0, R, ALU.is_ge, ALU.mult))
                if u >= 0:
                    ve.wait_ge(dchain, plus)
                    t1 = mark(ve.scalar_tensor_tensor(top, rowp[:, :, 0:w], 2.0, rowm[:, :, 0:w], ALU.mult, ALU.add))
                if s < 15:
                    ve.wait_ge(dchain, e0)
                    lcol = Lc[:, s, :, 0:re]
                    ve.tensor_tensor(lcol, E[:, :, s + 1:16, s], inv3.broadcast_to([128, 3, re]), ALU.mult)\
                      .then_inc(s_lc, 1)
                if 0 <= u < 15:
                    ve.wait_ge(dchain, t1)
                    t0 = mark(ve.reciprocal(invu, Tm[:, :, u, u:u + 1]))
                if s < 15:
                    ve.wait_ge(s_lc, s + 1)
                    prod = Pb[:, 0:3 * re * re].rearrange("p (a r c) -> p a r c", a=3, r=re)
                    e2 = mark(ve.tensor_tensor(prod, bc(lcol, 3, re), bc(E[:, :, s, s + 1:16], 2, re), ALU.mult))
                if 0 <= u < 15:
                    ve.wait_ge(dchain, t0)
                    t2 = mark(ve.tensor_tensor(lcolu[:, :, 0:ru], Tm[:, :, u + 1:16, u],
                                               invu.broadcast_to([128, 3, ru]), ALU.mult))
                if s < 15:
                    ve.wait_ge(dchain, e2)
                    below = E[:, :, s + 1:16, s + 1:16]
                    e_done = mark(ve.tensor_tensor(below, below, prod, ALU.subtract))
                if 0 <= u < 15:
                    ve.wait_ge(dchain, t2)
                    produ = Pu[:, 0:3 * ru * ru].rearrange("p (a r c) -> p a r c", a=3, r=ru)
                    t3 = mark(ve.tensor_tensor(produ, bc(lcolu[:, :, 0:ru], 3, ru), bc(Tm[:, :, u, u + 1:16], 2, ru),
                                               ALU.mult))
                if s < 16:
                    ve.wait_ge(s_sq, s + 1)
                    r0 = mark(ve.reciprocal(rs3[:, :, s:s + 1], sq3[:, :, s:s + 1]))
                if 0 <= u < 15:
                    ve.wait_ge(dchain, t3)
                    belowu = Tm[:, :, u + 1:16, u + 1:16]
                    t_done = mark(ve.tensor_tensor(belowu, belowu, produ, ALU.subtract))
                if s < 16:
                    ve.wait_ge(dchain, r0)
                    r_done = mark(ve.tensor_tensor(Rn[:, s % 2, :, 0:16 - s], E[:, :, s, s:16],
                                                   rs3[:, :, s:s + 1].broadcast_to([128, 3, 16 - s]), ALU.mult))
            ve.wait_ge(dchain, t1)
            diag = Tm[:, :, :, :].rearrange("p a r c -> p a (r c)")[:, :, 0:256:17]
            link(ve.tensor_scalar(tsg, diag, 0.0, -2.0, ALU.is_ge, ALU.mult))
            link(ve.scalar_tensor_tensor(nsg, tsg, 1.0, rs3, ALU.add, ALU.mult))
            ve.wait_ge(s_zero, 5)
            ve.wait_ge(s_inv, 1)
            for par in range(2):
                p0 = par * 64
                o = BLK[p0:p0 + 64].rearrange("p j (a x) -> p a j x", a=3)[:, :, :, par * 16:par * 16 + 16]
                last = ve.tensor_tensor(o, E[p0:p0 + 64, :, :, 16:32], bc(nsg[p0:p0 + 64], 3, 16), ALU.mult)
            last.then_inc(s_blk, 1)
            ve.wait_ge(s_back, 1)
            src = PS[0:C, 1, :].rearrange("p (j m) -> p m j", j=8)
            for par in range(2):
                last = ve.tensor_scalar(BD[0:C, :, par * 16 + 8:par * 16 + 16], src, parity[par], None, ALU.mult)
            last.then_inc(s_bdv, 1)
            for i in range(4):
                b = QK_BANKS[2 * i + 1]
                ve.wait_ge(s_qt, 2 * i + 2)
                ve.tensor_copy(qt[0:C, b * 8:(b + 1) * 8, :], PS[0:C, b, 0:320].rearrange("p (m n) -> p m n", m=8))\
                  .then_inc(s_qed, 1)
                if i < 2:
                    ve.wait_ge(s_qed, i + 1)
                    ve.wait_ge(s_qea, i + 1)
                    for hd in range(4):
                        last = ve.tensor_scalar(qb_out(i, hd), qb_in(i), head[hd], None, ALU.mult)
                    last.then_inc(s_qbv, 1)
            for u in range(5):
                if u < 4:
                    v = Mx[:, 2 * u:2 * u + 2, :, :, 0:TOKENS].rearrange("p t c a n -> p (t c a) n")
                    m = mx[:, 2 * u:2 * u + 2, :].rearrange("p t x -> p (t x)")
                    ve.wait_ge(s_mixe, 2 * u + 2)
                    link(ve.tensor_reduce(m, v, AX, ALU.max))
                    ve.tensor_tensor(v, v, bc(m, 2, TOKENS), ALU.subtract).then_inc(s_sub, 1)
                if u >= 1:
                    b = u - 1
                    v = Mx[:, 2 * b:2 * b + 2, :, :, 0:TOKENS].rearrange("p t c a n -> p (t c a) n")
                    m = sme[:, 2 * b:2 * b + 2, :].rearrange("p t x -> p (t x)")
                    q = rsm[:, 2 * b:2 * b + 2, :].rearrange("p t x -> p (t x)")
                    ve.wait_ge(s_exp, b + 1)
                    link(ve.tensor_reduce(m, v, AX, ALU.add))
                    link(ve.reciprocal(q, m))
                    ve.tensor_tensor(v, v, bc(q, 2, TOKENS), ALU.mult).then_inc(s_att, 1)

            ve.wait_ge(s_hb, 1)
            residual_norm(1, s_prj, 0)

            for t in range(T):
                ve.wait_ge(s_tok, T + t + 1)
                ve.tensor_tensor(A[:, t, :], PS[:, qk_bank(t), 0:2 * DIM], row[:, R_W1B:R_W1B + 2 * DIM], ALU.add)\
                  .then_inc(s_tokv, 1)
            for a in range(2):
                w = Wm[0:C, a * 16:(a + 1) * 16, :]
                ve.wait_ge(s_w_ps, a + 1)
                link(ve.scalar_tensor_tensor(w, PS[0:C, a, :].rearrange("p (m x) -> p m x", m=16),
                                             float(1.0 / np.sqrt(np.float32(TOKENS))),
                                             bc(con[0:C, K_NEG:K_NEG + 32], 1, 16), ALU.mult, ALU.add))
                link(ve.tensor_reduce(wmax[0:C, a * 16:(a + 1) * 16], w, AX, ALU.max))
                ve.tensor_tensor(w, w, bc(wmax[0:C, a * 16:(a + 1) * 16], 2, 32), ALU.subtract).then_inc(s_wsub, 1)
            for a in range(2):
                w = Wm[0:C, a * 16:(a + 1) * 16, :]
                ve.wait_ge(s_wexp, a + 1)
                ve.transpose(BD2[0:C, a * 16:(a + 1) * 16, :], w).then_inc(s_wT, 1)
                link(ve.tensor_reduce(wsum[0:C, a * 16:(a + 1) * 16], w, AX, ALU.add))
                link(ve.reciprocal(wrec[0:C, a * 16:(a + 1) * 16], wsum[0:C, a * 16:(a + 1) * 16]))
            ve.wait_ge(s_zero, 6)
            for b in range(4):
                ve.wait_ge(s_wv, b + 1)
                ve.tensor_tensor(oS[0:C, b * 8:(b + 1) * 8, :], PS[0:C, 2 + b, 0:COLS].rearrange("p (t n) -> p t n", t=T),
                                 bc(wrec[0:C, b * 8:(b + 1) * 8], 2, TOKENS), ALU.mult).then_inc(s_os, 1)
            ve.wait_ge(s_zb, 1)
            for t in range(T):
                ve.wait_ge(s_w2p, t + 1)
                ve.tensor_tensor(xn[:, t, :], PS[:, t % 4, 0:DIM], xn[:, t, :], ALU.add).then_inc(s_s, 1)
                if t >= 1:
                    ve.wait_ge(s_s, t)
                    ve.bn_stats(stats[:, t - 1, :], xn[:, t - 1, :])
            ve.wait_ge(s_s, T)
            link(ve.bn_stats(stats[:, T - 1, :], xn[:, T - 1, :]))

            def global_norm(r, p, parts, wcol, bcol):
                link(ve.bn_aggr(gmv[0:p], stats[0:p].rearrange("p t x -> p (t x)")[:, 0:parts]))
                ve.tensor_copy(gst[0:p, 0:1], gmv[0:p, 0:1])
                ve.scalar_tensor_tensor(gst[0:p, 1:2], gmv[0:p, 0:1], gmv[0:p, 0:1], gmv[0:p, 1:2], ALU.mult,
                                        ALU.add).then_inc(s_gst, 1)
                ve.wait_ge(s_gps, r + 1)
                link(ve.tensor_copy(gg[:, 0:2], PS[:, 0, 0:2]))
                ve.scalar_tensor_tensor(gg[:, 2:3], gg[:, 0:1], gg[:, 0:1], gg[:, 1:2], ALU.mult,
                                        ALU.subtract).then_inc(s_gva, 1)
                link(ve.tensor_scalar(gg[:, 5:6], gg[:, 0:1], -1.0, None, ALU.mult))
                ve.wait_ge(s_gsd, r + 1)
                link(ve.reciprocal(gg[:, 4:5], gg[:, 3:4]))
                link(ve.tensor_scalar(gsc[0:C], cq(wcol, C, KC), gg[0:C, 4:5], None, ALU.mult))
                ve.scalar_tensor_tensor(gbi[0:C], gsc[0:C], gg[0:C, 5:6], cq(bcol, C, KC), ALU.mult,
                                        ALU.add).then_inc(s_gsc, 1)

            global_norm(0, 128, T * 6, Q_LN1W, Q_LN1B)

            ve.wait_ge(s_gsc, 1)
            ve.wait_ge(s_x1p, 1)
            for b in range(2, 4):
                for kc in range(KC):
                    last = ve.tensor_scalar(x1_out(b, kc), x1_in(b, kc), gsc[0:C, kc:kc + 1], gbi[0:C, kc:kc + 1],
                                            ALU.mult, ALU.add)
            link(last)
            x1i = x1T[0:C, :, :].rearrange("p k (b n) -> p k b n", n=TOKENS)
            ve.tensor_reduce(xbar[0:C, :, 8:16], x1i[:, :, 8:16], AX, ALU.add)
            ve.wait_ge(s_x1, 1)
            ve.tensor_reduce(xbar[0:C, :, 0:8], x1i[:, :, 0:8], AX, ALU.add).then_inc(s_xbar, 1)
            ve.tensor_copy(acc[0:C, :, :], x1T[0:C, :, :])
            ve.wait_ge(s_rps, 1)
            link(ve.scalar_tensor_tensor(sc16[0:IMAGES], PS[0:IMAGES, 1, 0:EXPERTS], 1.0 / TOKENS,
                                         row[0:IMAGES, R_RB:R_RB + EXPERTS], ALU.mult, ALU.add))
            link(ve.tensor_reduce(gone[0:IMAGES, 0:1], sc16[0:IMAGES], AX, ALU.max))
            ve.tensor_scalar(sc16[0:IMAGES], sc16[0:IMAGES], gone[0:IMAGES, 0:1], None, ALU.subtract).then_inc(s_nm, 1)
            ve.wait_ge(s_ge, 1)
            link(ve.tensor_reduce(gone[0:IMAGES, 1:2], ga[0:IMAGES], AX, ALU.add))
            link(ve.reciprocal(gone[0:IMAGES, 2:3], gone[0:IMAGES, 1:2]))
            link(ve.tensor_scalar(ga[0:IMAGES], ga[0:IMAGES], gone[0:IMAGES, 2:3], None, ALU.mult))
            link(ve.max(g8[0:IMAGES], ga[0:IMAGES]))
            link(ve.max_index(gi[0:IMAGES], g8[0:IMAGES], ga[0:IMAGES]))
            link(ve.tensor_copy(gi_f[0:IMAGES], gi[0:IMAGES]))
            link(ve.tensor_scalar(gm[0:IMAGES], con[0:IMAGES, K_I8:K_I8 + 8], gi_f[0:IMAGES, 0:1], None, ALU.is_equal))
            link(ve.scalar_tensor_tensor(gm[0:IMAGES], con[0:IMAGES, K_I8:K_I8 + 8], gi_f[0:IMAGES, 1:2],
                                         gm[0:IMAGES], ALU.is_equal, ALU.add))
            link(ve.tensor_tensor(gm[0:IMAGES], gm[0:IMAGES], ga[0:IMAGES], ALU.mult))
            ve.tensor_tensor(Gd[:, :, :], bc(gm[0:IMAGES], 2, IMAGES), bc(con[0:IMAGES, K_ID:K_ID + IMAGES], 1, EXPERTS),
                             ALU.mult).then_inc(s_gd, 1)
            ve.wait_ge(s_gb, 1)
            link(ve.tensor_reduce(quarters[0:1], Gb[0:1, :, :].rearrange("p e (q i) -> p e q i", i=QI), AX, ALU.max))
            link(ve.scalar_tensor_tensor(quarters[0:1].rearrange("p e q -> p (e q)"),
                                         quarters[0:1].rearrange("p e q -> p (e q)"), 0.0,
                                         con[0:1, K_CODE:K_CODE + 4 * EXPERTS], ALU.is_gt, ALU.mult))
            ve.tensor_reduce(csum[0:1], quarters[0:1], AX, ALU.add)
            link(ve.tensor_reduce(cmax[0:1], quarters[0:1], AX, ALU.max))
            link(ve.tensor_tensor(several[0:1], csum[0:1], cmax[0:1], ALU.is_gt))
            link(ve.tensor_tensor(several[0:1], several[0:1], con[0:1, K_CODE3:K_CODE3 + EXPERTS], ALU.mult))
            link(ve.tensor_tensor(cmax[0:1], cmax[0:1], several[0:1], ALU.add))
            link(ve.tensor_reduce(gone[0:1, 3:4], cmax[0:1], AX, ALU.add))
            ve.tensor_copy(used_codes[0:1, 0:1], gone[0:1, 3:4]).then_inc(s_used, 1)
            ve.wait_ge(s_used, 1)
            codes = ve.value_load(used_codes[0:1, 0:1], min_val=0, max_val=8 ** EXPERTS - 1)
            ve.sem_inc(s_acc, 1)
            ve.sem_inc(s_bst, 1)
            with ve.Fori(0, EXPERTS // 2) as it:
                with ve.If(((codes >> (it * 6)) & 63) != 0):
                    for b in range(2):
                        with ve.If(code_of(codes, it * 2 + b) > 4):
                            ve.wait_ge(s_acc, it * 8 + (4 * b + 1))
                            ve.wait_ge(s_bst, it * 8 + (4 * b + 1))
                            for i in range(6):
                                if i < 4:
                                    kc, nh = divmod(i, 2)
                                    y = ytmp[0:C, i, :]
                                    g = Gb[0:C, it * 2 + b, nh * 8:(nh + 1) * 8]
                                    ve.wait_ge(s_yp, it * 8 + (b * 4 + i + 1))
                                    ve.scalar_tensor_tensor(y.rearrange("p (x n) -> p x n", n=TOKENS),
                                                            PS[0:C, 4 + i, 0:COLS].rearrange("p (x n) -> p x n", n=TOKENS),
                                                            col[0:C, it * 4 + (Q_PB + b * 2 + kc)].unsqueeze(1),
                                                            bc(g, 2, TOKENS), ALU.add, ALU.mult).then_inc(s_ytmp, 1)
                                if 1 <= i < 5:
                                    kc, nh = divmod(i - 1, 2)
                                    y = ytmp[0:C, i - 1, :]
                                    ve.wait_ge(s_ytmp, it * 8 + (b * 4 + i))
                                    ve.tensor_tensor(acc[0:C, kc, nh * COLS:(nh + 1) * COLS],
                                                     acc[0:C, kc, nh * COLS:(nh + 1) * COLS], y, ALU.add).then_inc(s_acc, 1)
                                if i >= 2:
                                    kc, nh = divmod(i - 2, 2)
                                    ve.wait_ge(s_acc, it * 8 + (4 * b + i))
                                    ve.bn_stats(stats[0:C, i - 2, :], acc[0:C, kc, nh * COLS:(nh + 1) * COLS])\
                                      .then_inc(s_bst, 1)
                        with ve.Else():
                            with ve.If(code_of(codes, it * 2 + b) != 0):
                                ve.wait_ge(s_acc, it * 8 + (4 * b + 1))
                                ve.wait_ge(s_bst, it * 8 + (4 * b + 1))
                                quarter = quarter_of(codes, it * 2 + b)
                                for kc in range(KC):
                                    y = ytmp[0:C, kc, 0:QCOLS]
                                    ve.wait_ge(s_yp, it * 8 + (b * 4 + 2 * kc + 2))
                                    ve.scalar_tensor_tensor(y.rearrange("p (x n) -> p x n", n=TOKENS),
                                                            PS[0:C, 4 + kc, 0:QCOLS].rearrange("p (x n) -> p x n", n=TOKENS),
                                                            col[0:C, it * 4 + (Q_PB + b * 2 + kc)].unsqueeze(1),
                                                            bc(Gbq[0:C, it * 2 + b, quarter, :], 2, TOKENS),
                                                            ALU.add, ALU.mult).then_inc(s_ytmp, 2)
                                    ve.wait_ge(s_ytmp, it * 8 + (b * 4 + 2 * kc + 2))
                                    ve.tensor_tensor(accq[0:C, kc, quarter, :], accq[0:C, kc, quarter, :], y, ALU.add)\
                                      .then_inc(s_acc, 2)
                                ve.wait_ge(s_acc, it * 8 + (4 * b + 5))
                                for i in range(4):
                                    kc, nh = divmod(i, 2)
                                    ve.bn_stats(stats[0:C, i, :], acc[0:C, kc, nh * COLS:(nh + 1) * COLS])\
                                      .then_inc(s_bst, 1)
                            with ve.Else():
                                ve.drain().then_inc(s_acc, 4)
                                ve.sem_inc(s_ytmp, 4)
                                ve.sem_inc(s_bst, 4)
                with ve.Else():
                    ve.drain().then_inc(s_acc, 2 * 4)
                    ve.sem_inc(s_ytmp, 2 * 4)
                    ve.sem_inc(s_bst, 2 * 4)
            ve.wait_ge(s_acc, 4 * EXPERTS + 1)
            ve.wait_ge(s_bst, 4 * EXPERTS + 1)
            global_norm(1, C, 24, Q_LN2W, Q_LN2B)
            residual_norm(2, s_x2p, 0)

            ve.wait_ge(s_q2e, 4)
            link(ve.tensor_reduce(sq2[0:C], qT2[0:C], AX, ALU.add, apply_absolute_value=True))
            link(ve.tensor_scalar(sq2[0:C], sq2[0:C], 1e-12, None, ALU.max))
            ve.wait_ge(s_kvp, 1)
            link(ve.tensor_scalar(sk2[0:C].rearrange("p (a m) -> p m a", a=2),
                                  PS[0:C, 4, 0:32].rearrange("p (m a) -> p m a", a=2), 1e-12, None, ALU.max))
            link(ve.reciprocal(sq2[0:C], sq2[0:C]))
            link(ve.reciprocal(sk2[0:C], sk2[0:C]))
            link(ve.tensor_tensor(sk2[0:C], sk2[0:C], sq2[0:C], ALU.mult))
            link(ve.tensor_tensor(kvs[0:C], bc(con[0:C, K_PAIR:K_PAIR + 32], 1, 32), bc(sk2[0:C], 2, 32), ALU.mult))
            for a in range(2):
                ve.wait_ge(s_kvm, a + 1)
                ve.tensor_tensor(BD2[0:C, a * 16:(a + 1) * 16, :], PS[0:C, a, :].rearrange("p (m x) -> p m x", m=16),
                                 kvs[0:C, a * 16:(a + 1) * 16, :], ALU.mult).then_inc(s_bd3, 1)
            ve.wait_ge(s_hb, 2)
            residual_norm(3, s_prj, T)

            ve.wait_ge(s_lg, 1)
            lg = PS[:, 2, 0:64].rearrange("p (g e) -> p g e", g=T)
            link(ve.tensor_reduce(lmax, lg, AX, ALU.max))
            ve.tensor_tensor(pr[:, :, :], lg, bc(lmax, 2, EXPERTS), ALU.subtract).then_inc(s_lsub, 1)
            ve.wait_ge(s_lexp, 1)
            link(ve.tensor_reduce(lmax, pr[:, :, :], AX, ALU.add))
            link(ve.reciprocal(lmax, lmax))
            link(ve.tensor_tensor(pr[:, :, :], pr[:, :, :], bc(lmax, 2, EXPERTS), ALU.mult))
            for g in range(T):
                last = ve.max(v8[:, g, :], pr[:, g, :])
            link(last)
            for g in range(T):
                last = ve.max_index(i8[:, g, :], v8[:, g, :], pr[:, g, :])
            link(last)
            link(ve.tensor_copy(i8f[:, :, :], i8[:, :, :]))
            for k in range(2):
                last = ve.tensor_tensor(m12[:, k], bc(con[:, K_I8:K_I8 + 8], 1, T), bc(i8f[:, :, k], 2, EXPERTS),
                                        ALU.is_equal)
            link(last)
            mf = m12[:, :, :, :].rearrange("p k g e -> p (k g e)")
            ve.tensor_scalar(mf, mf, con[:, K_VALID:K_VALID + 1], None, ALU.mult).then_inc(s_m12, 1)
            ve.wait_ge(s_rk, 1)
            ve.wait_ge(s_m12, 1)
            link(ve.tensor_tensor(rank[:, :, :, :].rearrange("p k g e -> p (k g e)"), PS[:, 5, 0:128], mf, ALU.mult))
            link(ve.tensor_tensor(rank[:, 0], rank[:, 0], rank[:, 1], ALU.add))
            link(ve.tensor_scalar(rank[:, 0], rank[:, 0], -1.0, None, ALU.add))
            link(ve.tensor_tensor(gse[:, :, :], m12[:, 0], m12[:, 1], ALU.add))
            link(ve.tensor_tensor(gse[:, :, :], gse[:, :, :], pr[:, :, :], ALU.mult))
            GEf = T * EXPERTS
            rk = bc(rank[:, 0].rearrange("p g e -> p (g e)"), 2, CAP)
            dv = Q[:, 0:T * GE].rearrange("p (x c) -> p x c", c=CAP)
            cv = Q[:, T * GE:2 * T * GE].rearrange("p (x c) -> p x c", c=CAP)
            for hf in range(2):
                x = slice(hf * GEf // 2, (hf + 1) * GEf // 2)
                if hf:
                    ve.wait_ge(s_rk, 2)
                    ve.tensor_reduce(filled[0:1, 0], PS[0:1, 6, 0:64].rearrange("p (g e) -> p e g", g=T), AX, ALU.max)
                ve.tensor_tensor(dv[:, x], rk[:, x], bc(con[:, K_I23:K_I23 + CAP], 1, GEf // 2),
                                 ALU.is_equal).then_inc(s_disp, 1)
            ve.wait_ge(s_disp, 2)
            ve.tensor_tensor(cv, dv, bc(gse[:, :, :].rearrange("p g e -> p (g e)"), 2, CAP), ALU.mult)\
              .then_inc(s_comb, 1)
            ve.tensor_scalar(filled[0:1, 1], filled[0:1, 0], float(FILL[0]), None, ALU.is_gt)
            link(ve.tensor_scalar(filled[0:1, 2], filled[0:1, 0], float(FILL[1]), None, ALU.is_gt))
            link(ve.tensor_tensor(filled[0:1, 1], filled[0:1, 1], filled[0:1, 2], ALU.add))
            link(ve.tensor_tensor(filled[0:1, 1], filled[0:1, 1], con[0:1, K_POW4:K_POW4 + EXPERTS], ALU.mult))
            link(ve.tensor_reduce(gone[0:1, 3:4], filled[0:1, 1], AX, ALU.add))
            ve.tensor_copy(fill_codes[0:1, 0:1], gone[0:1, 3:4]).then_inc(s_filled, 1)
            ve.sem_inc(s_y1, 2)
            with ve.Fori(0, EXPERTS // 2) as it:
                for b in range(2):
                    ve.wait_ge(s_edone, it * 2 + (b + 2))
                    ve.tensor_copy(yT[0:C, :, :, it * 2 + b, :],
                                   PS[0:C, 6 + b, 0:KC * SLOTS].rearrange("p (k c g) -> p k g c", k=KC, g=T))\
                      .then_inc(s_y1, 1)
            for t in range(T):
                ve.wait_ge(s_fin, t + 1)
                ve.tensor_tensor(h[:, t, :], PS[:, t, 0:DIM], h[:, t, :], ALU.add).then_inc(s_res, 1)


def constants():
    k = np.zeros((128, K_ALL), np.float32)
    p = np.arange(128)
    k[:, K_ID:K_ID + 128] = np.eye(128)
    k[:, K_TRI:K_TRI + 128] = p[:, None] <= p[None, :]
    k[:, K_VALID:K_VALID + 128] = (p % HALF < TOKENS)[:, None]
    k[:, K_ONE:K_ONE + 128] = 1
    k[:, K_II:K_II + 64] = (p % 64)[:, None] == np.arange(64)
    same = ((p // HD) % 2)[:, None] == np.arange(32) // HD
    k[:, K_PAIR:K_PAIR + 32] = same
    k[:, K_NEG:K_NEG + 32] = np.where(same, 0.0, -1e30)
    k[:, K_HEAD:K_HEAD + HC] = (p // HD)[:, None] == np.arange(HC)
    for hd in range(HEADS):
        c0 = K_E1 + (hd // HC) * 64 + (hd % HC) * NCH
        k[hd, c0:c0 + NCH] = 1
    q = p % 64
    k[:, K_DN:K_DN + NCH] = ((q % NCH)[:, None] == np.arange(NCH)) & (q < HC * NCH)[:, None]
    k[:, K_I8:K_I8 + EXPERTS] = np.arange(EXPERTS)
    k[:, K_I23:K_I23 + CAP] = np.arange(CAP)
    k[:, K_EYE:K_EYE + 256] = np.eye(16).reshape(-1)
    for a in range(2):
        k[a * HALF:a * HALF + TOKENS, K_HALF + a] = 1
    place = 8 ** np.arange(EXPERTS)
    k[:, K_CODE:K_CODE + 4 * EXPERTS] = (place[:, None] * np.arange(1, 5)).reshape(-1)
    k[:, K_CODE3:K_CODE3 + EXPERTS] = 3 * place
    k[:, K_POW4:K_POW4 + EXPERTS] = 4 ** np.arange(EXPERTS)
    k[:, K_MEANV:K_MEANV + 128] = (p % HALF < TOKENS)[:, None] / (2 * TOKENS)
    k[:, K_MEANC:K_MEANC + 128] = 1 / C
    return k


def layout(i):
    def chunks(w, parts, size):
        return w.reshape(parts, size, -1).transpose(1, 0, 2)

    pat = i["x"].reshape(IMAGES, 3, 6, 16, 6, 16).transpose(3, 5, 1, 0, 2, 4).reshape(PK, 128, IMAGES * PATCHES)
    rows = np.concatenate([i["L0_attn_qkv_b"], i["L0_attn_proj_b"], i["L0_ffn_W1_b"][:2 * DIM], i["L0_ffn_W2_b"],
                           i["L0_ffn_r_b"], i["L1_attn_b_proj"]])
    cols = np.zeros((128, Q_ALL), np.float32)
    cols[:C, Q_QKB:Q_QKB + 4] = i["L0_attn_qkv_b"][:2 * DIM].reshape(4, C).T
    cols[:C, Q_VB:Q_VB + 2] = i["L0_ffn_W1_b"][2 * DIM:].reshape(2, C).T
    for at, name in ((Q_LN1W, "ln1_w"), (Q_LN1B, "ln1_b"), (Q_LN2W, "ln2_w"), (Q_LN2B, "ln2_b")):
        cols[:C, at:at + 2] = i["L0_ffn_" + name].reshape(2, C).T
    cols[:C, Q_PB:Q_PB + 16] = i["L0_ffn_proj_b"].reshape(2 * EXPERTS, C).T
    cols[:, Q_FCB:Q_FCB + 48] = i["L0_ffn_fc_b"].reshape(FC * EXPERTS, 128).T
    cols[:C, Q_TB:Q_TB + KC] = i["L0_tok_b"].reshape(KC, C).T
    cols[:C, Q_CLS:Q_CLS + KC] = i["cls_tok"].reshape(KC, C).T
    cols[:, Q_GS] = i["L0_attn_grassman_scale"]
    cols[:HEADS, Q_CB] = i["L0_attn_conv_b"]
    cols[:HEADS, Q_CW:Q_CW + 24] = i["L0_attn_conv_w"].reshape(HEADS, 2, HEADS).transpose(2, 1, 0).reshape(HEADS, 24)
    ew = lambda w: w.reshape(EXPERTS, KC, C, FF).transpose(0, 2, 1, 3).reshape(EXPERTS, C, KC * FF)
    eo = lambda w: w.reshape(EXPERTS, FC, 128, DIM).transpose(0, 2, 1, 3).reshape(EXPERTS, 128, FC * DIM)
    return {
        "patches": pat.transpose(1, 0, 2),
        "tok_w": chunks(i["L0_tok_W"].reshape(DIM, 16, 16, 3).reshape(DIM, 768).T, PK, 128),
        "rows": rows,
        "cols": cols,
        "consts": constants(),
        "qkv_w": chunks(i["L0_attn_qkv_w"].T, KC, C),
        "proj_w": chunks(i["L0_attn_proj_w"].T, KC, C),
        "w1": chunks(i["L0_ffn_W1_w"], KC, C),
        "w2": chunks(i["L0_ffn_W2_w"], KC, C),
        "r_w": chunks(i["L0_ffn_r_w"], KC, C),
        "fc_w": ew(i["L0_ffn_fc_w"]),
        "pr_w": eo(i["L0_ffn_proj_w"]),
        "qkv2_w": chunks(i["L1_attn_w_qkv"].T, KC, C),
        "proj2_w": chunks(i["L1_attn_w_proj"].T, KC, C),
        "router_w": chunks(i["L1_ffn_w_router"], KC, C),
        "wi": ew(i["L1_ffn_wi"]),
        "wo": eo(i["L1_ffn_wo"]),
    }


def kernel(**inputs):
    import concourse.bacc as bacc
    from concourse.bass_utils import run_bass_kernel_spmd

    arrays = {f"in_{k}": np.ascontiguousarray(v) for k, v in layout({k: np.asarray(v) for k, v in inputs.items()}).items()}
    nc = bacc.Bacc("TRN2", target_bir_lowering=False, num_devices=1)
    args = [nc.dram_tensor(k, v.shape, mybir.dt.from_np(v.dtype), kind="ExternalInput").ap() for k, v in arrays.items()]
    scratch = nc.dram_tensor("scratch", (T, 2, KC, C, TOKENS), F32, kind="Internal").ap()
    out = nc.dram_tensor("out_0", (IMAGES, TOKENS, DIM), F32, kind="ExternalOutput").ap()
    vit_tower(nc, *args, scratch, out)
    return run_bass_kernel_spmd(nc, [arrays], core_ids=[0]).results[0]["out_0"]
```
